# Optimizing a Trainium2 kernel written in Bass

```python
import numpy as np
import jax
import jax.numpy as jnp

def _softmax(x, axis=-1):
    return jax.nn.softmax(x, axis=axis)

def _gelu(x):
    return jax.nn.gelu(x, approximate=True)

def _silu(x):
    return jax.nn.silu(x)

def _sigmoid(x):
    return jax.nn.sigmoid(x)

def _layernorm(x, axis=-1, eps=1e-05):
    m = jnp.mean(x, axis=axis, keepdims=True)
    v = jnp.var(x, axis=axis, keepdims=True)
    return (x - m) / jnp.sqrt(v + eps)

def _scatter_add(tgt, idx, src, axis=0):
    return tgt.at[idx].add(src)

def _segment_sum(src, seg, n):
    return jax.ops.segment_sum(src, seg, n)
kernel_name = 'mk_hybrid_d2_jaxref_r8_c39de5'

def setup_inputs(seed: int=0):
    np.random.seed(seed)
    _w = jnp.asarray

    def _L0_attn_a_setup():
        import jax, jax.numpy as jnp
        import numpy as np
        EMBED = 128
        HEADS = 16
        HEAD_DIM = EMBED // HEADS
        key = jax.random.key(seed)
        k1, k2, k3, k4, k5 = jax.random.split(key, 5)
        scale = 1.0 / np.sqrt(EMBED)
        return {'x': jax.random.normal(k1, (4, 256, EMBED), dtype=jnp.float32), 'qkv_w': jax.random.uniform(k2, (3 * EMBED, EMBED), minval=-scale, maxval=scale, dtype=jnp.float32), 'qkv_b': jax.random.uniform(k3, (3 * EMBED,), minval=-scale, maxval=scale, dtype=jnp.float32), 'out_w': jax.random.uniform(k4, (EMBED, EMBED), minval=-scale, maxval=scale, dtype=jnp.float32), 'out_b': jax.random.uniform(k5, (EMBED,), minval=-scale, maxval=scale, dtype=jnp.float32)}
    _L0_attn_a_in = _L0_attn_a_setup()

    def _L0_attn_b_setup():
        import jax, jax.numpy as jnp
        import numpy as np
        D_MODEL = 128
        QHEADS = 16
        KVHEADS = 4
        G = QHEADS // KVHEADS
        D_Q = D_MODEL // QHEADS
        D_KV = D_MODEL // QHEADS * KVHEADS
        BATCH, SEQ = (2, 256)

        def _xavier(key, shape):
            fan_out, fan_in = shape
            lim = (6.0 / (fan_in + fan_out)) ** 0.5
            return jax.random.uniform(key, shape, jnp.float32, -lim, lim)
        key = jax.random.key(seed)
        ks = jax.random.split(key, 5)
        x = jax.random.normal(ks[0], (BATCH, SEQ, D_MODEL), jnp.float32)
        wq = _xavier(ks[1], (D_MODEL, D_MODEL))
        bq = jnp.zeros((D_MODEL,), jnp.float32)
        wk = _xavier(ks[2], (D_KV, D_MODEL))
        bk = jnp.zeros((D_KV,), jnp.float32)
        wv = _xavier(ks[3], (D_KV, D_MODEL))
        bv = jnp.zeros((D_KV,), jnp.float32)
        wo = _xavier(ks[4], (D_MODEL, D_MODEL))
        bo = jnp.zeros((D_MODEL,), jnp.float32)
        return {'x': x, 'wq': wq, 'bq': bq, 'wk': wk, 'bk': bk, 'wv': wv, 'bv': bv, 'wo': wo, 'bo': bo}
    _L0_attn_b_in = _L0_attn_b_setup()

    def _L0_ffn_setup():
        import jax, jax.numpy as jnp
        import numpy as np
        from jax import lax
        H, DK, DV, N_EXP, CHUNK = (8, 64, 64, 4, 64)
        LORA, GATE_LR = (64, 16)
        NORMALIZER = 16.0
        EPS = 1e-05

        def chunk_gla(q, k, v, gk, C=CHUNK):
            L, h, dk = q.shape
            dv = v.shape[-1]
            nc = L // C
            qc, kc, vc, gc = (t.reshape(nc, C, h, -1) for t in (q, k, v, gk))
            g = jnp.cumsum(gc, axis=1)
            g_last = g[:, -1]
            qg = qc * jnp.exp(g)
            kg = kc * jnp.exp(-g)
            A = jnp.einsum('cthd,cshd->chts', qg, kg)
            A = A * jnp.tril(jnp.ones((C, C), q.dtype))
            o_intra = jnp.einsum('chts,cshe->cthe', A, vc)
            k_out = kc * jnp.exp(g_last[:, None] - g)
            chunk_kv = jnp.einsum('cthd,cthe->chde', k_out, vc)
            decay = jnp.exp(g_last)

            def step(S, inp):
                kv, dec, qg_c = inp
                o_inter = jnp.einsum('thd,hde->the', qg_c, S)
                return (S * dec[..., None] + kv, o_inter)
            S0 = jnp.zeros((h, dk, dv), q.dtype)
            _, o_inter = lax.scan(step, S0, (chunk_kv, decay, qg))
            return (o_intra + o_inter).reshape(L, h, dv)
        key = jax.random.key(seed)
        ks = jax.random.split(key, 20)
        B, L, Dh = (1, 512, 128)
        KD, VD = (H * DK, H * DV)
        w = lambda i, shape: jax.random.normal(ks[i], shape, jnp.float32) * 0.02
        return {'x': jax.random.normal(ks[0], (B, L, Dh), jnp.float32), 'Wq': w(1, (Dh, KD)), 'Wk': w(2, (Dh, KD)), 'Wv': w(3, (Dh, VD)), 'Wqa': w(4, (Dh, LORA)), 'Wqb': w(5, (LORA, KD)), 'Wka': w(6, (Dh, LORA)), 'Wkb': w(7, (LORA, KD)), 'Wg1a': w(8, (Dh, GATE_LR)), 'Wg1b': w(9, (GATE_LR, KD)), 'bg1': jnp.zeros((KD,), jnp.float32), 'Wg2a': w(10, (Dh, GATE_LR)), 'Wg2b': w(11, (GATE_LR, KD)), 'bg2': jnp.zeros((KD,), jnp.float32), 'We': w(12, (Dh, N_EXP)), 'Wga': w(13, (Dh, LORA)), 'Wgb': w(14, (LORA, VD)), 'norm_w': jnp.ones((DV,), jnp.float32), 'Wo': w(15, (VD, Dh))}
    _L0_ffn_in = _L0_ffn_setup()

    def _L1_attn_a_setup():
        import jax, jax.numpy as jnp
        import numpy as np
        import math
        D_MODEL = 128
        D_STATE = 16
        D_CONV = 4
        EXPAND = 2
        D_INNER = EXPAND * D_MODEL
        DT_RANK = math.ceil(D_MODEL / 16)
        BATCH, LENGTH = (2, 256)

        def _selective_scan(xs, dt, Bm, Cm, A_log, Dparam):
            A = -jnp.exp(A_log.astype(jnp.float32))

            def step(states, inp):
                x_t, dt_t, B_t, C_t = inp
                states = states * jnp.exp(dt_t[:, :, None] * A) + dt_t[:, :, None] * B_t[:, None, :] * x_t[:, :, None]
                y = jnp.einsum('bdn,bn->bd', states, C_t)
                return (states, y)
            b = xs.shape[0]
            init = jnp.zeros((b, D_INNER, D_STATE), dtype=xs.dtype)
            seq = (jnp.swapaxes(xs, 0, 1), jnp.swapaxes(dt, 0, 1), jnp.swapaxes(Bm, 0, 1), jnp.swapaxes(Cm, 0, 1))
            _, ys = jax.lax.scan(step, init, seq)
            return jnp.swapaxes(ys, 0, 1) + xs * Dparam
        key = jax.random.key(seed)
        ks = jax.random.split(key, 12)
        s_in = 1.0 / math.sqrt(D_MODEL)
        s_inner = 1.0 / math.sqrt(D_INNER)
        s_dt = 1.0 / math.sqrt(DT_RANK)
        x = jax.random.normal(ks[0], (BATCH, LENGTH, D_MODEL), dtype=jnp.float32)
        in_proj_w = jax.random.normal(ks[1], (D_MODEL, 2 * D_INNER), dtype=jnp.float32) * s_in
        conv_w = jax.random.normal(ks[2], (D_INNER, 1, D_CONV), dtype=jnp.float32) * (1.0 / math.sqrt(D_CONV))
        conv_b = jax.random.normal(ks[3], (D_INNER,), dtype=jnp.float32) * 0.01
        x_proj_w = jax.random.normal(ks[4], (D_INNER, DT_RANK + 2 * D_STATE), dtype=jnp.float32) * s_inner
        dt_proj_w = jax.random.normal(ks[5], (DT_RANK, D_INNER), dtype=jnp.float32) * s_dt
        dt_min, dt_max = (0.001, 0.1)
        dt = jnp.exp(jax.random.uniform(ks[6], (D_INNER,)) * (math.log(dt_max) - math.log(dt_min)) + math.log(dt_min))
        dt = jnp.clip(dt, dt_min, None)
        dt_proj_b = dt + jnp.log(-jnp.expm1(-dt))
        A_log = jnp.log(jax.random.uniform(ks[7], (D_INNER, D_STATE), minval=0.0001, maxval=1.0))
        Dparam = jnp.ones((D_INNER,), dtype=jnp.float32)
        out_proj_w = jax.random.normal(ks[8], (D_INNER, D_MODEL), dtype=jnp.float32) * s_inner
        return {'x': x, 'in_proj_w': in_proj_w, 'conv_w': conv_w, 'conv_b': conv_b, 'x_proj_w': x_proj_w, 'dt_proj_w': dt_proj_w, 'dt_proj_b': dt_proj_b, 'A_log': A_log, 'Dparam': Dparam, 'out_proj_w': out_proj_w}
    _L1_attn_a_in = _L1_attn_a_setup()

    def _L1_attn_b_setup():
        import jax, jax.numpy as jnp
        import numpy as np
        B, S, D, H = (2, 512, 128, 16)
        HD = D // H
        KCONV = 4

        def _rmsnorm(x, scale, eps=1e-06):
            return x * jax.lax.rsqrt(jnp.mean(x * x, axis=-1, keepdims=True) + eps) * scale

        def _l2norm(x, eps=1e-06):
            return x * jax.lax.rsqrt(jnp.sum(x * x, axis=-1, keepdims=True) + eps)

        def _causal_dwconv_silu(x, w):
            k = w.shape[1]
            s = x.shape[1]
            xp = jnp.pad(x, ((0, 0), (k - 1, 0), (0, 0)))
            out = sum((xp[:, i:i + s, :] * w[:, i] for i in range(k)))
            return jax.nn.silu(out)

        def _p20_scan(x, decay_log, theta):
            b, s, d = x.shape
            xc = x.reshape(b, s, d // 2, 2)
            u = jax.lax.complex(xc[..., 0], xc[..., 1])
            a = jnp.exp(-jnp.exp(decay_log)) * jnp.exp(1j * theta)

            def step(carry, u_t):
                st = carry * a + u_t
                return (st, st)
            _, ys = jax.lax.scan(step, jnp.zeros((b, d // 2), u.dtype), jnp.swapaxes(u, 0, 1))
            ys = jnp.swapaxes(ys, 0, 1)
            return jnp.stack([ys.real, ys.imag], axis=-1).reshape(b, s, d)

        def _gated_delta_rule(q, k, v, g, beta):
            scale = q.shape[-1] ** (-0.5)
            q = _l2norm(q)
            k = _l2norm(k)
            qt, kt, vt = (jnp.moveaxis(t, 1, 0) for t in (q, k, v))
            gt, bt = (jnp.moveaxis(t, 1, 0) for t in (g, beta))
            s0 = jnp.zeros((q.shape[0], q.shape[2], q.shape[3], v.shape[3]), v.dtype)

            def step(state, inp):
                q_t, k_t, v_t, g_t, b_t = inp
                state = state * jnp.exp(g_t)[..., None, None]
                v_err = (v_t - jnp.einsum('bhkv,bhk->bhv', state, k_t)) * b_t[..., None]
                state = state + jnp.einsum('bhk,bhv->bhkv', k_t, v_err)
                o_t = jnp.einsum('bhkv,bhk->bhv', state, q_t) * scale
                return (state, o_t)
            _, o = jax.lax.scan(step, s0, (qt, kt, vt, gt, bt))
            return jnp.moveaxis(o, 0, 1)
        key = jax.random.key(seed)
        ks = jax.random.split(key, 16)
        w = lambda k, shp, s=0.02: jax.random.normal(k, shp, jnp.float32) * s
        ctrl_out = 3 * D + 2 * H + D
        ctrl_b = jnp.concatenate([jnp.zeros((3 * D,), jnp.float32), jnp.full((H,), 1.5, jnp.float32), jnp.full((H,), -2.0, jnp.float32), jnp.full((D,), -1.5, jnp.float32)])

        def conv_w(k):
            base = jnp.zeros((D, KCONV), jnp.float32).at[:, -1].set(1.0)
            return base + w(k, (D, KCONV), 0.02)
        return {'hidden': jax.random.normal(ks[0], (B, S, D), jnp.float32), 'p20_decay_log': w(ks[1], (D // 2,), 1.0), 'p20_theta': jax.random.uniform(ks[2], (D // 2,), jnp.float32, 0.0, 2.0 * np.pi), 'ctrl_W': w(ks[3], (D, ctrl_out)), 'ctrl_b': ctrl_b, 'p20c_W': w(ks[4], (D, 3 * D), 0.001), 'qconv_w': conv_w(ks[5]), 'kconv_w': conv_w(ks[6]), 'vconv_w': conv_w(ks[7]), 'mnorm_scale': jnp.ones((HD,), jnp.float32), 'vnorm_scale': jnp.ones((D,), jnp.float32), 'ramp_logit': jnp.full((D,), -4.595, jnp.float32), 'out_W': w(ks[8], (2 * D, D), 0.02), 'out_b': jnp.zeros((D,), jnp.float32)}
    _L1_attn_b_in = _L1_attn_b_setup()

    def _L1_ffn_setup():
        import jax, jax.numpy as jnp
        import numpy as np
        DIM = 128
        INTER = 128
        N_EXPERTS = 8
        TOPK = 2
        N_SHARED = 2
        key = jax.random.key(seed)
        ks = jax.random.split(key, 10)
        s = 0.02
        return {'x': jax.random.normal(ks[0], (4, 256, DIM), dtype=jnp.float32), 'gate_w': jax.random.normal(ks[1], (N_EXPERTS, DIM), dtype=jnp.float32) * s, 'gate_bias': jax.random.normal(ks[2], (N_EXPERTS,), dtype=jnp.float32) * s, 'w1': jax.random.normal(ks[3], (N_EXPERTS, INTER, DIM), dtype=jnp.float32) * s, 'w3': jax.random.normal(ks[4], (N_EXPERTS, INTER, DIM), dtype=jnp.float32) * s, 'w2': jax.random.normal(ks[5], (N_EXPERTS, DIM, INTER), dtype=jnp.float32) * s, 'sw1': jax.random.normal(ks[6], (N_SHARED * INTER, DIM), dtype=jnp.float32) * s, 'sw3': jax.random.normal(ks[7], (N_SHARED * INTER, DIM), dtype=jnp.float32) * s, 'sw2': jax.random.normal(ks[8], (DIM, N_SHARED * INTER), dtype=jnp.float32) * s}
    _L1_ffn_in = _L1_ffn_setup()
    _d = {'L0_attn_a_x': _L0_attn_a_in['x'], 'L0_attn_a_qkv_w': _L0_attn_a_in['qkv_w'], 'L0_attn_a_qkv_b': _L0_attn_a_in['qkv_b'], 'L0_attn_a_out_w': _L0_attn_a_in['out_w'], 'L0_attn_a_out_b': _L0_attn_a_in['out_b'], 'L0_attn_b_wq': _L0_attn_b_in['wq'], 'L0_attn_b_bq': _L0_attn_b_in['bq'], 'L0_attn_b_wk': _L0_attn_b_in['wk'], 'L0_attn_b_bk': _L0_attn_b_in['bk'], 'L0_attn_b_wv': _L0_attn_b_in['wv'], 'L0_attn_b_bv': _L0_attn_b_in['bv'], 'L0_attn_b_wo': _L0_attn_b_in['wo'], 'L0_attn_b_bo': _L0_attn_b_in['bo'], 'L0_ffn_Wq': _L0_ffn_in['Wq'], 'L0_ffn_Wk': _L0_ffn_in['Wk'], 'L0_ffn_Wv': _L0_ffn_in['Wv'], 'L0_ffn_Wqa': _L0_ffn_in['Wqa'], 'L0_ffn_Wqb': _L0_ffn_in['Wqb'], 'L0_ffn_Wka': _L0_ffn_in['Wka'], 'L0_ffn_Wkb': _L0_ffn_in['Wkb'], 'L0_ffn_Wg1a': _L0_ffn_in['Wg1a'], 'L0_ffn_Wg1b': _L0_ffn_in['Wg1b'], 'L0_ffn_bg1': _L0_ffn_in['bg1'], 'L0_ffn_Wg2a': _L0_ffn_in['Wg2a'], 'L0_ffn_Wg2b': _L0_ffn_in['Wg2b'], 'L0_ffn_bg2': _L0_ffn_in['bg2'], 'L0_ffn_We': _L0_ffn_in['We'], 'L0_ffn_Wga': _L0_ffn_in['Wga'], 'L0_ffn_Wgb': _L0_ffn_in['Wgb'], 'L0_ffn_norm_w': _L0_ffn_in['norm_w'], 'L0_ffn_Wo': _L0_ffn_in['Wo'], 'L1_attn_a_in_proj_w': _L1_attn_a_in['in_proj_w'], 'L1_attn_a_conv_w': _L1_attn_a_in['conv_w'], 'L1_attn_a_conv_b': _L1_attn_a_in['conv_b'], 'L1_attn_a_x_proj_w': _L1_attn_a_in['x_proj_w'], 'L1_attn_a_dt_proj_w': _L1_attn_a_in['dt_proj_w'], 'L1_attn_a_dt_proj_b': _L1_attn_a_in['dt_proj_b'], 'L1_attn_a_A_log': _L1_attn_a_in['A_log'], 'L1_attn_a_Dparam': _L1_attn_a_in['Dparam'], 'L1_attn_a_out_proj_w': _L1_attn_a_in['out_proj_w'], 'L1_attn_b_p20_decay_log': _L1_attn_b_in['p20_decay_log'], 'L1_attn_b_p20_theta': _L1_attn_b_in['p20_theta'], 'L1_attn_b_ctrl_W': _L1_attn_b_in['ctrl_W'], 'L1_attn_b_ctrl_b': _L1_attn_b_in['ctrl_b'], 'L1_attn_b_p20c_W': _L1_attn_b_in['p20c_W'], 'L1_attn_b_qconv_w': _L1_attn_b_in['qconv_w'], 'L1_attn_b_kconv_w': _L1_attn_b_in['kconv_w'], 'L1_attn_b_vconv_w': _L1_attn_b_in['vconv_w'], 'L1_attn_b_mnorm_scale': _L1_attn_b_in['mnorm_scale'], 'L1_attn_b_vnorm_scale': _L1_attn_b_in['vnorm_scale'], 'L1_attn_b_ramp_logit': _L1_attn_b_in['ramp_logit'], 'L1_attn_b_out_W': _L1_attn_b_in['out_W'], 'L1_attn_b_out_b': _L1_attn_b_in['out_b'], 'L1_ffn_gate_w': _L1_ffn_in['gate_w'], 'L1_ffn_gate_bias': _L1_ffn_in['gate_bias'], 'L1_ffn_w1': _L1_ffn_in['w1'], 'L1_ffn_w3': _L1_ffn_in['w3'], 'L1_ffn_w2': _L1_ffn_in['w2'], 'L1_ffn_sw1': _L1_ffn_in['sw1'], 'L1_ffn_sw3': _L1_ffn_in['sw3'], 'L1_ffn_sw2': _L1_ffn_in['sw2']}
    _x0 = _d['L0_attn_a_x']
    _d['L0_attn_a_x'] = jax.random.normal(jax.random.fold_in(jax.random.key(seed), 1), (1, 2048, 128), dtype=_x0.dtype)
    del _x0
    return _d

def reference(L0_attn_a_x, L0_attn_a_qkv_w, L0_attn_a_qkv_b, L0_attn_a_out_w, L0_attn_a_out_b, L0_attn_b_wq, L0_attn_b_bq, L0_attn_b_wk, L0_attn_b_bk, L0_attn_b_wv, L0_attn_b_bv, L0_attn_b_wo, L0_attn_b_bo, L0_ffn_Wq, L0_ffn_Wk, L0_ffn_Wv, L0_ffn_Wqa, L0_ffn_Wqb, L0_ffn_Wka, L0_ffn_Wkb, L0_ffn_Wg1a, L0_ffn_Wg1b, L0_ffn_bg1, L0_ffn_Wg2a, L0_ffn_Wg2b, L0_ffn_bg2, L0_ffn_We, L0_ffn_Wga, L0_ffn_Wgb, L0_ffn_norm_w, L0_ffn_Wo, L1_attn_a_in_proj_w, L1_attn_a_conv_w, L1_attn_a_conv_b, L1_attn_a_x_proj_w, L1_attn_a_dt_proj_w, L1_attn_a_dt_proj_b, L1_attn_a_A_log, L1_attn_a_Dparam, L1_attn_a_out_proj_w, L1_attn_b_p20_decay_log, L1_attn_b_p20_theta, L1_attn_b_ctrl_W, L1_attn_b_ctrl_b, L1_attn_b_p20c_W, L1_attn_b_qconv_w, L1_attn_b_kconv_w, L1_attn_b_vconv_w, L1_attn_b_mnorm_scale, L1_attn_b_vnorm_scale, L1_attn_b_ramp_logit, L1_attn_b_out_W, L1_attn_b_out_b, L1_ffn_gate_w, L1_ffn_gate_bias, L1_ffn_w1, L1_ffn_w3, L1_ffn_w2, L1_ffn_sw1, L1_ffn_sw3, L1_ffn_sw2):

    def _L0_attn_a_ref(x, qkv_w, qkv_b, out_w, out_b):
        import jax, jax.numpy as jnp
        import numpy as np
        EMBED = 128
        HEADS = 16
        HEAD_DIM = EMBED // HEADS
        b, n, _ = x.shape
        qkv = (jnp.einsum('bne,fe->bnf', x, qkv_w) + qkv_b).reshape(b, n, 3, HEADS, HEAD_DIM)
        q, k, v = (qkv[:, :, 0], qkv[:, :, 1], qkv[:, :, 2])
        scores = jnp.einsum('bnhd,bmhd->bhnm', q, k) / jnp.sqrt(jnp.float32(HEAD_DIM))
        attn = jax.nn.softmax(scores, axis=-1)
        out = jnp.einsum('bhnm,bmhd->bnhd', attn, v).reshape(b, n, EMBED)
        return jnp.einsum('bne,fe->bnf', out, out_w) + out_b

    def _L0_attn_b_ref(x, wq, bq, wk, bk, wv, bv, wo, bo):
        import jax, jax.numpy as jnp
        import numpy as np
        D_MODEL = 128
        QHEADS = 16
        KVHEADS = 4
        G = QHEADS // KVHEADS
        D_Q = D_MODEL // QHEADS
        D_KV = D_MODEL // QHEADS * KVHEADS
        BATCH, SEQ = (2, 256)

        def _xavier(key, shape):
            fan_out, fan_in = shape
            lim = (6.0 / (fan_in + fan_out)) ** 0.5
            return jax.random.uniform(key, shape, jnp.float32, -lim, lim)
        b, n, _ = x.shape
        scaling = D_Q ** (-0.5)
        q = (x @ wq.T + bq).reshape(b, n, QHEADS, D_Q).transpose(0, 2, 1, 3)
        k = (x @ wk.T + bk).reshape(b, n, KVHEADS, D_Q).transpose(0, 2, 1, 3)
        v = (x @ wv.T + bv).reshape(b, n, KVHEADS, D_Q).transpose(0, 2, 1, 3)
        q = q.reshape(b, KVHEADS, G, n, D_Q).transpose(0, 2, 1, 3, 4)
        attn = jnp.einsum('bghnd,bhsd->bghns', q, k) * scaling
        attn = jax.nn.softmax(attn, axis=-1)
        out = jnp.einsum('bghns,bhsd->bghnd', attn, v)
        out = out.transpose(0, 3, 2, 1, 4).reshape(b, n, D_MODEL)
        return out @ wo.T + bo

    def _L0_ffn_ref(x, Wq, Wk, Wv, Wqa, Wqb, Wka, Wkb, Wg1a, Wg1b, bg1, Wg2a, Wg2b, bg2, We, Wga, Wgb, norm_w, Wo):
        import jax, jax.numpy as jnp
        import numpy as np
        from jax import lax
        H, DK, DV, N_EXP, CHUNK = (8, 64, 64, 4, 64)
        LORA, GATE_LR = (64, 16)
        NORMALIZER = 16.0
        EPS = 1e-05

        def chunk_gla(q, k, v, gk, C=CHUNK):
            L, h, dk = q.shape
            dv = v.shape[-1]
            nc = L // C
            qc, kc, vc, gc = (t.reshape(nc, C, h, -1) for t in (q, k, v, gk))
            g = jnp.cumsum(gc, axis=1)
            g_last = g[:, -1]
            qg = qc * jnp.exp(g)
            kg = kc * jnp.exp(-g)
            A = jnp.einsum('cthd,cshd->chts', qg, kg)
            A = A * jnp.tril(jnp.ones((C, C), q.dtype))
            o_intra = jnp.einsum('chts,cshe->cthe', A, vc)
            k_out = kc * jnp.exp(g_last[:, None] - g)
            chunk_kv = jnp.einsum('cthd,cthe->chde', k_out, vc)
            decay = jnp.exp(g_last)

            def step(S, inp):
                kv, dec, qg_c = inp
                o_inter = jnp.einsum('thd,hde->the', qg_c, S)
                return (S * dec[..., None] + kv, o_inter)
            S0 = jnp.zeros((h, dk, dv), q.dtype)
            _, o_inter = lax.scan(step, S0, (chunk_kv, decay, qg))
            return (o_intra + o_inter).reshape(L, h, dv)
        B, L, Dh = x.shape
        scale = DK ** (-0.5)
        q1 = (x @ Wq).reshape(B, L, H, DK) * scale
        k1 = (x @ Wk).reshape(B, L, H, DK)
        v = (x @ Wv).reshape(B, L, H, DV)
        q2 = (x @ Wqa @ Wqb).reshape(B, L, H, DK) * scale
        k2 = jax.nn.softmax((x @ Wka @ Wkb).reshape(B, L, H, DK), axis=-1)
        gk1 = (jax.nn.log_sigmoid(x @ Wg1a @ Wg1b + bg1) / NORMALIZER).reshape(B, L, H, DK)
        gk2 = (jax.nn.log_sigmoid(x @ Wg2a @ Wg2b + bg2) / NORMALIZER).reshape(B, L, H, DK)
        e = jax.nn.softmax(x @ We, axis=-1)
        _, idx = lax.top_k(e, 1)
        mask = jax.nn.one_hot(idx, N_EXP, dtype=x.dtype).sum(-2)
        rw = e * mask
        fac = jnp.swapaxes(rw, 1, 2)[:, :, :, None, None]
        mfac = jnp.swapaxes(mask, 1, 2)[:, :, :, None, None]
        q_e = q2[:, None] * fac
        k_e = k2[:, None] * fac
        gk_e = gk2[:, None] * mfac
        gla_b = jax.vmap(chunk_gla)
        o_dense = gla_b(q1, k1, v, gk1)
        gla_be = jax.vmap(jax.vmap(chunk_gla, in_axes=(0, 0, None, 0)))
        o_sparse = gla_be(q_e, k_e, v, gk_e).sum(axis=1)
        o = o_dense + o_sparse
        g = (x @ Wga @ Wgb).reshape(B, L, H, DV)
        o = o * lax.rsqrt(jnp.mean(o * o, axis=-1, keepdims=True) + EPS) * norm_w
        o = o * (g * jax.nn.sigmoid(g))
        return o.reshape(B, L, H * DV) @ Wo

    def _L1_attn_a_ref(x, in_proj_w, conv_w, conv_b, x_proj_w, dt_proj_w, dt_proj_b, A_log, Dparam, out_proj_w):
        import jax, jax.numpy as jnp
        import numpy as np
        import math
        D_MODEL = 128
        D_STATE = 16
        D_CONV = 4
        EXPAND = 2
        D_INNER = EXPAND * D_MODEL
        DT_RANK = math.ceil(D_MODEL / 16)
        BATCH, LENGTH = (2, 256)

        def _selective_scan(xs, dt, Bm, Cm, A_log, Dparam):
            A = -jnp.exp(A_log.astype(jnp.float32))

            def step(states, inp):
                x_t, dt_t, B_t, C_t = inp
                states = states * jnp.exp(dt_t[:, :, None] * A) + dt_t[:, :, None] * B_t[:, None, :] * x_t[:, :, None]
                y = jnp.einsum('bdn,bn->bd', states, C_t)
                return (states, y)
            b = xs.shape[0]
            init = jnp.zeros((b, D_INNER, D_STATE), dtype=xs.dtype)
            seq = (jnp.swapaxes(xs, 0, 1), jnp.swapaxes(dt, 0, 1), jnp.swapaxes(Bm, 0, 1), jnp.swapaxes(Cm, 0, 1))
            _, ys = jax.lax.scan(step, init, seq)
            return jnp.swapaxes(ys, 0, 1) + xs * Dparam
        b, l, _ = x.shape
        xr = x @ in_proj_w
        xi, res = (xr[..., :D_INNER], xr[..., D_INNER:])
        xc = jnp.swapaxes(xi, 1, 2)
        xc = jax.lax.conv_general_dilated(xc, conv_w, window_strides=(1,), padding=[(D_CONV - 1, 0)], dimension_numbers=('NCH', 'OIH', 'NCH'), feature_group_count=D_INNER)
        xc = xc + conv_b[None, :, None]
        xi = jax.nn.silu(jnp.swapaxes(xc, 1, 2))
        x_dbl = xi @ x_proj_w
        delta = x_dbl[..., :DT_RANK]
        Bm = x_dbl[..., DT_RANK:DT_RANK + D_STATE]
        Cm = x_dbl[..., DT_RANK + D_STATE:]
        dt = jax.nn.softplus(delta @ dt_proj_w + dt_proj_b)
        y = _selective_scan(xi, dt, Bm, Cm, A_log, Dparam)
        y = y * jax.nn.silu(res)
        return y @ out_proj_w

    def _L1_attn_b_ref(hidden, p20_decay_log, p20_theta, ctrl_W, ctrl_b, p20c_W, qconv_w, kconv_w, vconv_w, mnorm_scale, vnorm_scale, ramp_logit, out_W, out_b):
        import jax, jax.numpy as jnp
        import numpy as np
        B, S, D, H = (2, 512, 128, 16)
        HD = D // H
        KCONV = 4

        def _rmsnorm(x, scale, eps=1e-06):
            return x * jax.lax.rsqrt(jnp.mean(x * x, axis=-1, keepdims=True) + eps) * scale

        def _l2norm(x, eps=1e-06):
            return x * jax.lax.rsqrt(jnp.sum(x * x, axis=-1, keepdims=True) + eps)

        def _causal_dwconv_silu(x, w):
            k = w.shape[1]
            s = x.shape[1]
            xp = jnp.pad(x, ((0, 0), (k - 1, 0), (0, 0)))
            out = sum((xp[:, i:i + s, :] * w[:, i] for i in range(k)))
            return jax.nn.silu(out)

        def _p20_scan(x, decay_log, theta):
            b, s, d = x.shape
            xc = x.reshape(b, s, d // 2, 2)
            u = jax.lax.complex(xc[..., 0], xc[..., 1])
            a = jnp.exp(-jnp.exp(decay_log)) * jnp.exp(1j * theta)

            def step(carry, u_t):
                st = carry * a + u_t
                return (st, st)
            _, ys = jax.lax.scan(step, jnp.zeros((b, d // 2), u.dtype), jnp.swapaxes(u, 0, 1))
            ys = jnp.swapaxes(ys, 0, 1)
            return jnp.stack([ys.real, ys.imag], axis=-1).reshape(b, s, d)

        def _gated_delta_rule(q, k, v, g, beta):
            scale = q.shape[-1] ** (-0.5)
            q = _l2norm(q)
            k = _l2norm(k)
            qt, kt, vt = (jnp.moveaxis(t, 1, 0) for t in (q, k, v))
            gt, bt = (jnp.moveaxis(t, 1, 0) for t in (g, beta))
            s0 = jnp.zeros((q.shape[0], q.shape[2], q.shape[3], v.shape[3]), v.dtype)

            def step(state, inp):
                q_t, k_t, v_t, g_t, b_t = inp
                state = state * jnp.exp(g_t)[..., None, None]
                v_err = (v_t - jnp.einsum('bhkv,bhk->bhv', state, k_t)) * b_t[..., None]
                state = state + jnp.einsum('bhk,bhv->bhkv', k_t, v_err)
                o_t = jnp.einsum('bhkv,bhk->bhv', state, q_t) * scale
                return (state, o_t)
            _, o = jax.lax.scan(step, s0, (qt, kt, vt, gt, bt))
            return jnp.moveaxis(o, 0, 1)
        b, s, d = hidden.shape
        p20_read = _p20_scan(hidden, p20_decay_log, p20_theta)
        normed_p20 = _rmsnorm(p20_read, vnorm_scale)
        p20_q, p20_k, p20_v = jnp.split(normed_p20 @ p20c_W, 3, axis=-1)
        ramp = jax.nn.sigmoid(ramp_logit)
        ctrl = hidden @ ctrl_W + ctrl_b
        q_in, k_in, v_in, dec_in, beta_in, gate_in = jnp.split(ctrl, np.cumsum([d, d, d, H, H]).tolist(), axis=-1)
        q_in = _causal_dwconv_silu(q_in, qconv_w)
        k_in = _causal_dwconv_silu(k_in, kconv_w)
        v_in = _causal_dwconv_silu(v_in, vconv_w)
        queries = (q_in + ramp * p20_q).reshape(b, s, H, HD)
        keys = (k_in + ramp * p20_k).reshape(b, s, H, HD)
        values = (v_in + ramp * p20_v).reshape(b, s, H, HD)
        g = jax.nn.log_sigmoid(dec_in.astype(jnp.float32)).astype(hidden.dtype)
        beta = jax.nn.sigmoid(beta_in)
        reads = _gated_delta_rule(queries, keys, values, g, beta)
        normed_reads = _rmsnorm(reads, mnorm_scale).reshape(b, s, d)
        fused = jnp.concatenate([normed_reads, normed_p20], axis=-1)
        projected = fused @ out_W + out_b
        return jax.nn.sigmoid(gate_in) * projected

    def _L1_ffn_ref(x, gate_w, gate_bias, w1, w3, w2, sw1, sw3, sw2):
        import jax, jax.numpy as jnp
        import numpy as np
        DIM = 128
        INTER = 128
        N_EXPERTS = 8
        TOPK = 2
        N_SHARED = 2
        shape = x.shape
        xt = x.reshape(-1, shape[-1])
        scores = jax.nn.softmax((xt @ gate_w.T).astype(jnp.float32), axis=-1)
        _, idx = jax.lax.top_k(scores + gate_bias, TOPK)
        weights = jnp.take_along_axis(scores, idx, axis=1).astype(x.dtype)
        y = jnp.zeros_like(xt)
        for e in range(N_EXPERTS):
            gate_e = jnp.sum(jnp.where(idx == e, weights, 0.0), axis=1)
            h = jax.nn.silu(xt @ w1[e].T) * (xt @ w3[e].T)
            y = y + gate_e[:, None] * (h @ w2[e].T)
        z = jax.nn.silu(xt @ sw1.T) * (xt @ sw3.T) @ sw2.T
        return (y + z).reshape(shape)
    x = L0_attn_a_x
    x = x + _L0_attn_a_ref(_layernorm(x, axis=-1), L0_attn_a_qkv_w, L0_attn_a_qkv_b, L0_attn_a_out_w, L0_attn_a_out_b)
    x = x + _L0_ffn_ref(_layernorm(x, axis=-1), L0_ffn_Wq, L0_ffn_Wk, L0_ffn_Wv, L0_ffn_Wqa, L0_ffn_Wqb, L0_ffn_Wka, L0_ffn_Wkb, L0_ffn_Wg1a, L0_ffn_Wg1b, L0_ffn_bg1, L0_ffn_Wg2a, L0_ffn_Wg2b, L0_ffn_bg2, L0_ffn_We, L0_ffn_Wga, L0_ffn_Wgb, L0_ffn_norm_w, L0_ffn_Wo)
    x = x + _L0_attn_b_ref(_layernorm(x, axis=-1), L0_attn_b_wq, L0_attn_b_bq, L0_attn_b_wk, L0_attn_b_bk, L0_attn_b_wv, L0_attn_b_bv, L0_attn_b_wo, L0_attn_b_bo)
    x = x + _L0_ffn_ref(_layernorm(x, axis=-1), L0_ffn_Wq, L0_ffn_Wk, L0_ffn_Wv, L0_ffn_Wqa, L0_ffn_Wqb, L0_ffn_Wka, L0_ffn_Wkb, L0_ffn_Wg1a, L0_ffn_Wg1b, L0_ffn_bg1, L0_ffn_Wg2a, L0_ffn_Wg2b, L0_ffn_bg2, L0_ffn_We, L0_ffn_Wga, L0_ffn_Wgb, L0_ffn_norm_w, L0_ffn_Wo)
    x = x + _L1_attn_a_ref(_layernorm(x, axis=-1), L1_attn_a_in_proj_w, L1_attn_a_conv_w, L1_attn_a_conv_b, L1_attn_a_x_proj_w, L1_attn_a_dt_proj_w, L1_attn_a_dt_proj_b, L1_attn_a_A_log, L1_attn_a_Dparam, L1_attn_a_out_proj_w)
    x = x + _L1_ffn_ref(_layernorm(x, axis=-1), L1_ffn_gate_w, L1_ffn_gate_bias, L1_ffn_w1, L1_ffn_w3, L1_ffn_w2, L1_ffn_sw1, L1_ffn_sw3, L1_ffn_sw2)
    x = x + _L1_attn_b_ref(_layernorm(x, axis=-1), L1_attn_b_p20_decay_log, L1_attn_b_p20_theta, L1_attn_b_ctrl_W, L1_attn_b_ctrl_b, L1_attn_b_p20c_W, L1_attn_b_qconv_w, L1_attn_b_kconv_w, L1_attn_b_vconv_w, L1_attn_b_mnorm_scale, L1_attn_b_vnorm_scale, L1_attn_b_ramp_logit, L1_attn_b_out_W, L1_attn_b_out_b)
    x = x + _L1_ffn_ref(_layernorm(x, axis=-1), L1_ffn_gate_w, L1_ffn_gate_bias, L1_ffn_w1, L1_ffn_w3, L1_ffn_w2, L1_ffn_sw1, L1_ffn_sw3, L1_ffn_sw2)
    return x

_drawn_inputs = setup_inputs


def setup_inputs(seed=0):
    import zlib

    import numpy as np

    out = dict(_drawn_inputs(seed))
    spreads = {'L0_attn_b_bq': (0.0, 0.1),
     'L0_attn_b_bk': (0.0, 2.0),
     'L0_attn_b_bv': (0.0, 0.1),
     'L0_attn_b_bo': (0.0, 0.1),
     'L0_ffn_bg1': (0.0, 0.8),
     'L0_ffn_bg2': (0.0, 0.8),
     'L0_ffn_norm_w': (1.0, 0.6),
     'L1_attn_a_Dparam': (1.0, 0.2),
     'L1_attn_b_mnorm_scale': (1.0, 0.6),
     'L1_attn_b_vnorm_scale': (1.0, 0.6),
     'L1_attn_b_ramp_logit': (-4.59499979019165, 0.6),
     'L1_attn_b_out_b': (0.0, 0.594)}
    factors = {'L0_ffn_Wq': 2.721,
     'L0_ffn_Wk': 2.732,
     'L0_ffn_Wv': 2.715,
     'L0_ffn_Wqa': 8.0,
     'L0_ffn_Wqb': 8.0,
     'L0_ffn_Wka': 8.0,
     'L0_ffn_Wkb': 8.0,
     'L0_ffn_Wg1a': 8.0,
     'L0_ffn_Wg1b': 8.0,
     'L0_ffn_Wg2a': 8.0,
     'L0_ffn_Wg2b': 8.0,
     'L0_ffn_We': 8.0,
     'L0_ffn_Wga': 2.743,
     'L0_ffn_Wgb': 2.699,
     'L0_ffn_Wo': 2.7,
     'L1_attn_a_conv_b': 4.118,
     'L1_attn_b_p20_decay_log': 3.677,
     'L1_attn_b_p20c_W': 34.31,
     'L1_ffn_gate_w': 8.0,
     'L1_ffn_gate_bias': 8.0,
     'L1_ffn_w1': 8.0,
     'L1_ffn_w3': 8.0,
     'L1_ffn_w2': 8.0,
     'L1_ffn_sw1': 4.84,
     'L1_ffn_sw3': 4.8,
     'L1_ffn_sw2': 4.792}
    for name, (base, spread) in spreads.items():
        noise = np.random.default_rng([zlib.crc32(name.encode()), seed]).standard_normal(out[name].shape)
        drawn = base * np.exp(spread * noise) if base else spread * noise
        out[name] = jnp.asarray(drawn.astype(out[name].dtype))
    for name, factor in factors.items():
        out[name] = (out[name] * factor).astype(out[name].dtype)
    return out
```

```python
import math
from contextlib import ExitStack

import concourse.bass as bass
from concourse import mybir

F32 = mybir.dt.float32
BF16 = mybir.dt.bfloat16
ALU = mybir.AluOpType
ACT = mybir.ActivationFunctionType
AX = mybir.AxisListType

N = 2048
D = 128
NT = N // 128
NB = N // 512
EPS_LN = 1e-5
BIAS = 1024


class Mark:

    def __init__(self, stream, loop, value):
        self.stream, self.loop, self.value = stream, loop, value

    def before(self):
        return Mark(self.stream, self.loop, self.value - self.loop.per[self.stream])


class Loop:
    def __init__(self, times):
        self.times, self.per, self.base, self.index = times, {}, {}, 0


class Stream:

    def __init__(self, prog, engine, sem, step=1):
        self.prog, self.engine, self.sem, self.step, self.count = prog, engine, sem, step, 0
        prog.streams.append(self)

    def do(self, make, *args, after=(), **kw):
        self.prog.wait(self.engine, after)
        if not self.prog.counting:
            make(*args, **kw).then_inc(self.sem, self.step)
        self.count += self.step
        return Mark(self, self.prog.loop, self.count)

    def last(self):
        return Mark(self, self.prog.loop, self.count)


class Program:

    def __init__(self, nc):
        self.nc, self.streams, self.loop, self.counting = nc, [], None, False
        self.waited = {}
        self.held_waits = [nc.alloc_semaphore(f"held_waits_{e}") for e in ("pool", "sync")]

    def stream(self, engine, name, step=1):
        s = Stream(self, engine, self.nc.alloc_semaphore(name), step)
        engine.sem_inc(s.sem, BIAS)
        s.count = BIAS
        return s

    def value(self, mark):
        loop = mark.loop
        if loop is None:
            return mark.value
        per, base = loop.per.get(mark.stream, 0), loop.base.get(mark.stream, 0)
        if loop is self.loop:
            return base + mark.value + loop.index * per
        return base + (loop.times - 1) * per + mark.value

    def wait(self, engine, marks):
        if self.counting:
            return
        for mark in marks:
            if mark is None:
                continue
            key = (id(engine), id(mark.stream), id(mark.loop if mark.loop is self.loop else None))
            least = mark.value if mark.loop is self.loop else self.value(mark)
            if self.waited.get(key, -10**9) >= least:
                continue
            self.waited[key] = least
            engine.wait_ge(mark.stream.sem, self.value(mark))
            if self.loop is not None and engine in (self.nc.sync, self.nc.gpsimd):
                engine.sem_inc(self.held_waits[engine is self.nc.sync], 1)

    def repeat(self, times, body):
        loop = Loop(times)
        at = {s: s.count for s in self.streams}
        for s in self.streams:
            s.count = 0
        outer_loop = self.loop
        assert outer_loop is None
        self.loop, self.counting = loop, True
        for s in self.streams:
            loop.per[s] = 0
        body(0)
        loop.per = {s: s.count for s in self.streams}
        for s in self.streams:
            s.count = 0
        loop.base = at
        self.counting = False
        self.waited = {}
        with self.nc.Fori(0, times) as index:
            loop.index = index
            body(index)
        self.waited = {}
        self.loop = None
        for s in self.streams:
            s.count = at[s] + times * loop.per[s]

    def pipeline(self, times, body, state):
        def age(x):
            if isinstance(x, (list, tuple)):
                return [age(y) for y in x]
            return x.before() if x is not None else None

        def blank(x):
            return [blank(y) for y in x] if isinstance(x, (list, tuple)) else None

        ends = {}

        def traced(i):
            if self.counting:
                state.update({k: blank(x) for k, x in state.items()})
            else:
                state.update({k: age(x) for k, x in ends.items()})
            body(i)
            if self.counting:
                ends.update(state)

        self.join()
        self.repeat(times, traced)

    def join(self):
        for engine in (self.nc.tensor, self.nc.vector, self.nc.scalar, self.nc.gpsimd, self.nc.sync):
            self.wait(engine, [s.last() for s in self.streams])


HEADS, HD = 16, 8
PARTS = 3
ROWS = PARTS * PARTS * HD
LEAD = 16

def layer_norm_T(g):
    nc, V, A, T = g.nc, g.V, g.A, g.T
    with ExitStack() as mem:
        sb = lambda n, s, d=F32: mem.enter_context(nc.sbuf_tensor(f"{n}{g.uid()}", s, d))
        xc, sq = sb("ln_centred", [128, NT, D]), sb("ln_squares", [128, NT, D])
        st = sb("ln_stats", [128, 4, NT])
        total, neg_mean, var, rstd = (st[:, k, :] for k in range(4))
        up = lambda ap: ap.unsqueeze(2).broadcast_to([128, NT, D])
        m = V.do(nc.vector.tensor_reduce, total, g.x_tok[:, :, :], AX.X, ALU.add)
        m = V.do(nc.vector.tensor_scalar, neg_mean, total, -1.0 / D, None, ALU.mult, after=[m])
        m = V.do(nc.vector.tensor_tensor, xc[:, :, :], g.x_tok[:, :, :], up(neg_mean), ALU.add, after=[m])
        m = A.do(nc.scalar.activation, sq[:, :, :], xc[:, :, :], ACT.Square, after=[m])
        m = V.do(nc.vector.tensor_reduce, var, sq[:, :, :], AX.X, ALU.add, after=[m])
        m = A.do(nc.scalar.activation, rstd, var, ACT.Ln, bias=g.eps_ln[:, :], scale=1.0 / D, after=[m])
        m = A.do(nc.scalar.activation, rstd, rstd, ACT.Exp, scale=-0.5, after=[m])
        m = V.do(nc.vector.tensor_tensor, sq[:, :, :], xc[:, :, :], up(rstd), ALU.mult, after=[m])
        for b in range(NB):
            for c in range(4):
                t = T.do(nc.tensor.transpose, g.ps[b][:, c * 128:(c + 1) * 128], sq[:, b * 4 + c, :], g.ident[:, :], after=[m])
            if b % 2:
                last = A.do(nc.scalar.copy, g.xnT[:, b * 512:(b + 1) * 512], g.ps[b][:, :], after=[t])
            else:
                last2 = V.do(nc.vector.tensor_copy, g.xnT[:, b * 512:(b + 1) * 512], g.ps[b][:, :], after=[t])
        g.p.join()

def attention(g, w, tag):
    nc, p, V, A, T, G = g.nc, g.p, g.V, g.A, g.T, g.G
    with ExitStack() as mem:
        sb = lambda n, s, d=F32: mem.enter_context(nc.sbuf_tensor(f"{n}{g.uid()}", s, d))
        Q1 = [sb(f"q_max{i}", [ROWS, N], BF16) for i in range(2)]
        K1 = [sb(f"k_max{i}", [ROWS, N], BF16) for i in range(2)]
        Q2 = [sb(f"q_exp{i}", [ROWS + PARTS, N], BF16) for i in range(2)]
        K2 = [sb(f"k_exp{i}", [ROWS + PARTS, N], BF16) for i in range(2)]
        Vs = [sb(f"v_head{i}", [128, NT, 32]) for i in range(2)]
        v_tok = sb("v_tok", [128, NT, HEADS, HD])
        o_tok = sb("o_tok", [128, NT, HEADS, HD])
        PT = sb("probs", [128, 8, 512])
        mxp = [sb(f"max_parts{i}", [128, 64]) for i in range(2)]
        nmx = sb("neg_max", [128, NT])
        nhi = sb("neg_max_hi", [NT, PARTS, 128], BF16)
        nres = sb("neg_max_rest", [NT, 2, 128])
        osb = sb("pv_copy", [128, 512])
        rec = sb("recip_sums", [128, 4, 4])
        Ld1 = [p.stream(nc.sync, f"{tag}_load_max{i}", 16) for i in range(2)]
        Ld2 = [p.stream(nc.sync, f"{tag}_load_exp{i}", 16) for i in range(2)]
        Lmx = [p.stream(nc.sync, f"{tag}_load_negmax{i}", 16) for i in range(2)]
        Lsc = p.stream(nc.sync, f"{tag}_scratch", 16)
        S1b, S2b, PVb, misc = g.ps[0:3], g.ps[3:6], g.ps[6], g.ps[7]
        qs, ks = g.q_scratch, g.k_scratch

        part = sb("qk_parts", [128, 2, PARTS, 512], BF16)
        full = sb("qk_full", [128, 2, 512])
        rest = sb("qk_rest", [128, 2, 512])
        sent = [None, None]
        unit = 0
        evac = {}
        for wT, bias, dst in ((w["wqT"], w["bq"], qs), (w["wkT"], w["bk"], ks)):
            for b in range(NB):
                k = unit % 2
                mm = T.do(nc.tensor.matmul, g.ps[k][:, :], wT, g.xnT[:, b * 512:(b + 1) * 512], start=True, stop=True,
                          after=[evac.get(k)])
                f = evac[k] = V.do(nc.vector.tensor_scalar, full[:, k, :], g.ps[k][:, :], bias, None, ALU.add, after=[mm, V.last()])
                h = A.do(nc.scalar.copy, part[:, k, 0, :], full[:, k, :], after=[f, sent[k]])
                r = V.do(nc.vector.tensor_tensor, rest[:, k, :], full[:, k, :], part[:, k, 0, :], ALU.subtract, after=[h])
                h2 = A.do(nc.scalar.copy, part[:, k, 1, :], rest[:, k, :], after=[r])
                lo = V.do(nc.vector.tensor_tensor, part[:, k, 2, :], rest[:, k, :], part[:, k, 1, :], ALU.subtract, after=[h2, sent[k]])
                s = Lsc if k == 0 else g.Lsc2
                sent[k] = s.do(nc.sync.dma_start, dst[:, :, b * 512:(b + 1) * 512].rearrange("a p n -> p a n"), part[:, k, :, :], after=[lo])
                unit += 1
        for t in range(NT):
            bank = g.ps[2 + t // 4]
            o = bank[:, (t % 4) * 128:(t % 4) * 128 + 128]
            T.do(nc.tensor.matmul, o, g.xnT[:, t * 128:(t + 1) * 128], w["wvT"], start=True, stop=False)
            mm = T.do(nc.tensor.matmul, o, g.ones_row[:, 0:128], w["bv"], start=False, stop=True)
            if t % 4 == 3:
                A.do(nc.scalar.copy, v_tok[:, t - 3:t + 1, :, :], bank[:, :].rearrange("p (t h d) -> p t h d", t=4, h=HEADS), after=[mm])
        v_ready = A.last()
        ini = []
        for i in range(2):
            ini.append(G.do(nc.gpsimd.memset, Vs[i][:, :, :], 0.0))
            ini.append(G.do(nc.gpsimd.memset, Q2[i][:, :], 1.0))
            ini.append(G.do(nc.gpsimd.memset, K2[i][:, :], 1.0))
        for i in range(2):
            G.do(nc.gpsimd.memset, Vs[i][:, :, HD:HD + 1], 1.0, after=[ini[-1]])
        inited = G.last()

        def load(stream, Q, K, h, after):
            for a in range(PARTS):
                r = slice(a * PARTS * HD, (a + 1) * PARTS * HD)
                stream.do(nc.sync.dma_start, Q[r, :], qs[a:a + 1, bass.ts(h, HD), :].broadcast_to([PARTS, HD, N]), after=after)
                d = stream.do(nc.sync.dma_start, K[r, :], ks[:, bass.ts(h, HD), :], after=after)
            return d

        def stage_v(i, h, after):
            return G.do(nc.gpsimd.tensor_copy, Vs[i][:, :, 0:HD], v_tok[:, :, h, :] if isinstance(h, int) else
                        v_tok[:, :, :, :].rearrange("p t h d -> p t (h d)")[:, :, bass.ts(h, HD)], after=after)

        scratch_done = [Lsc.last(), g.Lsc2.last()]
        st = dict(red=[None] * 3, exp=[None] * 3, maxed=None, pv=[None] * 8, evac=None, s1end=[None, None], mxred=[None, None],
                  load1=[None, None], load2=[None, None], vs=[None, None], negmax=[None, None], misc=None,
                  s2end=[None, None], pvend=[None, None], nhi=None, recm=None, tr4=None)

        def scores_max(par, u, slot):
            t, b = u // 4, u % 4
            mm = T.do(nc.tensor.matmul, S1b[slot][:, :], Q1[par][:, t * 128:(t + 1) * 128], K1[par][:, b * 512:(b + 1) * 512],
                      start=True, stop=True, after=[st["red"][slot], st["load1"][par]])
            st["red"][slot] = V.do(nc.vector.tensor_reduce, mxp[par][:, u:u + 1], S1b[slot][:, :], AX.X, ALU.max,
                                    after=[mm] + ([st["mxred"][par]] if u == 0 else []))
            st["maxed"] = st["red"][slot]
            if u == 63:
                st["s1end"][par] = mm

        def maxima(par):
            m = V.do(nc.vector.tensor_reduce, nmx[:, :], mxp[par][:, :].rearrange("p (t b) -> p t b", b=4), AX.X, ALU.max,
                     negate=True, after=[st["maxed"], st["misc"]])
            st["mxred"][par] = m
            tr = T.do(nc.tensor.transpose, misc[0:NT, 0:128], nmx[:, :], g.ident[:, :], after=[m, st["recm"]])
            m = V.do(nc.vector.tensor_copy, nhi[:, 0, :], misc[0:NT, 0:128], after=[tr, st["nhi"]])
            m = V.do(nc.vector.tensor_tensor, nres[:, 0, :], misc[0:NT, 0:128], nhi[:, 0, :], ALU.subtract, after=[m])
            st["misc"] = m
            m = V.do(nc.vector.tensor_copy, nhi[:, 1, :], nres[:, 0, :], after=[m])
            m = V.do(nc.vector.tensor_tensor, nhi[:, 2, :], nres[:, 0, :], nhi[:, 1, :], ALU.subtract, after=[m])
            for r in range(PARTS):
                d = Lmx[par].do(nc.sync.dma_start, Q2[par][ROWS + r:ROWS + r + 1, :], nhi[:, r, :], after=[m, st["s2end"][par], inited])
            st["negmax"][par] = st["nhi"] = d

        def scores_exp(par, u, slot):
            t, j = u // 4, u % 4
            mm = T.do(nc.tensor.matmul, S2b[slot][:, :], K2[par][:, t * 128:(t + 1) * 128], Q2[par][:, j * 512:(j + 1) * 512],
                      start=True, stop=True, after=[st["exp"][slot], st["load2"][par], st["negmax"][par], inited])
            st["exp"][slot] = A.do(nc.scalar.activation, PT[:, u % 8, :], S2b[slot][:, :], ACT.Exp, scale=float(HD) ** -0.5,
                                    after=[mm, st["pv"][u % 8]])
            if u == 63:
                st["s2end"][par] = mm
            return st["exp"][slot]

        def values(par, u, probs):
            t, j = u // 4, u % 4
            st["pv"][u % 8] = T.do(nc.tensor.matmul, PVb[32 * j:32 * j + 32, :], Vs[par][:, t, :], PT[:, u % 8, :],
                                   start=(t == 0), stop=(t == NT - 1), after=[probs, st["evac"], st["vs"][par]])
            if u == 63:
                st["pvend"][par] = st["pv"][u % 8]

        def normalise(par, h):
            e = st["evac"] = A.do(nc.scalar.copy, osb[:, :], PVb[:, :], after=[st["pvend"][par], st["tr4"]])
            for c in range(4):
                tr = T.do(nc.tensor.transpose, misc[:, c * 128:(c + 1) * 128], osb[:, c * 128:(c + 1) * 128], g.ident[:, :],
                          after=[e, st["misc"], st["recm"]])
            st["tr4"] = tr
            turned = misc[:, :].rearrange("p (c j r) -> p c j r", c=4, j=4)
            m = V.do(nc.vector.reciprocal, rec[:, :, :], turned[:, :, :, HD], after=[tr, st["recm"]])
            out = o_tok[:, :, :, :].rearrange("p t h d -> p t (h d)")[:, :, bass.ts(h, HD)].rearrange("p (j c) d -> p c j d", c=4)
            st["recm"] = V.do(nc.vector.tensor_tensor, out, turned[:, :, :, 0:HD],
                              rec[:, :, :].unsqueeze(3).broadcast_to([128, 4, 4, HD]), ALU.mult, after=[m])

        def pair(h0, more, prev):
            probs = {}
            if more:
                st["load1"][0] = load(Ld1[0], Q1[0], K1[0], h0 + 2, [st["s1end"][0]])
            for v in range(128):
                w1 = v + 64 + LEAD
                if more or w1 < 128:
                    scores_max((w1 // 64) % 2, w1 % 64, v % 3)
                    if w1 % 64 == 63:
                        maxima((w1 // 64) % 2)
                        if more and w1 // 64 == 1:
                            st["load1"][1] = load(Ld1[1], Q1[1], K1[1], h0 + 3, [st["s1end"][1]])
                probs[v] = scores_exp(v // 64, v % 64, v % 3)
                if v % 4 == 3 and v >= 7:
                    for y in range(v - 7, v - 3):
                        values(y // 64, y % 64, probs[y])
                if v == 67:
                    normalise(0, h0)
                    if more:
                        st["load2"][0] = load(Ld2[0], Q2[0], K2[0], h0 + 2, [st["s2end"][0]])
                        st["vs"][0] = stage_v(0, h0 + 2, [st["pvend"][0]])
            for y in range(124, 128):
                values(1, y % 64, probs[y])
            normalise(1, h0 + 1)
            if more:
                st["load2"][1] = load(Ld2[1], Q2[1], K2[1], h0 + 3, [st["s2end"][1]])
                st["vs"][1] = stage_v(1, h0 + 3, [st["pvend"][1]])

        for i in range(2):
            st["load1"][i] = load(Ld1[i], Q1[i], K1[i], i, scratch_done)
            st["load2"][i] = load(Ld2[i], Q2[i], K2[i], i, scratch_done + [inited])
            st["vs"][i] = stage_v(i, i, [v_ready, inited])
        p.wait(nc.tensor, [V.last(), v_ready])
        for u in range(64):
            scores_max(0, u, u % 3)
        maxima(0)
        for u in range(LEAD):
            scores_max(1, u, u % 3)
        p.pipeline(HEADS // 2 - 1, lambda i: pair(2 * i, True, None), st)
        pair(HEADS - 2, False, None)
        p.join()

        oT = sb("o_T", [128, N])
        for b in range(NB):
            for c in range(4):
                t = 4 * b + c
                tr = T.do(nc.tensor.transpose, g.ps[b][:, c * 128:(c + 1) * 128], o_tok[:, t, :, :].rearrange("p h d -> p (h d)"), g.ident[:, :])
            A.do(nc.scalar.copy, oT[:, b * 512:(b + 1) * 512], g.ps[b][:, :], after=[tr])
        for b in range(NB):
            bank = g.ps[4 + b]
            for c in range(4):
                t = 4 * b + c
                o = bank[:, c * 128:(c + 1) * 128]
                T.do(nc.tensor.matmul, o, oT[:, t * 128:(t + 1) * 128], w["woT"], start=True, stop=False, after=[A.last()])
                mm = T.do(nc.tensor.matmul, o, g.ones_row[:, 0:128], w["bo"], start=False, stop=True)
            x = g.x_tok[:, 4 * b:4 * b + 4, :]
            V.do(nc.vector.tensor_tensor, x, x, bank[:, :].rearrange("p (t f) -> p t f", t=4), ALU.add, after=[mm])
        p.join()


FH, DK = 8, 64
NEXP = 4
KD = FH * DK
ST = 1 + NEXP

ORDER = "bbbbbacbabcbcacaaccbbabaaa" + "abc" * 4

def gla_ffn(g, w, tag):
    nc, p, V, A, T, G = g.nc, g.p, g.V, g.A, g.T, g.G
    with ExitStack() as mem:
        sb = lambda n, s, d=F32: mem.enter_context(nc.sbuf_tensor(f"{n}{g.uid()}", s, d))
        a1T = sb("low_rank_qk", [128, N])
        a2T = sb("low_rank_gates", [128, N])
        gate = sb("out_gate", [128, NT, KD])
        mask = sb("expert_mask", [128, NT, NEXP])
        prob = sb("expert_prob", [128, NT, NEXP])
        rw = sb("expert_weight", [128, NT])
        rws = sb("expert_weight_scaled", [128, NT])
        et = sb("expert_tmp", [128, NT])
        half = sb("half_mask", [128, NT, 2, NEXP])
        tri_s = sb("same_expert_tri", [128, NT, 128])
        cum_s = sb("same_expert_cum", [128, NT, 128])
        early = ExitStack()
        maskT = early.enter_context(nc.sbuf_tensor(f"expert_maskT{g.uid()}", [NEXP, N], F32))
        m = G.do(nc.gpsimd.memset, a2T[64:128, :], 1.0)
        for b in range(NB):
            c = slice(b * 512, (b + 1) * 512)
            m1 = T.do(nc.tensor.matmul, g.ps[b][:, :], w["Wa"][:, 0:128], g.xnT[:, c], start=True, stop=True)
            A.do(nc.scalar.copy, a1T[:, c], g.ps[b][:, :], after=[m1])
            o = g.ps[4 + b]
            T.do(nc.tensor.matmul, o[0:64, :], w["Wa"][:, 128:192], g.xnT[:, c], start=True, stop=True)
            T.do(nc.tensor.matmul, o[64:80, :], w["Wa"][:, 192:208], g.xnT[:, c], start=True, stop=True)
            m2 = T.do(nc.tensor.matmul, o[96:112, :], w["Wa"][:, 208:224], g.xnT[:, c], start=True, stop=True)
            V.do(nc.vector.tensor_copy, a2T[0:64, c], o[0:64, :], after=[m2])
            V.do(nc.vector.tensor_copy, a2T[64:80, c], o[64:80, :], after=[m])
            V.do(nc.vector.tensor_copy, a2T[96:112, c], o[96:112, :])
        le = g.ps[0][:, 0:NT * NEXP].rearrange("p (t e) -> p t e", e=NEXP)
        for t in range(NT):
            mm = T.do(nc.tensor.matmul, g.ps[0][:, t * NEXP:(t + 1) * NEXP], g.xnT[:, t * 128:(t + 1) * 128], w["We"], start=True, stop=True, after=[A.last()])
        up = lambda ap, k: ap.unsqueeze(2).broadcast_to([128, NT, k])
        m = V.do(nc.vector.tensor_reduce, et[:, :], le, AX.X, ALU.max, after=[mm])
        m = V.do(nc.vector.tensor_tensor, prob[:, :, :], le, up(et[:, :], NEXP), ALU.subtract, after=[m])
        m = A.do(nc.scalar.activation, prob[:, :, :], prob[:, :, :], ACT.Exp, after=[m])
        m = V.do(nc.vector.tensor_reduce, et[:, :], prob[:, :, :], AX.X, ALU.add, after=[m])
        m = V.do(nc.vector.reciprocal, et[:, :], et[:, :], after=[m])
        m = V.do(nc.vector.tensor_tensor, prob[:, :, :], prob[:, :, :], up(et[:, :], NEXP), ALU.mult, after=[m])
        m = V.do(nc.vector.tensor_reduce, rw[:, :], prob[:, :, :], AX.X, ALU.max, after=[m])
        V.do(nc.vector.tensor_scalar, rws[:, :], rw[:, :], DK ** -0.5, None, ALU.mult, after=[m])
        m = V.do(nc.vector.tensor_tensor, mask[:, :, :], prob[:, :, :], up(rw[:, :], NEXP), ALU.is_equal, after=[m])
        m = V.do(nc.vector.tensor_copy, et[:, :], mask[:, :, 0], after=[m])
        for e in range(1, NEXP):
            m = V.do(nc.vector.tensor_tensor, mask[:, :, e], mask[:, :, e], et[:, :], ALU.is_gt, after=[m])
            m = V.do(nc.vector.tensor_tensor, et[:, :], et[:, :], mask[:, :, e], ALU.add, after=[m])
        for k in range(2):
            V.do(nc.vector.tensor_scalar, half[:, :, k, :], mask[:, :, :], g.half_col[:, k:k + 1], None, ALU.mult, after=[m])
        masked = V.last()
        for t in range(NT):
            tr = T.do(nc.tensor.transpose, g.ps[1 + t // 4][0:NEXP, (t % 4) * 128:(t % 4) * 128 + 128], mask[:, t, :], g.ident[:, :], after=[masked])
            if t % 4 == 3:
                A.do(nc.scalar.copy, maskT[:, (t - 3) * 128:(t + 1) * 128], g.ps[1 + t // 4][0:NEXP, :], after=[tr])
        for b in range(NB):
            bank = g.ps[4 + b]
            for c in range(4):
                ts = slice((4 * b + c) * 128, (4 * b + c + 1) * 128)
                mm = T.do(nc.tensor.matmul, bank[:, c * 128:(c + 1) * 128], maskT[:, ts], maskT[:, ts], start=True, stop=True, after=[A.last(), V.last()])
            same = bank[:, :].rearrange("p (t k) -> p t k", t=4)
            four = lambda ap: ap.unsqueeze(1).broadcast_to([128, 4, 128])
            V.do(nc.vector.tensor_tensor, tri_s[:, 4 * b:4 * b + 4, :], same, four(g.tri[:, :]), ALU.mult, after=[mm])
            V.do(nc.vector.tensor_tensor, cum_s[:, 4 * b:4 * b + 4, :], same, four(g.cum[:, :]), ALU.mult)
        p.join()
        early.close()
        nc.scalar.preload_act_table(ACT.Silu)
        used = [None] * 4
        for t in range(NT):
            k = t % 4
            mm = T.do(nc.tensor.matmul, g.ps[k][:, :], a2T[0:64, t * 128:(t + 1) * 128], w["Wc"][0:64, :], start=True, stop=True, after=[used[k]])
            s = used[k] = A.do(nc.scalar.activation, gate[:, t, :], g.ps[k][:, :], ACT.Silu, after=[mm])
            V.do(nc.vector.tensor_tensor, gate[:, t, :].rearrange("p (h e) -> p h e", h=FH), gate[:, t, :].rearrange("p (h e) -> p h e", h=FH),
                 w["norm"].unsqueeze(1).broadcast_to([128, FH, DK]), ALU.mult, after=[s])
        nc.scalar.preload_act_table_set("natural_log_exp_and_others")

        two = lambda n, s, d=F32: [sb(f"{n}{i}", s, d) for i in range(2)]
        xs, a1s, a2s, cs = two("x_tile", [128, 128]), two("qk_tile", [128, 128]), two("gate_tile", [128, 128]), two("cum_tile", [128, 128])
        v_t, vm = two("v_tile", [128, FH, DK]), two("v_experts", [128, FH, NEXP, DK])
        ms = two("mask_tile", [128, NEXP])
        qg, kg = two("q_decayed", [128, 2, KD]), two("k_decayed", [128, 2, KD])
        qT, kT = two("q_decayedT", [128, 2, 4, 128]), two("k_decayedT", [128, 2, 4, 128])
        eh = two("exp_halves", [128, 4, 2, ST])
        gk = sb("log_decay", [128, 2, KD])
        ab = sb("abs_logit", [128, 2, KD])
        eg, en = sb("exp_cum", [128, 2, KD]), sb("exp_neg_cum", [128, 2, KD])
        k2 = sb("k_softmax", [128, KD])
        ks1 = sb("k_stats", [128, FH])
        sA = sb("scores_dense", [128, 2, 4, 128])
        sB = sb("scores_expert", [128, 2, 4, 128])
        SX, SD = sb("state_experts", [128, 4, NEXP, DK]), sb("state_dense", [128, 4, 2, DK])
        U = sb("state_end", [128, 4, ST, DK])
        dec = sb("state_decay", [128, 4, ST])
        o_t, o_q = two("out_tile", [128, KD]), sb("out_square", [128, KD])
        rms = sb("out_rms", [128, FH])
        oT = sb("out_T", [128, 4, 128])
        i1 = G.do(nc.gpsimd.memset, U[:, :, :, :], 0.0)
        i3 = G.do(nc.gpsimd.memset, SD[:, :, :, :], 0.0)
        i2 = G.do(nc.gpsimd.memset, eh[1][:, :, :, :], 1.0)
        hv = lambda ap: ap.rearrange("p (h e) -> p h e", h=FH)
        P3, Abank, Obank, Ybank = g.ps[0:3], g.ps[3:5], g.ps[5], g.ps[6:8]

        st = dict(bank=[None] * 3, A=[None] * 2, O=None, Y=[None] * 2, B=[None] * 2, gk=None, eg=None, gkr=None, kgd=None, k2=None, xs=None, U=None,
                  Send=None, O_read=None, turn=[None, None], out=[None, None], out_read=[None, None], oT_read=None, rms_read=None, staged=[None, None], projected=[None, None])
        nb = [0]

        def bank(*more):
            k = nb[0] % 3
            nb[0] += 1
            return k, P3[k]

        def stage_tile(q, t):
            for dst, src in ((a2s[q], a2T[:, bass.ts(t, 128)]), (a1s[q], a1T[:, bass.ts(t, 128)]), (xs[q], g.xnT[:, bass.ts(t, 128)]),
                             (cs[q], cum_s[:, :, :].rearrange("p t k -> p (t k)")[:, bass.ts(t, 128)])):
                st["staged"][q] = G.do(nc.gpsimd.tensor_copy, dst[:, :], src, after=[st["projected"][q]])

        def stage_a(q, t, st, more):
            free, c = st["B"][q], st["staged"][q]
            zs = []
            for k, r in ((0, 64), (1, 96)):
                b, ps = bank()
                mm = T.do(nc.tensor.matmul, ps[:, :], a2s[q][r:r + 17, :], w["Wc"][r:r + 17, :], start=True, stop=True, after=[c, st["bank"][b]])
                m = A.do(nc.scalar.activation, ab[:, k, :], ps[:, :], ACT.Abs, after=[mm, st["gk"]])
                z = V.do(nc.vector.tensor_scalar, gk[:, k, :], ps[:, :], 0.0, 1 / 16.0, ALU.min, ALU.mult, after=[m, st["gkr"]])
                st["bank"][b] = z
            m = A.do(nc.scalar.activation, ab[:, :, :], ab[:, :, :], ACT.Exp, scale=-1.0, after=[m])
            m = A.do(nc.scalar.activation, ab[:, :, :], ab[:, :, :], ACT.Ln, bias=1.0, after=[m])
            mc = G.do(nc.gpsimd.tensor_copy, ms[q][:, :], mask[:, :, :].rearrange("p t e -> p (t e)")[:, bass.ts(t, NEXP)], after=[free])
            b, ps = bank()
            mm = T.do(nc.tensor.matmul, ps[:, :], xs[q][:, :], w["Wp"][:, 1024:1536], start=True, stop=True, after=[c, st["bank"][b]])
            vv = st["bank"][b] = A.do(nc.scalar.copy, v_t[q][:, :, :].rearrange("p h e -> p (h e)"), ps[:, :], after=[mm, free])
            for e in range(NEXP):
                G.do(nc.gpsimd.tensor_scalar, vm[q][:, :, e, :], v_t[q][:, :, :], ms[q][:, e:e + 1], 1.0, ALU.mult, ALU.mult, after=[vv, mc, free])
            yield
            b, ps = bank()
            mm = T.do(nc.tensor.matmul, ps[:, :], a1s[q][64:128, :], w["Wb"][64:128, :], start=True, stop=True, after=[c, st["bank"][b]])
            r = V.do(nc.vector.tensor_reduce, ks1[:, :], hv(ps[:, :]), AX.X, ALU.max, after=[mm])
            gm = st["gk"] = V.do(nc.vector.scalar_tensor_tensor, gk[:, :, :], ab[:, :, :], -1 / 16.0, gk[:, :, :], ALU.mult, ALU.add, after=[m, z])
            bc = lambda ap: ap.unsqueeze(2).broadcast_to([128, FH, DK])
            r = st["bank"][b] = V.do(nc.vector.tensor_tensor, hv(k2[:, :]), hv(ps[:, :]), bc(ks1[:, :]), ALU.subtract, after=[r])
            r = A.do(nc.scalar.activation, k2[:, :], k2[:, :], ACT.Exp, after=[r])
            es = []
            for k, lhs in ((0, g.cum), (1, cs[q])):
                b, ps = bank()
                mm = T.do(nc.tensor.matmul, ps[:, :], lhs[:, :], gk[:, k, :], start=True, stop=True, after=[gm, c, st["bank"][b]])
                A.do(nc.scalar.activation, eg[:, k, :], ps[:, :], ACT.Exp, after=[mm, st["kgd"]])
                st["bank"][b] = A.do(nc.scalar.activation, en[:, k, :], ps[:, :], ACT.Exp, scale=-1.0)
                es.append(st["bank"][b])
            yield
            b, ps = bank()
            for pr in range(4):
                o = ps[:, pr * 16:pr * 16 + 10].rearrange("p (k s) -> p k s", s=ST)
                T.do(nc.tensor.matmul, o[:, :, 0], gk[:, 0, pr * 128:(pr + 1) * 128], g.half_col[:, :], start=True, stop=True, after=[st["bank"][b]])
                mm = T.do(nc.tensor.matmul, o[:, :, 1:ST], gk[:, 1, pr * 128:(pr + 1) * 128],
                          half[:, :, :, :].rearrange("p t k e -> p t (k e)")[:, bass.ds(t, 1), :].rearrange("p t (k e) -> p (t k) e", k=2),
                          start=True, stop=True)
            st["gkr"] = mm
            st["bank"][b] = A.do(nc.scalar.activation, eh[q][:, :, :, :].rearrange("p r k s -> p r (k s)"),
                                 ps[:, 0:64].rearrange("p (r x) -> p r x", r=4)[:, :, 0:10], ACT.Exp, after=[mm, free])
            s = V.do(nc.vector.tensor_reduce, ks1[:, :], hv(k2[:, :]), AX.X, ALU.add, after=[r])
            s = V.do(nc.vector.reciprocal, ks1[:, :], ks1[:, :], after=[s])
            s = V.do(nc.vector.tensor_scalar, ks1[:, :], ks1[:, :], rw[:, bass.ds(t, 1)], None, ALU.mult, after=[s])
            s = V.do(nc.vector.tensor_tensor, hv(k2[:, :]), hv(k2[:, :]), bc(ks1[:, :]), ALU.mult, after=[s])
            s = V.do(nc.vector.tensor_tensor, kg[q][:, 1, :], k2[:, :], en[:, 1, :], ALU.mult, after=[s, es[1], free])
            yield
            def turn(src, dst, k, made):
                b, ps = bank()
                for pr in range(4):
                    tr = T.do(nc.tensor.transpose, ps[:, pr * 128:(pr + 1) * 128], src[:, k, pr * 128:(pr + 1) * 128], g.ident[:, :], after=[made, st["bank"][b]])
                eng, fn = ((A, nc.scalar.copy), (V, nc.vector.tensor_copy))[k]
                st["turn"][k] = st["bank"][b] = eng.do(fn, dst[:, k, :, :].rearrange("p r t -> p (r t)"), ps[:, :], after=[tr, free])

            b, ps = bank()
            mm = T.do(nc.tensor.matmul, ps[:, :], xs[q][:, :], w["Wp"][:, 512:1024], start=True, stop=True, after=[st["bank"][b]])
            k1 = st["bank"][b] = V.do(nc.vector.tensor_tensor, kg[q][:, 0, :], ps[:, :], en[:, 0, :], ALU.mult, after=[mm, es[0], free])
            b, ps = bank()
            mm = T.do(nc.tensor.matmul, ps[:, :], a1s[q][0:64, :], w["Wb"][0:64, :], start=True, stop=True, after=[st["bank"][b]])
            q2 = st["bank"][b] = V.do(nc.vector.scalar_tensor_tensor, qg[q][:, 1, :], ps[:, :], rws[:, bass.ds(t, 1)], eg[:, 1, :], ALU.mult, ALU.mult, after=[mm, free])
            yield
            turn(kg[q], kT[q], 1, s)
            b, ps = bank()
            mm = T.do(nc.tensor.matmul, ps[:, :], xs[q][:, :], w["Wp"][:, 0:512], start=True, stop=True, after=[st["bank"][b]])
            q1 = st["bank"][b] = st["kgd"] = V.do(nc.vector.scalar_tensor_tensor, qg[q][:, 0, :], ps[:, :], DK ** -0.5, eg[:, 0, :], ALU.mult, ALU.mult, after=[mm, free])
            st["projected"][q] = mm
            if more:
                stage_tile(q, t + 2)
            yield
            turn(kg[q], kT[q], 0, k1)
            yield
            turn(qg[q], qT[q], 1, q2)
            yield
            turn(qg[q], qT[q], 0, q1)
            yield

        def stage_b(q, t, st):
            o_s = o_t[q]
            turned = list(st["turn"])
            d = V.do(nc.vector.tensor_tensor, dec[:, :, :], eh[1 - q][:, :, 1, :], eh[q][:, :, 0, :], ALU.mult, after=turned + [st["Send"]])
            wide = lambda ap, k: ap.unsqueeze(3).broadcast_to([ap.shape[0], 4, k, DK])
            for x in range(2):
                r = slice(64 * x, 64 * x + 64)
                sd = V.do(nc.vector.tensor_tensor, SD[r, :, x, :], U[r, :, 0, :], dec[r, :, 0:1].broadcast_to([64, 4, DK]), ALU.mult,
                          after=[d, st["U"], st["Send"]])
            sm = G.do(nc.gpsimd.tensor_tensor, SX[:, :, :, :], U[:, :, 1:ST, :], wide(dec[:, :, 1:ST], NEXP), ALU.mult,
                      after=[d, st["U"], st["Send"]])
            for k, dst in ((0, sA), (1, sB)):
                for x in range(2):
                    r = slice(64 * x, 64 * x + 64)
                    for y in range(4):
                        mm = T.do(nc.tensor.matmul, Abank[x][:, y * 128:y * 128 + 128], kT[q][r, k, y, :], qT[q][r, k, y, :],
                                  start=True, stop=True, after=turned + [st["A"][x]])
                    mt = g.tri[:, :] if k == 0 else tri_s[:, :, :].rearrange("p t k -> p (t k)")[:, bass.ts(t, 128)]
                    st["A"][x] = V.do(nc.vector.tensor_tensor, dst[:, x, :, :], Abank[x][:, :].rearrange("p (h t) -> p h t", h=4),
                                      mt.unsqueeze(1).broadcast_to([128, 4, 128]), ALU.mult, after=[mm, st["O"]])
                    yield
            scored = V.last()
            ao = G.do(nc.gpsimd.tensor_tensor, sA[:, :, :, :], sA[:, :, :, :], sB[:, :, :, :], ALU.add, after=[scored])

            def on_states(z):
                x = z % 2
                r = slice(64 * x, 64 * x + 64)
                for y in (0, 1):
                    mm = T.do(nc.tensor.matmul, Ybank[x][:, y * 256:y * 256 + 256], qT[q][r, 1, 2 * (z // 2) + y, :], SX[r, 2 * (z // 2) + y, :, :],
                              start=True, stop=True, after=[sm, st["Y"][x]])
                return mm

            ys = [on_states(0), on_states(1)]
            yield
            for y in range(4):
                T.do(nc.tensor.matmul, Obank[:, y * 128:(y + 1) * 128], qT[q][:, 0, y, :], SD[:, y, :, :], start=True, stop=False, after=[sd, st["O_read"]],
                     skip_group_check=True)
                for x in range(2):
                    h = 2 * y + x
                    mm = T.do(nc.tensor.matmul, Obank[:, h * DK:(h + 1) * DK], sA[:, x, y, :], v_t[q][:, h, :], start=False, stop=True, after=[ao],
                              skip_group_check=True)
            st["O"] = mm
            oc = st["O_read"] = A.do(nc.scalar.copy, o_s[:, :], Obank[:, :], after=[mm, st["out_read"][q]])
            yield
            for z in range(4):
                x = z % 2
                if z >= 2:
                    ys.append(on_states(z))
                o2 = o_s[:, :].rearrange("p (y x e) -> p y x e", x=2, e=DK)[:, 2 * (z // 2):2 * (z // 2) + 2, x, :]
                y = Ybank[x][:, :].rearrange("p (h x e) -> p h x e", h=2, x=NEXP)
                m = oc
                for e in range(NEXP):
                    m = V.do(nc.vector.scalar_tensor_tensor, o2, y[:, :, e, :], mask[:, :, :].rearrange("p t e -> p (t e)")[:, bass.ds(t * NEXP + e, 1)], o2,
                             ALU.mult, ALU.add, after=[ys[z], m])
                st["Y"][x] = m
            st["out"][q] = m
            yield
            for x in range(3):
                bnk = (Abank[0], Abank[1], Ybank[0])[x]
                prev = (st["A"][0], st["A"][1], st["Y"][0])[x]
                if x < 2:
                    for h in range(4 * x, 4 * x + 4):
                        r = slice(64 * (h % 2), 64 * (h % 2) + 64)
                        mm = T.do(nc.tensor.matmul, bnk[r, (h // 2 % 2) * 256:(h // 2 % 2) * 256 + 256], kg[q][:, 1, h * DK:(h + 1) * DK], vm[q][:, h, :, :],
                                  start=True, stop=True, after=[prev, G.last()])
                    m = V.do(nc.vector.tensor_tensor, U[:, 2 * x:2 * x + 2, 1:ST, :], SX[:, 2 * x:2 * x + 2, :, :],
                             bnk[:, :].rearrange("p (r x e) -> p r x e", r=2, x=NEXP), ALU.add, after=[mm, sm])
                    st["A"][x] = m
                else:
                    for h in range(FH):
                        r = slice(64 * (h % 2), 64 * (h % 2) + 64)
                        mm = T.do(nc.tensor.matmul, bnk[r, (h // 2) * DK:(h // 2 + 1) * DK], kg[q][:, 0, h * DK:(h + 1) * DK], v_t[q][:, h, :],
                                  start=True, stop=True, after=[prev])
                    for y in range(2):
                        r = slice(64 * y, 64 * y + 64)
                        m = V.do(nc.vector.tensor_tensor, U[r, :, 0, :], SD[r, :, y, :], bnk[r, 0:256].rearrange("p (r e) -> p r e", r=4), ALU.add, after=[mm])
                    st["Y"][0] = m
            st["B"][q] = mm
            st["U"] = st["Send"] = m

        def stage_c(q, t, st):
            o_s = o_t[q]
            m = A.do(nc.scalar.activation, o_q[:, :], o_s[:, :], ACT.Square, after=[st["out"][q], st["rms_read"]])
            gt = G.do(nc.gpsimd.tensor_tensor, o_s[:, :], o_s[:, :], gate[:, :, :].rearrange("p t k -> p (t k)")[:, bass.ts(t, KD)], ALU.mult, after=[m])
            yield
            m = V.do(nc.vector.tensor_reduce, rms[:, :], hv(o_q[:, :]), AX.X, ALU.add, after=[m])
            st["rms_read"] = m
            m = A.do(nc.scalar.activation, rms[:, :], rms[:, :], ACT.Ln, bias=g.eps_ln[:, :], scale=1.0 / DK, after=[m])
            m = A.do(nc.scalar.activation, rms[:, :], rms[:, :], ACT.Exp, scale=-0.5, after=[m])
            yield
            m = V.do(nc.vector.tensor_tensor, hv(o_s[:, :]), hv(o_s[:, :]), rms[:, :].unsqueeze(2).broadcast_to([128, FH, DK]), ALU.mult, after=[m, gt])
            yield
            b, ps = bank()
            for c in range(4):
                tr = T.do(nc.tensor.transpose, ps[:, c * 128:(c + 1) * 128], o_s[:, c * 128:(c + 1) * 128], g.ident[:, :], after=[m, st["bank"][b]])
            st["out_read"][q] = tr
            m = st["bank"][b] = A.do(nc.scalar.copy, oT[:, :, :].rearrange("p c t -> p (c t)"), ps[:, :], after=[tr, st["oT_read"]])
            yield
            b, ps = bank()
            for c in range(4):
                mm = T.do(nc.tensor.matmul, ps[:, 0:128], oT[:, c, :], w["Wo"][:, c * 128:(c + 1) * 128], start=(c == 0), stop=(c == 3), after=[m, st["bank"][b]])
            st["oT_read"] = mm
            x = g.x_tok[:, :, :].rearrange("p t d -> p (t d)")[:, bass.ts(t, 128)]
            st["bank"][b] = V.do(nc.vector.tensor_tensor, x, x, ps[:, 0:128], ALU.add, after=[mm])
            yield

        def together(*gens):
            gens = list(gens)
            while gens:
                for x in list(gens):
                    if next(x, "end") == "end":
                        gens.remove(x)

        p.join()
        stage_tile(0, 0)
        stage_tile(1, 1)
        together(stage_a(0, 0, st, True))

        def step(t, par, after, before, more=True):
            stages = dict(b=stage_b(par, t, st), a=stage_a(1 - par, t + 1, st, more) if after else iter(()),
                          c=stage_c(1 - par, t - 1, st) if before else iter(()))
            for name in ORDER:
                next(stages[name], None)

        def tiles(t):
            nb[0] = 0
            step(t, 1, True, True)
            step(t + 1, 0, True, True)

        step(0, 0, True, False)
        p.pipeline(NT // 2 - 2, lambda i: tiles(2 * i + 1), st)
        step(NT - 3, 1, True, True, False)
        step(NT - 2, 0, True, True, False)
        step(NT - 1, 1, False, True)
        together(stage_c(1, NT - 1, st))
        p.join()


DI, NS, RANK, CONV = 256, 16, 8, 4
CHK = 1024

def mamba(g, w, tag):
    nc, p, V, A, T, G = g.nc, g.p, g.V, g.A, g.T, g.G
    with ExitStack() as mem:
        sb = lambda n, s, d=F32: mem.enter_context(nc.sbuf_tensor(f"{n}{g.uid()}", s, d))
        res, xi = sb("silu_res", [128, 2, N]), sb("conv_out", [128, 2, N])
        dt, dtx = sb("dt", [128, 2, N]), sb("dt_x", [128, 2, N])
        BC = sb("bc_parts", [96, N], BF16)
        sel = sb("row_select", [96, 2 * NS, 128], BF16)
        negA = sb("neg_A", [128, 2, NS])
        with ExitStack() as early:
            sbe = lambda n, s, d=F32: early.enter_context(nc.sbuf_tensor(f"{n}{g.uid()}", s, d))
            xp = sbe("conv_in", [128, 2, CONV - 1 + N])
            bcf = sbe("bc_full", [32, 2, N])
            dlt = sbe("delta", [RANK, N])
            z = G.do(nc.gpsimd.memset, xp[:, :, 0:CONV - 1], 0.0)
            m = G.do(nc.gpsimd.memset, sel[:, :, :], 0.0)
            for k in range(3):
                m = G.do(nc.gpsimd.affine_select, out=sel[:, :, :], in_=sel[:, :, :], compare_op=ALU.not_equal, fill=1.0, base=-32 * k,
                         pattern=[[-1, 2 * NS], [0, 128]], channel_multiplier=1, after=[m])
            m = A.do(nc.scalar.activation, negA[:, :, :], w["A_log"], ACT.Exp)
            V.do(nc.vector.tensor_scalar, negA[:, :, :], negA[:, :, :], -1.0, None, ALU.mult, after=[m])
            nc.scalar.preload_act_table(ACT.Silu)
            free = [None] * 8
            conv = []
            for c in range(4):
                for b in range(NB):
                    k = (c * NB + b) % 8
                    ts = slice(b * 512, (b + 1) * 512)
                    mm = T.do(nc.tensor.matmul, g.ps[k][:, :], w["in_proj"][:, c * 128:(c + 1) * 128], g.xnT[:, ts], start=True, stop=True, after=[free[k]])
                    if c < 2:
                        free[k] = A.do(nc.scalar.copy, xp[:, c, CONV - 1 + b * 512:CONV - 1 + (b + 1) * 512], g.ps[k][:, :], after=[mm])
                    else:
                        free[k] = A.do(nc.scalar.activation, res[:, c - 2, ts], g.ps[k][:, :], ACT.Silu, after=[mm])
                if c < 2:
                    m = V.do(nc.vector.tensor_scalar, xi[:, c, :], xp[:, c, 0:N], w["conv_w"][:, c, 0:1], w["conv_b"][:, c:c + 1], ALU.mult, ALU.add,
                             after=[free[k], z])
                    for q in range(1, CONV):
                        m = V.do(nc.vector.scalar_tensor_tensor, xi[:, c, :], xp[:, c, q:q + N], w["conv_w"][:, c, q:q + 1], xi[:, c, :], ALU.mult, ALU.add, after=[m])
                    conv.append(m)
            for c in range(2):
                a = A.do(nc.scalar.activation, xi[:, c, :], xi[:, c, :], ACT.Silu, after=[conv[c]])
            for b in range(NB):
                ts = slice(b * 512, (b + 1) * 512)
                k0, k1 = 2 * (b % 2), 2 * (b % 2) + 1
                for c in range(2):
                    mb = T.do(nc.tensor.matmul, g.ps[k0][0:32, :], w["x_proj"][:, c, RANK:RANK + 32], xi[:, c, ts], start=(c == 0), stop=(c == 1), after=[a, free[k0], free[k1]])
                for c in range(2):
                    md = T.do(nc.tensor.matmul, g.ps[k1][0:RANK, :], w["x_proj"][:, c, 0:RANK], xi[:, c, ts], start=(c == 0), stop=(c == 1))
                f0 = V.do(nc.vector.tensor_copy, bcf[:, 0, ts], g.ps[k0][0:32, :], after=[mb])
                f1 = V.do(nc.vector.tensor_copy, dlt[:, ts], g.ps[k1][0:RANK, :], after=[md])
                free[k0], free[k1] = f0, f1
            m = V.do(nc.vector.tensor_copy, BC[0:32, :], bcf[:, 0, :], after=[f0])
            m = V.do(nc.vector.tensor_tensor, bcf[:, 1, :], bcf[:, 0, :], BC[0:32, :], ALU.subtract, after=[m])
            m = V.do(nc.vector.tensor_copy, BC[32:64, :], bcf[:, 1, :], after=[m])
            m = A.do(nc.scalar.copy, bcf[:, 0, :], BC[32:64, :], after=[m])
            m = V.do(nc.vector.tensor_tensor, BC[64:96, :], bcf[:, 1, :], bcf[:, 0, :], ALU.subtract, after=[m])
            nc.scalar.preload_act_table_set("natural_log_exp_and_others")
            zb = xp[:, :, 0:N]
            ee, uu = dtx, sbe("one_plus_e", [128, N])
            for c in range(2):
                for b in range(NB):
                    k = 4 + (c * NB + b) % 4
                    ts = slice(b * 512, (b + 1) * 512)
                    mm = T.do(nc.tensor.matmul, g.ps[k][:, :], w["dt_w"][0:RANK, c * 128:(c + 1) * 128], dlt[:, ts], start=True, stop=True, after=[f1, free[k]])
                    free[k] = A.do(nc.scalar.activation, zb[:, c, ts], g.ps[k][:, :], ACT.Identity, bias=w["dt_b"][:, c:c + 1], after=[mm, V.last()])
                m = A.do(nc.scalar.activation, ee[:, c, :], zb[:, c, :], ACT.Abs, after=[free[k]])
                m = A.do(nc.scalar.activation, ee[:, c, :], ee[:, c, :], ACT.Exp, scale=-1.0, after=[m])
                u = V.do(nc.vector.tensor_scalar, uu[:, :], ee[:, c, :], 1.0, None, ALU.add, after=[m])
                ln = A.do(nc.scalar.activation, dt[:, c, :], uu[:, :], ACT.Ln, after=[u])
                m = V.do(nc.vector.scalar_tensor_tensor, ee[:, c, :], uu[:, :], 1.0, ee[:, c, :], ALU.subtract, ALU.subtract, after=[u])
                m = V.do(nc.vector.tensor_tensor, dt[:, c, :], dt[:, c, :], ee[:, c, :], ALU.subtract, after=[ln, m])
                m = V.do(nc.vector.scalar_tensor_tensor, dt[:, c, :], zb[:, c, :], 0.0, dt[:, c, :], ALU.max, ALU.add, after=[m])
                V.do(nc.vector.tensor_tensor, dtx[:, c, :], dt[:, c, :], xi[:, c, :], ALU.mult, after=[m])
            p.join()
        nc.scalar.preload_act_table_set("natural_log_exp_and_others")
        E = [[sb(f"decay{i}{c}", [128, CHK]) for c in range(2)] for i in range(2)]
        F = [[sb(f"state{i}{c}", [128, CHK]) for c in range(2)] for i in range(2)]
        Cs = [sb(f"c_row{i}", [128, CHK]) for i in range(2)]
        carry = sb("state_carry", [128, 2, NS])
        zero = sb("zero_row", [1, 512], BF16)
        y = sb("scan_out", [128, 2, N])
        G.do(nc.gpsimd.memset, carry[:, :, :], 0.0)
        zz = G.do(nc.gpsimd.memset, zero[:, :], 0.0)
        Bb, Cb, Yb = g.ps[0:2], g.ps[2:4], g.ps[4:8]
        for chunk in range(N // CHK):
            t0 = chunk * CHK
            st = dict(B=[None, None], C=None, E=[[None, None], [None, None]], Cs=[None, None], Fh=[[None, None], [None, None]], car=[[None, None], [None, None]])
            for k in range(4):
                T.do(nc.tensor.matmul, Yb[k][:, :], zero[:, 0:128], zero[:, :], start=True, stop=True, after=[zz, V.last()], skip_group_check=True)

            def front(n, i):
                for b in range(2):
                    ts = slice(t0 + b * 512, t0 + (b + 1) * 512)
                    mb = T.do(nc.tensor.matmul, Bb[b][:, :], sel[:, bass.ds(n, 1), :].rearrange("p a b -> p (a b)"), BC[:, ts], start=True, stop=True, after=[st["B"][1]])
                for b in range(2):
                    ts = slice(t0 + b * 512, t0 + (b + 1) * 512)
                    mc = T.do(nc.tensor.matmul, Cb[b][:, :], sel[:, bass.ds(n + NS, 1), :].rearrange("p a b -> p (a b)"), BC[:, ts], start=True, stop=True, after=[st["C"]])
                dec = []
                for c in range(2):
                    dec.append(A.do(nc.scalar.activation, E[i][c][:, :], dt[:, c, t0:t0 + CHK], ACT.Exp, scale=negA[:, c, bass.ds(n, 1)], after=[st["E"][i][c]]))
                cb = st["C"] = A.do(nc.scalar.copy, Cs[i][:, :], g.wide(2)[:, :], after=[mc, st["Cs"][i]])
                for c in range(2):
                    st["B"][c] = V.do(nc.vector.tensor_tensor, F[i][c][:, :], dtx[:, c, t0:t0 + CHK], g.wide(0)[:, :], ALU.mult, after=[mb, st["Fh"][i][c], st["car"][i][c]])
                for c in range(2):
                    h = V.do(nc.vector.tensor_tensor_scan, F[i][c][:, :], E[i][c][:, :], F[i][c][:, :], carry[:, c, bass.ds(n, 1)], ALU.mult, ALU.add,
                             after=[dec[c], st["B"][c]])
                    st["car"][i][c] = A.do(nc.scalar.copy, carry[:, c, bass.ds(n, 1)], F[i][c][:, CHK - 1:CHK], after=[h])
                    st["Cs"][i] = st["Fh"][i][c] = G.do(nc.gpsimd.tensor_tensor, E[i][c][:, :], F[i][c][:, :], Cs[i][:, :], ALU.mult, after=[h, cb])

            def back(i):
                for c in range(2):
                    for b in range(2):
                        st["E"][i][c] = T.do(nc.tensor.matmul, Yb[2 * c + b][:, :], g.ident[:, :], E[i][c][:, b * 512:(b + 1) * 512], start=False, stop=True,
                                             after=[st["Fh"][i][c]], skip_group_check=True)

            def pair(n0):
                front(n0 + 1, 1)
                back(0)
                front(n0 + 2, 0)
                back(1)

            p.join()
            front(0, 0)
            p.pipeline(NS // 2 - 1, lambda i: pair(2 * i), st)
            front(NS - 1, 1)
            back(0)
            back(1)
            p.join()
            for c in range(2):
                for b in range(2):
                    ts = slice(t0 + b * 512, t0 + (b + 1) * 512)
                    m = V.do(nc.vector.scalar_tensor_tensor, y[:, c, ts], xi[:, c, ts], w["Dp"][:, c:c + 1], Yb[2 * c + b][:, :], ALU.mult, ALU.add)
                G.do(nc.gpsimd.tensor_tensor, y[:, c, t0:t0 + CHK], y[:, c, t0:t0 + CHK], res[:, c, t0:t0 + CHK], ALU.mult, after=[m])
        gm = G.last()
        for b in range(NB):
            for q in range(4):
                t = 4 * b + q
                for c in range(2):
                    mm = T.do(nc.tensor.matmul, g.ps[b][:, q * 128:(q + 1) * 128], y[:, c, t * 128:(t + 1) * 128], w["out_proj"][:, c, :], start=(c == 0), stop=(c == 1), after=[gm, V.last()])
            xx = g.x_tok[:, 4 * b:4 * b + 4, :]
            V.do(nc.vector.tensor_tensor, xx, xx, g.ps[b][:, :].rearrange("p (t f) -> p t f", t=4), ALU.add, after=[mm])
        p.join()


EXPERTS, SHARED = 8, 2
UNITS = EXPERTS + SHARED

def first_of(g, V, mask, count, one, after):
    nc = g.nc
    m = V.do(nc.vector.tensor_copy, count, mask[:, :, 0], after=after)
    for e in range(1, one):
        m = V.do(nc.vector.tensor_tensor, mask[:, :, e], mask[:, :, e], count, ALU.is_gt, after=[m])
        m = V.do(nc.vector.tensor_tensor, count, count, mask[:, :, e], ALU.add, after=[m])
    return m

def moe(g, w, tag):
    nc, p, V, A, T, G = g.nc, g.p, g.V, g.A, g.T, g.G
    with ExitStack() as mem:
        sb = lambda n, s, d=F32: mem.enter_context(nc.sbuf_tensor(f"{n}{g.uid()}", s, d))
        sc, bs, m1, m2 = (sb(f"route{i}", [128, NT, EXPERTS]) for i in range(4))
        et = sb("route_tmp", [128, NT])
        GT = sb("gate_parts", [96, N], BF16)
        gf = sb("gate_full", [EXPERTS, 3, N])
        sel = sb("gate_select", [96, EXPERTS, 128], BF16)
        sa = sb("silu_a", [128, 3, 512])
        hs = sb("hidden", [128, 3, 512])
        gm = G.do(nc.gpsimd.memset, GT[:, :], 0.0)
        m = G.do(nc.gpsimd.memset, sel[:, :, :], 0.0)
        for k in range(3):
            m = G.do(nc.gpsimd.affine_select, out=sel[:, :, :], in_=sel[:, :, :], compare_op=ALU.not_equal, fill=1.0, base=-32 * k,
                     pattern=[[-1, EXPERTS], [0, 128]], channel_multiplier=1, after=[m])
        le = g.ps[0][:, 0:NT * EXPERTS].rearrange("p (t e) -> p t e", e=EXPERTS)
        for t in range(NT):
            mm = T.do(nc.tensor.matmul, g.ps[0][:, t * EXPERTS:(t + 1) * EXPERTS], g.xnT[:, t * 128:(t + 1) * 128], w["gate"], start=True, stop=True)
        up = lambda ap: ap.unsqueeze(2).broadcast_to([128, NT, EXPERTS])
        m = V.do(nc.vector.tensor_reduce, et[:, :], le, AX.X, ALU.max, after=[mm])
        m = V.do(nc.vector.tensor_tensor, sc[:, :, :], le, up(et[:, :]), ALU.subtract, after=[m])
        m = A.do(nc.scalar.activation, sc[:, :, :], sc[:, :, :], ACT.Exp, after=[m])
        m = V.do(nc.vector.tensor_reduce, et[:, :], sc[:, :, :], AX.X, ALU.add, after=[m])
        m = V.do(nc.vector.reciprocal, et[:, :], et[:, :], after=[m])
        m = V.do(nc.vector.tensor_tensor, sc[:, :, :], sc[:, :, :], up(et[:, :]), ALU.mult, after=[m])
        nc.scalar.preload_act_table(ACT.Silu)
        m = V.do(nc.vector.tensor_tensor, bs[:, :, :], sc[:, :, :], w["gate_bias"].unsqueeze(1).broadcast_to([128, NT, EXPERTS]), ALU.add, after=[m])
        for mk in (m1, m2):
            m = V.do(nc.vector.tensor_reduce, et[:, :], bs[:, :, :], AX.X, ALU.max, after=[m])
            m = V.do(nc.vector.tensor_tensor, mk[:, :, :], bs[:, :, :], up(et[:, :]), ALU.is_equal, after=[m])
            m = first_of(g, V, mk, et[:, :], EXPERTS, [m])
            if mk is m1:
                m = V.do(nc.vector.scalar_tensor_tensor, bs[:, :, :], m1[:, :, :], -1e30, bs[:, :, :], ALU.mult, ALU.add, after=[m])
        m = V.do(nc.vector.tensor_tensor, m1[:, :, :], m1[:, :, :], m2[:, :, :], ALU.add, after=[m])
        m = V.do(nc.vector.tensor_tensor, m1[:, :, :], m1[:, :, :], sc[:, :, :], ALU.mult, after=[m])
        for b in range(NB):
            for c in range(4):
                t = 4 * b + c
                tr = T.do(nc.tensor.transpose, g.ps[b][0:EXPERTS, c * 128:(c + 1) * 128], m1[:, t, :], g.ident[:, :], after=[m])
            cp = A.do(nc.scalar.copy, gf[:, 0, b * 512:(b + 1) * 512], g.ps[b][0:EXPERTS, :], after=[tr])
        m = V.do(nc.vector.tensor_copy, GT[0:8, :], gf[:, 0, :], after=[cp, gm])
        m = V.do(nc.vector.tensor_tensor, gf[:, 1, :], gf[:, 0, :], GT[0:8, :], ALU.subtract, after=[m])
        m = V.do(nc.vector.tensor_copy, GT[32:40, :], gf[:, 1, :], after=[m])
        m = A.do(nc.scalar.copy, gf[:, 2, :], GT[32:40, :], after=[m])
        m = V.do(nc.vector.tensor_tensor, GT[64:72, :], gf[:, 1, :], gf[:, 2, :], ALU.subtract, after=[m])
        p.join()
        st = dict(a=[None] * 2, b=[None] * 2, gb=None, h=[None] * 3, y=None, sa=[None] * 3)
        Ab, Bb, Gb, Yb = g.ps[0:2], g.ps[2:4], g.ps[4], g.ps[5]

        def block(b):
            ts = bass.ts(b, 512)
            hid = {}
            def front(u):
                k = u % 2
                ma = T.do(nc.tensor.matmul, Ab[k], w["w1"][:, u, :], g.xnT[:, ts], start=True, stop=True, after=[st["a"][k]])
                mb = T.do(nc.tensor.matmul, Bb[k], w["w3"][:, u, :], g.xnT[:, ts], start=True, stop=True, after=[st["b"][k]])
                if u < EXPERTS:
                    mg = T.do(nc.tensor.matmul, Gb, sel[:, u, :], GT[:, ts], start=True, stop=True, after=[st["gb"]])
                s = st["a"][k] = A.do(nc.scalar.activation, sa[:, u % 3, :], Ab[k], ACT.Silu, after=[ma, st["sa"][u % 3]])
                h = st["b"][k] = V.do(nc.vector.tensor_tensor, hs[:, u % 3, :], sa[:, u % 3, :], Bb[k], ALU.mult, after=[mb, s, st["h"][u % 3]])
                st["sa"][u % 3] = h
                if u < EXPERTS:
                    h = st["gb"] = V.do(nc.vector.tensor_tensor, hs[:, u % 3, :], hs[:, u % 3, :], Gb, ALU.mult, after=[mg, h])
                hid[u] = h
            def back(u):
                for c in range(4):
                    mm = T.do(nc.tensor.matmul, Yb[:, c * 128:(c + 1) * 128], hs[:, u % 3, c * 128:(c + 1) * 128], w["w2"][:, u, :],
                              start=(u == 0 and c == 0), stop=(u == UNITS - 1), after=[hid[u], st["y"]], skip_group_check=True)
                st["h"][u % 3] = mm
                return mm
            front(0)
            for u in range(1, UNITS):
                front(u)
                back(u - 1)
            mm = back(UNITS - 1)
            x = g.x_tok[:, :, :].rearrange("p t d -> p (t d)")[:, ts]
            st["y"] = V.do(nc.vector.tensor_tensor, x, x, Yb, ALU.add, after=[mm])
        p.pipeline(NB, block, st)
        p.join()
        nc.scalar.preload_act_table_set("natural_log_exp_and_others")


TAPS = 4
SEG = 32
STEPS = N // SEG
GRP = 8
EPS_R = 1e-6

def delta(g, w, tag):
    nc, p, V, A, T, G = g.nc, g.p, g.V, g.A, g.T, g.G
    with ExitStack() as mem:
        sb = lambda n, s, d=F32: mem.enter_context(nc.sbuf_tensor(f"{n}{g.uid()}", s, d))
        blk = lambda b: slice(b * 512, (b + 1) * 512)
        npT = sb("normed_p20", [128, N])
        swap = sb("swap", [128, 128])
        ones = sb("ones", [128, 128])
        bd = sb("head_ones", [128, HEADS, HD])
        selk = sb("key_select", [128, HD, HEADS, HD])
        z = G.do(nc.gpsimd.memset, swap[:, :], 0.0)
        v = swap[:, :].rearrange("p (m r) -> p m r", r=2)
        z = G.do(nc.gpsimd.affine_select, out=v[:, :, 0], in_=v[:, :, 0], compare_op=ALU.not_equal, fill=1.0, base=-1, pattern=[[-2, 64]], channel_multiplier=1, after=[z])
        z = G.do(nc.gpsimd.affine_select, out=v[:, :, 1], in_=v[:, :, 1], compare_op=ALU.not_equal, fill=-1.0, base=0, pattern=[[-2, 64]], channel_multiplier=1, after=[z])
        G.do(nc.gpsimd.memset, ones[:, :], 1.0)
        z = G.do(nc.gpsimd.memset, bd[:, :, :], 1.0)
        z = G.do(nc.gpsimd.affine_select, out=bd[:, :, :], in_=bd[:, :, :], compare_op=ALU.is_ge, fill=0.0, base=0, pattern=[[-HD, HEADS], [0, HD]], channel_multiplier=1, after=[z])
        z = G.do(nc.gpsimd.affine_select, out=bd[:, :, :], in_=bd[:, :, :], compare_op=ALU.is_ge, fill=0.0, base=HD - 1, pattern=[[HD, HEADS], [0, HD]], channel_multiplier=-1, after=[z])
        z = G.do(nc.gpsimd.memset, selk[:, :, :, :], 0.0)
        for k in range(HD):
            G.do(nc.gpsimd.affine_select, out=selk[:, k, :, :], in_=selk[:, k, :, :], compare_op=ALU.not_equal, fill=1.0, base=-k, pattern=[[-HD, HEADS], [0, HD]],
                 channel_multiplier=1, after=[z])
        made = G.last()

        with ExitStack() as early:
            sbe = lambda n, s, d=F32: early.enter_context(nc.sbuf_tensor(f"{n}{g.uid()}", s, d))
            CT, STb, x1, x2 = sbe("cos_table", [128, N]), sbe("sin_table", [128, N]), sbe("p20_a", [128, N]), sbe("p20_b", [128, N])
            col = sbe("p20_cols", [128, 24])
            ki = sbe("turns", [128, 1], mybir.dt.int32)
            cc = lambda k: col[:, k:k + 1]
            vs = lambda o, i, a, b, o1, o2=ALU.bypass, **kw: V.do(nc.vector.tensor_scalar, o, i, a, b, o1, o2, after=[V.last(), A.last()])
            vt = lambda o, a, b, op: V.do(nc.vector.tensor_tensor, o, a, b, op, after=[V.last(), A.last()])
            TWO_PI = 2 * math.pi
            hi = 6.28125
            vs(cc(0), w["theta"], 1 / TWO_PI, None, ALU.mult)
            V.do(nc.vector.tensor_copy, ki[:, :], cc(0), after=[V.last()])
            V.do(nc.vector.tensor_copy, cc(0), ki[:, :], after=[V.last()])
            V.do(nc.vector.scalar_tensor_tensor, cc(1), cc(0), -hi, w["theta"], ALU.mult, ALU.add, after=[V.last()])
            V.do(nc.vector.scalar_tensor_tensor, cc(1), cc(0), -(TWO_PI - hi), cc(1), ALU.mult, ALU.add, after=[V.last()])
            vs(cc(1), cc(1), 0.5, None, ALU.mult)
            vs(cc(2), cc(1), -1.0, None, ALU.mult)
            vt(cc(2), cc(1), cc(2), ALU.max)
            vs(cc(2), cc(2), -1.0, math.pi / 2, ALU.mult, ALU.add)
            nc.scalar.preload_act_table(ACT.Sin)
            A.do(nc.scalar.activation, cc(3), cc(1), ACT.Sin, after=[V.last()])
            A.do(nc.scalar.activation, cc(4), cc(2), ACT.Sin)
            nc.scalar.preload_act_table_set("natural_log_exp_and_others")
            vt(cc(6), cc(3), cc(4), ALU.mult)
            vs(cc(6), cc(6), 2.0, None, ALU.mult)
            vt(cc(5), cc(3), cc(3), ALU.mult)
            vs(cc(5), cc(5), -2.0, 1.0, ALU.mult, ALU.add)
            A.do(nc.scalar.activation, cc(8), w["decay_log"], ACT.Exp, after=[V.last()])
            A.do(nc.scalar.activation, cc(9), cc(8), ACT.Exp, scale=-1.0, after=[A.last()])
            vs(cc(10), cc(8), 0.25, None, ALU.min)
            vs(cc(11), cc(10), -1 / 7.0, 1.0, ALU.mult, ALU.add)
            for k in range(6, 0, -1):
                V.do(nc.vector.scalar_tensor_tensor, cc(11), cc(11), -1.0 / k, cc(10), ALU.mult, ALU.mult, after=[V.last()])
                vs(cc(11), cc(11), 1.0, None, ALU.add)
            vs(cc(12), cc(8), 0.25, None, ALU.is_lt)
            vt(cc(11), cc(11), cc(9), ALU.subtract)
            V.do(nc.vector.scalar_tensor_tensor, cc(7), cc(11), cc(12), cc(9), ALU.mult, ALU.add, after=[V.last()])
            V.do(nc.vector.memset, CT[:, 0:1], 1.0)
            V.do(nc.vector.memset, STb[:, 0:1], 0.0)
            n = 1
            while n < N:
                vs(cc(13), cc(6), -1.0, None, ALU.mult)
                V.do(nc.vector.tensor_scalar, x1[:, 0:n], STb[:, 0:n], cc(13), None, ALU.mult, after=[V.last()])
                V.do(nc.vector.tensor_scalar, x2[:, 0:n], CT[:, 0:n], cc(6), None, ALU.mult)
                V.do(nc.vector.scalar_tensor_tensor, CT[:, n:2 * n], CT[:, 0:n], cc(5), x1[:, 0:n], ALU.mult, ALU.add, after=[V.last()])
                V.do(nc.vector.scalar_tensor_tensor, STb[:, n:2 * n], STb[:, 0:n], cc(5), x2[:, 0:n], ALU.mult, ALU.add)
                vt(cc(14), cc(5), cc(6), ALU.mult)
                vt(cc(15), cc(6), cc(6), ALU.mult)
                vs(cc(6), cc(14), 2.0, None, ALU.mult)
                V.do(nc.vector.scalar_tensor_tensor, cc(5), cc(5), cc(5), cc(15), ALU.mult, ALU.subtract, after=[V.last()])
                n *= 2
            inv = x1
            m = A.do(nc.scalar.activation, x1[:, :], CT[:, :], ACT.Square, after=[V.last()])
            m = A.do(nc.scalar.activation, x2[:, :], STb[:, :], ACT.Square)
            V.do(nc.vector.scalar_tensor_tensor, x1[:, :], x1[:, :], -1.0, x2[:, :], ALU.mult, ALU.subtract, after=[m])
            iv = V.do(nc.vector.tensor_scalar, x1[:, :], x1[:, :], 2.0, None, ALU.add, after=[V.last()])
            for b in range(NB):
                mm = T.do(nc.tensor.matmul, g.ps[b], swap[:, :], g.xnT[:, blk(b)], start=True, stop=True, after=[made])
                V.do(nc.vector.tensor_tensor, x2[:, blk(b)], STb[:, blk(b)], g.ps[b], ALU.mult, after=[mm, iv])
            m = G.do(nc.gpsimd.tensor_tensor, npT[:, :], g.xnT[:, :], CT[:, :], ALU.mult, after=[iv])
            m = V.do(nc.vector.tensor_tensor, npT[:, :], npT[:, :], x2[:, :], ALU.add, after=[V.last(), m])
            m = V.do(nc.vector.tensor_tensor, x2[:, :], npT[:, :], x1[:, :], ALU.mult, after=[V.last()])
            m = V.do(nc.vector.tensor_tensor_scan, x1[:, :], cc(7).broadcast_to([128, N]), x2[:, :], 0.0, ALU.mult, ALU.add, after=[V.last()])
            y = G.do(nc.gpsimd.tensor_tensor, CT[:, :], CT[:, :], x1[:, :], ALU.mult, after=[m])
            for b in range(NB):
                mm = T.do(nc.tensor.matmul, g.ps[b], swap[:, :], x1[:, blk(b)], start=True, stop=True, after=[m])
                V.do(nc.vector.tensor_tensor, x2[:, blk(b)], STb[:, blk(b)], g.ps[b], ALU.mult, after=[mm])
            y = V.do(nc.vector.tensor_tensor, x1[:, :], CT[:, :], x2[:, :], ALU.subtract, after=[y, V.last(), T.last()])
            sq = A.do(nc.scalar.activation, x2[:, :], x1[:, :], ACT.Square, after=[y])
            for b in range(NB):
                mm = T.do(nc.tensor.matmul, g.ps[4 + b], ones[:, :], x2[:, blk(b)], start=True, stop=True, after=[sq])
                m = A.do(nc.scalar.activation, CT[:, blk(b)], g.ps[4 + b], ACT.Ln, bias=g.eps_rms[:, :], scale=1.0 / D, after=[mm])
                m = A.do(nc.scalar.activation, CT[:, blk(b)], CT[:, blk(b)], ACT.Exp, scale=-0.5, after=[m])
                V.do(nc.vector.scalar_tensor_tensor, npT[:, blk(b)], x1[:, blk(b)], w["vnorm"], CT[:, blk(b)], ALU.mult, ALU.mult, after=[m, V.last()])
            p.join()

        q, k, bv = sb("queries", [128, N]), sb("keys", [128, N]), sb("beta_values", [128, N])
        dec, nb = sb("decay", [128, N]), sb("neg_beta_decay", [128, N])
        gt = sb("gate", [128, NT, D])
        ramp = sb("ramp", [128, 1])
        with ExitStack() as early:
            sbe = lambda n, s, d=F32: early.enter_context(nc.sbuf_tensor(f"{n}{g.uid()}", s, d))
            pads = [sbe(f"conv_in{i}", [128, TAPS - 1 + N]) for i in range(3)]
            sq = sbe("squares", [128, 2, N])
            nc.scalar.preload_act_table(ACT.Silu)
            for i, dst in enumerate((q, k, bv)):
                z = G.do(nc.gpsimd.memset, pads[i][:, 0:TAPS - 1], 0.0)
                for b in range(NB):
                    kk = (4 * i + b) % 8
                    mm = T.do(nc.tensor.matmul, g.ps[kk], w["ctrl"][:, i * 128:(i + 1) * 128], g.xnT[:, blk(b)], start=True, stop=True, after=[A.last()])
                    a = A.do(nc.scalar.activation, pads[i][:, TAPS - 1 + b * 512:TAPS - 1 + (b + 1) * 512], g.ps[kk], ACT.Identity, bias=w["ctrl_b"][:, i:i + 1], after=[mm])
                m = V.do(nc.vector.tensor_scalar, dst[:, :], pads[i][:, 0:N], w["convs"][:, i, 0:1], None, ALU.mult, after=[a, z])
                for c in range(1, TAPS):
                    m = V.do(nc.vector.scalar_tensor_tensor, dst[:, :], pads[i][:, c:c + N], w["convs"][:, i, c:c + 1], dst[:, :], ALU.mult, ALU.add, after=[m])
                A.do(nc.scalar.activation, dst[:, :], dst[:, :], ACT.Silu, after=[m])
            silud = A.last()
            nc.scalar.preload_act_table(ACT.Sigmoid)
            rm = A.do(nc.scalar.activation, ramp[:, :], w["ramp_logit"], ACT.Sigmoid)
            for i, dst in ((0, dec), (1, nb)):
                for b in range(NB):
                    kk = 4 * i + b
                    mm = T.do(nc.tensor.matmul, g.ps[kk], w["dec_beta"][:, i * 128:(i + 1) * 128], g.xnT[:, blk(b)],
                              start=True, stop=True, after=[A.last()])
                    A.do(nc.scalar.activation, dst[:, blk(b)], g.ps[kk], ACT.Sigmoid, bias=w["ctrl_b"][:, 3 + i:4 + i], after=[mm])
            for b in range(NB):
                for c in range(4):
                    t = 4 * b + c
                    o = g.ps[b][:, c * 128:(c + 1) * 128]
                    T.do(nc.tensor.matmul, o, g.xnT[:, t * 128:(t + 1) * 128], w["ctrl"][:, 384:512], start=True, stop=False, after=[A.last()] if b + c == 0 else [])
                    mm = T.do(nc.tensor.matmul, o, g.ones_row[:, 0:128], w["gate_b"], start=False, stop=True)
                A.do(nc.scalar.activation, gt[:, 4 * b:4 * b + 4, :].rearrange("p t d -> p (t d)"), g.ps[b], ACT.Sigmoid, after=[mm])
            nc.scalar.preload_act_table_set("natural_log_exp_and_others")
            for i, dst in enumerate((q, k, bv)):
                for b in range(NB):
                    kk = 4 + b
                    mm = T.do(nc.tensor.matmul, g.ps[kk], w["p20c"][:, i * 128:(i + 1) * 128], npT[:, blk(b)], start=True, stop=True, after=[V.last(), A.last()])
                    V.do(nc.vector.scalar_tensor_tensor, dst[:, blk(b)], g.ps[kk], ramp[:, :], dst[:, blk(b)], ALU.mult, ALU.add, after=[mm, silud, rm])
            m = V.do(nc.vector.tensor_tensor, bv[:, :], bv[:, :], nb[:, :], ALU.mult, after=[V.last(), A.last()])
            m = V.do(nc.vector.scalar_tensor_tensor, nb[:, :], nb[:, :], -1.0, dec[:, :], ALU.mult, ALU.mult, after=[m])
            for i, dst in enumerate((q, k)):
                s = A.do(nc.scalar.activation, sq[:, i, :], dst[:, :], ACT.Square, after=[m])
                for b in range(NB):
                    mm = T.do(nc.tensor.matmul, g.ps[b], bd[:, :, :].rearrange("p h d -> p (h d)"), sq[:, i, blk(b)], start=True, stop=True, after=[s, A.last()])
                    a = A.do(nc.scalar.activation, pads[i][:, blk(b)], g.ps[b], ACT.Ln, bias=g.eps_rms[:, :], after=[mm])
                a = A.do(nc.scalar.activation, pads[i][:, 0:N], pads[i][:, 0:N], ACT.Exp, scale=-0.5, after=[a])
                V.do(nc.vector.tensor_tensor, dst[:, :], dst[:, :], pads[i][:, 0:N], ALU.mult, after=[a])
            p.join()

        KB = [sb(f"keys_spread{i}", [128, GRP, SEG, HD]) for i in range(2)]
        QB = [sb(f"queries_spread{i}", [128, GRP, SEG, HD]) for i in range(2)]
        S = [sb(f"state{i}", [128, 2, SEG, HD]) for i in range(2)]
        SD = sb("state_decayed", [128, 2, SEG, HD])
        M, X = sb("state_keys", [128, 2, SEG, HD]), sb("update", [128, 2, SEG, HD])
        MQ = [sb(f"state_queries{i}", [128, 2, SEG, HD]) for i in range(2)]
        pr = sb("predicted", [128, 2, SEG])
        ou = sb("outs", [128, 2, N])
        seg = lambda ap: ap.rearrange("p (g s) -> p g s", s=STEPS)
        z = G.do(nc.gpsimd.memset, S[1][:, :, :, :], 0.0)
        z = V.do(nc.vector.tensor_reduce, pr[:, 0, 0:HD], selk[:, :, :, 0], AX.X, ALU.add, after=[z])
        z = V.do(nc.vector.tensor_copy, S[1][:, 1, :, :], pr[:, 0, 0:HD].unsqueeze(1).broadcast_to([128, SEG, HD]), after=[z])
        st = dict(bank=[None] * 8, kb=[None, None], use=[None, None], S=None, MQ=[None, None], qread=[None, None])

        def spread(i, s0):
            n = 0
            for src, dst in ((k, KB[i]), (q, QB[i])):
                cols = seg(src[:, :])[:, :, bass.ds(s0, GRP)].rearrange("p g s -> p s g")
                for kk in range(HD):
                    b = n % 8
                    n += 1
                    o = g.ps[b][:, 0:GRP * SEG]
                    mm = T.do(nc.tensor.matmul, o, selk[:, kk, :, :].rearrange("p h v -> p (h v)"), cols, start=True, stop=True, after=[st["bank"][b]])
                    st["bank"][b] = A.do(nc.scalar.copy, dst[:, :, :, kk], o.rearrange("p (s g) -> p s g", s=GRP), after=[mm, st["use"][i]])
                    st["kb"][i] = st["bank"][b]
                    yield

        def step(i, j, s):
            two = lambda ap: ap.rearrange("p g k -> p (g k)").unsqueeze(1).broadcast_to([128, 2, SEG * HD])
            flat = lambda t: t[:, :, :, :].rearrange("p x g k -> p x (g k)")
            per = lambda t, x=None: seg(t[:, :])[:, :, bass.ds(s, 1)].rearrange("p g o -> p (g o)")
            a, b = j % 2, 1 - j % 2
            kb = two(KB[i][:, j, :, :])
            m = V.do(nc.vector.tensor_tensor, flat(M), flat(S[b]), kb, ALU.mult, after=[st["S"], st["kb"][i], st["X"]])
            d = G.do(nc.gpsimd.tensor_tensor, SD[:, :, :, :],
                     S[b][:, :, :, :], per(dec).unsqueeze(1).unsqueeze(3).broadcast_to([128, 2, SEG, HD]), ALU.mult, after=[st["S"]])
            m = V.do(nc.vector.tensor_reduce, pr[:, :, :], M[:, :, :, :], AX.X, ALU.add, after=[m])
            m = V.do(nc.vector.tensor_tensor, pr[:, :, :], pr[:, :, :], per(nb).unsqueeze(1).broadcast_to([128, 2, SEG]), ALU.mult, after=[m])
            m = V.do(nc.vector.tensor_tensor, pr[:, 0, :], pr[:, 0, :], per(bv), ALU.add, after=[m])
            m = st["X"] = V.do(nc.vector.tensor_tensor, X[:, :, :, :], pr[:, :, :].unsqueeze(3).broadcast_to([128, 2, SEG, HD]), KB[i][:, j, :, :].unsqueeze(1).broadcast_to([128, 2, SEG, HD]), ALU.mult, after=[m])
            emit_out()
            m = st["S"] = V.do(nc.vector.tensor_tensor, S[a][:, :, :, :], SD[:, :, :, :], X[:, :, :, :], ALU.add, after=[m, d, st["MQ"][a]])
            st["MQ"][a] = G.do(nc.gpsimd.tensor_tensor, flat(MQ[a]), flat(S[a]), two(QB[i][:, j, :, :]), ALU.mult, after=[m, st["qread"][a]])
            st["use"][i] = st["MQ"][a]
            pend.append((a, s, st["MQ"][a]))

        pend = []

        def emit_out():
            while pend:
                a, s, mk = pend.pop(0)
                o = ou[:, :, :].rearrange("p x (g s) -> p x g s", s=STEPS)[:, :, :, bass.ds(s, 1)].rearrange("p x g o -> p x (g o)")
                st["qread"][a] = V.do(nc.vector.tensor_reduce, o, MQ[a][:, :, :, :], AX.X, ALU.add, after=[mk])

        st["X"] = None
        for _ in spread(0, 0):
            pass

        def groups(s0, more):
            nxt = spread(1, s0 + GRP)
            for i in range(2):
                for j in range(GRP):
                    step(i, j, s0 + GRP * i + j)
                    for _ in range(2):
                        next(nxt, None)
                if i == 0 and more:
                    nxt = spread(0, s0 + 2 * GRP)
            emit_out()
        p.pipeline(STEPS // (2 * GRP) - 1, lambda i: groups(i * 2 * GRP, True), st)
        groups(STEPS - 2 * GRP, False)
        p.join()

        fin = S[1]
        BDT, BDS = KB, QB
        for half in range(2):
            for kind, dst in ((1, BDT), (0, BDS)):
                src = fin[:, kind, 16 * half:16 * half + 16, :].unsqueeze(2).broadcast_to([128, 16, HEADS, HD])
                out = dst[half][:, :, :, :].rearrange("p a b c -> p (a b c)").rearrange("p (g h k) -> p g h k", g=16, h=HEADS)
                eng, f = (V, nc.vector) if kind else (G, nc.gpsimd)
                for gq in range(16):
                    eng.do(f.tensor_tensor, out[:, gq, :, :], fin[:, kind, 16 * half + gq, :].unsqueeze(1).broadcast_to([128, HEADS, HD]), bd[:, :, :], ALU.mult)
        p.join()
        S0 = [sb(f"start_state{i}", [128, 128]) for i in range(2)]
        z = V.do(nc.vector.memset, S0[0][:, :], 0.0)
        cor = None
        for n in range(SEG):
            ident = g.ident[:, :]
            cur, nx = S0[n % 2], S0[(n + 1) % 2]
            part = lambda t: t[n // 16][:, :, :, :].rearrange("p a b c -> p (a b c)")[:, (n % 16) * 128:(n % 16) * 128 + 128]
            if n + 1 < SEG:
                bank = g.ps[n % 2][:, 0:128]
                T.do(nc.tensor.matmul, bank, part(BDS), ident, start=True, stop=False)
                mm = T.do(nc.tensor.matmul, bank, part(BDT), cur[:, :], start=False, stop=True, after=[z])
            ob = g.ps[4 + n // 8][:, (n % 8) * STEPS:(n % 8 + 1) * STEPS]
            cm = T.do(nc.tensor.matmul, ob, cur[:, :], ou[:, 1, n * STEPS:(n + 1) * STEPS], start=True, stop=True, after=[z])
            if n + 1 < SEG:
                z = V.do(nc.vector.tensor_copy, nx[:, :], bank, after=[mm, cor])
            cor = cm
        o_, t1, t2 = ou[:, 0, :], ou[:, 1, :], q
        for b in range(NB):
            m = V.do(nc.vector.tensor_tensor, o_[:, blk(b)], o_[:, blk(b)], g.ps[4 + b], ALU.add, after=[cm])
            s = A.do(nc.scalar.activation, t1[:, blk(b)], o_[:, blk(b)], ACT.Square, scale=float(HD) ** -0.5, after=[m])
            mm = T.do(nc.tensor.matmul, g.ps[b], bd[:, :, :].rearrange("p h d -> p (h d)"), t1[:, blk(b)], start=True, stop=True, after=[s])
            a = A.do(nc.scalar.activation, t2[:, blk(b)], g.ps[b], ACT.Ln, bias=g.eps_rms[:, :], scale=1.0 / HD, after=[mm])
            a = A.do(nc.scalar.activation, t2[:, blk(b)], t2[:, blk(b)], ACT.Exp, scale=-0.5, after=[a])
            m = V.do(nc.vector.scalar_tensor_tensor, o_[:, blk(b)], o_[:, blk(b)], w["mnorm"], t2[:, blk(b)], ALU.mult, ALU.mult, after=[a, m])
            m = V.do(nc.vector.tensor_scalar, o_[:, blk(b)], o_[:, blk(b)], float(HD) ** -0.5, None, ALU.mult, after=[m])
        for b in range(NB):
            for c in range(4):
                t = 4 * b + c
                o = g.ps[4 + b][:, c * 128:(c + 1) * 128]
                ts = slice(t * 128, (t + 1) * 128)
                T.do(nc.tensor.matmul, o, o_[:, ts], w["out"][:, 0, :], start=True, stop=False, after=[m])
                T.do(nc.tensor.matmul, o, npT[:, ts], w["out"][:, 1, :], start=False, stop=False)
                mm = T.do(nc.tensor.matmul, o, g.ones_row[:, 0:128], w["out_b"], start=False, stop=True)
            ge = gt[:, 4 * b:4 * b + 4, :]
            xx = g.x_tok[:, 4 * b:4 * b + 4, :]
            m = V.do(nc.vector.tensor_tensor, ge, ge, g.ps[4 + b].rearrange("p (t f) -> p t f", t=4), ALU.mult, after=[mm])
            V.do(nc.vector.tensor_tensor, xx, xx, ge, ALU.add, after=[m])
        p.join()


ATTN_COLS = (("wqT", 128), ("wkT", 128), ("wvT", 128), ("woT", 128), ("bq", 1), ("bk", 1))
GLA_COLS = (("Wp", 3 * KD), ("Wa", 224), ("Wb", KD), ("Wc", KD), ("Wo", KD), ("We", NEXP), ("norm", DK))
MAMBA_COLS = (("in_proj", 512), ("x_proj", 80), ("out_proj", 256), ("dt_w", 256), ("conv_w", 8), ("conv_b", 2),
              ("dt_b", 2), ("A_log", 32), ("Dp", 2))
MOE_COLS = (("w1", UNITS * 128), ("w3", UNITS * 128), ("w2", UNITS * 128), ("gate", EXPERTS), ("gate_bias", EXPERTS))
DELTA_COLS = (("ctrl", 512), ("dec_beta", 256), ("ctrl_b", 5), ("p20c", 384), ("convs", 12), ("out", 256),
              ("theta", 1), ("decay_log", 1), ("ramp_logit", 1), ("vnorm", 1), ("mnorm", 1))
BLOCKS = {"x_proj": 2, "out_proj": 2, "conv_w": 2, "A_log": 2, "w1": UNITS, "w3": UNITS, "w2": UNITS, "convs": 3, "out": 2}
ROW_PAIRS = 3


def width(cols):
    return sum(k for _, k in cols)


def views(sbuf, cols):
    out, at = {}, 0
    for name, k in cols:
        v = sbuf[:, at:at + k]
        out[name] = v.rearrange("p (i c) -> p i c", i=BLOCKS[name]) if name in BLOCKS else v
        at += k
    return out


class Context:
    pass


def build(nc):
    dram = lambda n, s: nc.dram_tensor(n, s, F32, kind="ExternalInput").ap()
    x = dram("x", (N, D))
    src = {n: dram(n, (128, width(c))) for n, c in
           (("attn_a", ATTN_COLS), ("attn_b", ATTN_COLS), ("gla", GLA_COLS), ("mamba", MAMBA_COLS), ("moe", MOE_COLS), ("delta", DELTA_COLS))}
    row_src = dram("row_biases", (ROW_PAIRS, 2 * D))
    out = nc.dram_tensor("out", (1, N, D), F32, kind="ExternalOutput").ap()

    g = Context()
    g.nc, g.p = nc, Program(nc)
    p = g.p
    g.V, g.A, g.T, g.G = p.stream(nc.vector, "vec"), p.stream(nc.scalar, "act"), p.stream(nc.tensor, "pe"), p.stream(nc.gpsimd, "pool")
    g.L, g.Lsc2 = p.stream(nc.sync, "load", 16), p.stream(nc.sync, "scratch_2", 16)
    names = []

    def uid():
        names.append(None)
        return f"_{len(names)}"

    g.uid = uid
    keep = lambda n, s, d=F32: nc.alloc_sbuf_tensor(n, s, d)
    g.x_tok, g.xnT = keep("x_tok", [128, NT, D]), keep("xnT", [128, N])
    g.ident, g.tri, g.cum = keep("ident", [128, 128]), keep("tri", [128, 128]), keep("cum", [128, 128])
    g.half_col, g.eps_ln, g.eps_rms = keep("half_col", [128, 2]), keep("eps_ln", [128, 1]), keep("eps_rms", [128, 1])
    g.ones_row, rows = keep("ones_row", [1, 128]), keep("row_biases_sb", [1, 2 * D])
    mixer_w = keep("mixer_weights", [128, max(width(c) for c in (ATTN_COLS, MAMBA_COLS, DELTA_COLS))])
    ffn_w = keep("ffn_weights", [128, max(width(GLA_COLS), width(MOE_COLS))])
    whole = nc.alloc_psum_tensor("banks", [128, 8 * 512], F32)
    g.ps = [whole[:, i * 512:(i + 1) * 512] for i in range(8)]
    g.wide = lambda i: whole[:, i * 512:(i + 2) * 512]
    g.q_scratch = nc.dram_tensor("q_scratch", (PARTS, 128, N), BF16, kind="Internal").ap()
    g.k_scratch = nc.dram_tensor("k_scratch", (PARTS, 128, N), BF16, kind="Internal").ap()

    def load(sbuf, name):
        a = src[name]
        return g.L.do(nc.sync.dma_start, sbuf[:, 0:a.shape[1]], a)

    def load_rows(k):
        return g.L.do(nc.sync.dma_start, rows[:, :], row_src[k:k + 1, :])

    for b in range(NB):
        xb = g.L.do(nc.sync.dma_start, g.x_tok[:, 4 * b:4 * b + 4, :], x[b * 512:(b + 1) * 512, :].rearrange("(t p) d -> p t d", p=128))
    load(mixer_w, "attn_a")
    load_rows(0)
    first = g.L.last()
    ffn_loads = p.stream(nc.sync, "load_gla", 16)
    ffn_loads.do(nc.sync.dma_start, ffn_w[:, 0:width(GLA_COLS)], src["gla"])

    G = g.G
    m = G.do(nc.gpsimd.memset, g.ident[:, :], 0.0)
    G.do(nc.gpsimd.affine_select, out=g.ident[:, :], in_=g.ident[:, :], compare_op=ALU.not_equal, fill=1.0, base=0,
         pattern=[[-1, 128]], channel_multiplier=1, after=[m])
    G.do(nc.gpsimd.memset, g.ones_row[:, :], 1.0)
    G.do(nc.gpsimd.memset, g.eps_ln[:, :], EPS_LN)
    G.do(nc.gpsimd.memset, g.eps_rms[:, :], EPS_R)
    m = G.do(nc.gpsimd.memset, g.tri[:, :], 1.0)
    m = G.do(nc.gpsimd.affine_select, out=g.tri[:, :], in_=g.tri[:, :], compare_op=ALU.is_ge, fill=0.0, base=0,
             pattern=[[1, 128]], channel_multiplier=-1, after=[m])
    m = G.do(nc.gpsimd.memset, g.half_col[:, :], 1.0)
    m = G.do(nc.gpsimd.affine_select, out=g.half_col[:, 0:1], in_=g.half_col[:, 0:1], compare_op=ALU.is_ge, fill=0.0,
             base=63, pattern=[[0, 1]], channel_multiplier=-1, after=[m])
    m = G.do(nc.gpsimd.affine_select, out=g.half_col[:, 1:2], in_=g.half_col[:, 1:2], compare_op=ALU.is_ge, fill=0.0,
             base=-64, pattern=[[0, 1]], channel_multiplier=1, after=[m])
    g.V.do(nc.vector.tensor_scalar, g.cum[:, :], g.tri[:, :], g.half_col[:, 0:1], None, ALU.subtract, after=[m])
    nc.scalar.preload_act_table_set("natural_log_exp_and_others")

    row_1, row_2 = rows[:, 0:D], rows[:, D:2 * D]
    for e in (nc.tensor, nc.vector, nc.scalar, nc.gpsimd):
        p.wait(e, [first, G.last(), g.V.last()])
    layer_norm_T(g)
    attention(g, dict(views(mixer_w, ATTN_COLS), bv=row_1, bo=row_2), "a")
    load(mixer_w, "attn_b")
    load_rows(1)
    layer_norm_T(g)
    gla_ffn(g, views(ffn_w, GLA_COLS), "f1")
    layer_norm_T(g)
    attention(g, dict(views(mixer_w, ATTN_COLS), bv=row_1, bo=row_2), "b")
    load(mixer_w, "mamba")
    load_rows(2)
    layer_norm_T(g)
    gla_ffn(g, views(ffn_w, GLA_COLS), "f2")
    load(ffn_w, "moe")
    layer_norm_T(g)
    mamba(g, views(mixer_w, MAMBA_COLS), "m")
    load(mixer_w, "delta")
    layer_norm_T(g)
    moe(g, views(ffn_w, MOE_COLS), "e1")
    layer_norm_T(g)
    delta(g, dict(views(mixer_w, DELTA_COLS), gate_b=row_1, out_b=row_2), "d")
    layer_norm_T(g)
    moe(g, views(ffn_w, MOE_COLS), "e2")
    stored = g.L.do(nc.sync.dma_start, out[0].rearrange("(t p) d -> p t d", p=128), g.x_tok[:, :, :])
    p.wait(nc.sync, [stored])


def kernel(**a):
    import concourse.bacc as _bacc
    import numpy as np
    from concourse.bass_utils import run_bass_kernel_spmd as _run

    a = {k: np.asarray(v) for k, v in a.items()}
    w, b = a["L0_attn_a_qkv_w"], a["L0_attn_a_qkv_b"]
    attn_a = np.concatenate([w[0:128].T, w[128:256].T, w[256:384].T, a["L0_attn_a_out_w"].T, b[0:128, None], b[128:256, None]], 1)
    rows = [b[256:384], a["L0_attn_a_out_b"]]
    f = lambda n: a["L0_attn_b_" + n]
    kv_heads = f("wk").shape[0] // HD
    grp = HEADS // kv_heads
    again = lambda v: np.repeat(v.reshape((kv_heads, HD) + v.shape[1:]), grp, 0).reshape((HEADS * HD,) + v.shape[1:])
    attn_b = np.concatenate([f("wq").T, again(f("wk")).T, again(f("wv")).T, f("wo").T, f("bq")[:, None],
                             again(f("bk"))[:, None]], 1)
    rows += [again(f("bv")), f("bo")]
    f = lambda n: a["L0_ffn_" + n]
    blocks = lambda v: v.reshape(v.shape[0] // 128, 128, -1).transpose(1, 0, 2).reshape(128, -1)
    wc = np.zeros((128, f("Wgb").shape[1]), np.float32)
    wc[0:64], wc[64:80], wc[80], wc[96:112], wc[112] = f("Wgb"), f("Wg1b"), f("bg1"), f("Wg2b"), f("bg2")
    gla = np.concatenate([f("Wq"), f("Wk"), f("Wv"), f("Wqa"), f("Wka"), f("Wga"), f("Wg1a"), f("Wg2a"),
                          np.concatenate([f("Wqb"), f("Wkb")], 0), wc, blocks(f("Wo")), f("We"), np.tile(f("norm_w")[None], (128, 1))], 1)
    f = lambda n: a["L1_attn_a_" + n]
    dt_w = np.zeros((128, f("dt_proj_w").shape[1]), np.float32)
    dt_w[0:f("dt_proj_w").shape[0]] = f("dt_proj_w")
    mamba_w = np.concatenate([f("in_proj_w"), blocks(f("x_proj_w")), blocks(f("out_proj_w")), dt_w, blocks(f("conv_w")[:, 0, :]),
                              blocks(f("conv_b")[:, None]), blocks(f("dt_proj_b")[:, None]), blocks(f("A_log")), blocks(f("Dparam")[:, None])], 1)
    f = lambda n: a["L1_ffn_" + n]
    up = lambda r, s: np.concatenate([f(r), f(s).reshape(-1, 128, 128)], 0).transpose(2, 0, 1).reshape(128, -1)
    down = np.concatenate([f("w2").transpose(0, 2, 1), f("sw2").T.reshape(-1, 128, 128)], 0).transpose(1, 0, 2).reshape(128, -1)
    moe_w = np.concatenate([up("w1", "sw1"), up("w3", "sw3"), down, f("gate_w").T, np.tile(f("gate_bias")[None], (128, 1))], 1)
    f = lambda n: a["L1_attn_b_" + n]
    w, b = f("ctrl_W"), f("ctrl_b")
    cols = [b[0:128], b[128:256], b[256:384], np.repeat(b[384:400], HD), np.repeat(b[400:416], HD)]
    delta_w = np.concatenate([w[:, 0:384], w[:, 416:544], np.repeat(w[:, 384:416], HD, 1), np.stack(cols, 1), f("p20c_W"),
                              f("qconv_w"), f("kconv_w"), f("vconv_w"), blocks(f("out_W")), np.repeat(f("p20_theta"), 2)[:, None],
                              np.repeat(f("p20_decay_log"), 2)[:, None], f("ramp_logit")[:, None], f("vnorm_scale")[:, None],
                              np.tile(f("mnorm_scale"), HEADS)[:, None]], 1)
    rows += [b[416:544], f("out_b")]
    inputs = dict(x=a["L0_attn_a_x"][0], attn_a=attn_a, attn_b=attn_b, gla=gla, mamba=mamba_w, moe=moe_w, delta=delta_w,
                  row_biases=np.concatenate(rows).reshape(-1, 256))
    inputs = {k: np.ascontiguousarray(v) for k, v in inputs.items()}
    nc = _bacc.Bacc("TRN2", target_bir_lowering=False, num_devices=1)
    build(nc)
    nc.compile()
    return _run(nc, [inputs], core_ids=[0]).results[0]["out"]
```

```python
import math
from contextlib import ExitStack

import concourse.bass as bass
from concourse import mybir

F32 = mybir.dt.float32
BF16 = mybir.dt.bfloat16
ALU = mybir.AluOpType
ACT = mybir.ActivationFunctionType
AX = mybir.AxisListType

N = 2048
D = 128
NT = N // 128
NB = N // 512
EPS_LN = 1e-5
BIAS = 1024


class Mark:

    def __init__(self, stream, loop, value):
        self.stream, self.loop, self.value = stream, loop, value

    def before(self):
        return Mark(self.stream, self.loop, self.value - self.loop.per[self.stream])


class Loop:
    def __init__(self, times):
        self.times, self.per, self.base, self.index = times, {}, {}, 0


class Stream:

    def __init__(self, prog, engine, sem, step=1):
        self.prog, self.engine, self.sem, self.step, self.count = prog, engine, sem, step, 0
        prog.streams.append(self)

    def do(self, make, *args, after=(), **kw):
        self.prog.wait(self.engine, after)
        if not self.prog.counting:
            make(*args, **kw).then_inc(self.sem, self.step)
        self.count += self.step
        return Mark(self, self.prog.loop, self.count)

    def last(self):
        return Mark(self, self.prog.loop, self.count)


class Program:

    def __init__(self, nc):
        self.nc, self.streams, self.loop, self.counting = nc, [], None, False
        self.waited = {}
        self.held_waits = [nc.alloc_semaphore(f"held_waits_{e}") for e in ("pool", "sync")]

    def stream(self, engine, name, step=1):
        s = Stream(self, engine, self.nc.alloc_semaphore(name), step)
        engine.sem_inc(s.sem, BIAS)
        s.count = BIAS
        return s

    def value(self, mark):
        loop = mark.loop
        if loop is None:
            return mark.value
        per, base = loop.per.get(mark.stream, 0), loop.base.get(mark.stream, 0)
        if loop is self.loop:
            return base + mark.value + loop.index * per
        return base + (loop.times - 1) * per + mark.value

    def wait(self, engine, marks):
        if self.counting:
            return
        for mark in marks:
            if mark is None:
                continue
            key = (id(engine), id(mark.stream), id(mark.loop if mark.loop is self.loop else None))
            least = mark.value if mark.loop is self.loop else self.value(mark)
            if self.waited.get(key, -10**9) >= least:
                continue
            self.waited[key] = least
            engine.wait_ge(mark.stream.sem, self.value(mark))
            if self.loop is not None and engine in (self.nc.sync, self.nc.gpsimd):
                engine.sem_inc(self.held_waits[engine is self.nc.sync], 1)

    def repeat(self, times, body):
        loop = Loop(times)
        at = {s: s.count for s in self.streams}
        for s in self.streams:
            s.count = 0
        outer_loop = self.loop
        assert outer_loop is None
        self.loop, self.counting = loop, True
        for s in self.streams:
            loop.per[s] = 0
        body(0)
        loop.per = {s: s.count for s in self.streams}
        for s in self.streams:
            s.count = 0
        loop.base = at
        self.counting = False
        self.waited = {}
        with self.nc.Fori(0, times) as index:
            loop.index = index
            body(index)
        self.waited = {}
        self.loop = None
        for s in self.streams:
            s.count = at[s] + times * loop.per[s]

    def pipeline(self, times, body, state, leave=()):
        def age(x):
            if isinstance(x, (list, tuple)):
                return [age(y) for y in x]
            return x.before() if x is not None else None

        def blank(x):
            return [blank(y) for y in x] if isinstance(x, (list, tuple)) else None

        ends = {}

        def traced(i):
            if self.counting:
                state.update({k: blank(x) for k, x in state.items()})
            else:
                state.update({k: age(x) for k, x in ends.items()})
            body(i)
            if self.counting:
                ends.update(state)

        self.join(leave)
        self.repeat(times, traced)

    def join(self, leave=()):
        left = [s.engine for s in leave]
        for engine in (self.nc.tensor, self.nc.vector, self.nc.scalar, self.nc.gpsimd, self.nc.sync):
            if engine not in left:
                self.wait(engine, [s.last() for s in self.streams if s not in leave])


HEADS, HD = 16, 8
PARTS = 3
ROWS = PARTS * PARTS * HD
SEAM = 8
LEAD = 12

def layer_norm_T(g):
    nc, V, A, T = g.nc, g.V, g.A, g.T
    with ExitStack() as mem:
        sb = lambda n, s, d=F32: mem.enter_context(nc.sbuf_tensor(f"{n}{g.uid()}", s, d))
        xn = sb("ln_normed", [128, NT, D])
        stats, mv, rstd = sb("ln_stats", [128, NT, 6]), sb("ln_mean_var", [128, NT, 2]), sb("ln_rstd", [128, NT])
        scaled = {}

        def statistics(b):
            for t in range(4 * b, 4 * b + 4):
                V.do(nc.vector.bn_stats, stats[:, t, :], g.x_tok[:, t, :])
            m = V.last()
            for t in range(4 * b, 4 * b + 4):
                v = V.do(nc.vector.bn_aggr, mv[:, t, :], stats[:, t, :], after=[m])
            r = rstd[:, 4 * b:4 * b + 4]
            m = A.do(nc.scalar.activation, r, mv[:, 4 * b:4 * b + 4, 1], ACT.Ln, bias=g.eps_ln[:, :], after=[v])
            scaled[b] = A.do(nc.scalar.activation, r, r, ACT.Exp, scale=-0.5, after=[m])

        def apply(b):
            for c in range(4):
                t = 4 * b + c
                m = V.do(nc.vector.tensor_scalar, xn[:, t, :], g.x_tok[:, t, :], mv[:, t, 0:1], rstd[:, t:t + 1], ALU.subtract, ALU.mult, after=[scaled[b]])
                tr = T.do(nc.tensor.transpose, g.ps[b][:, c * 128:(c + 1) * 128], xn[:, t, :], g.ident[:, :], after=[m])
            A.do(nc.scalar.copy, g.xnT[:, b * 512:(b + 1) * 512], g.ps[b][:, :], after=[tr])

        statistics(0)
        for b in range(1, NB):
            statistics(b)
            apply(b - 1)
        apply(NB - 1)
        g.p.join()

def attention(g, w, tag):
    nc, p, V, A, T, G = g.nc, g.p, g.V, g.A, g.T, g.G
    with ExitStack() as mem:
        sb = lambda n, s, d=F32: mem.enter_context(nc.sbuf_tensor(f"{n}{g.uid()}", s, d))
        Q1 = [sb(f"q_max{i}", [ROWS, N], BF16) for i in range(2)]
        K1 = [sb(f"k_max{i}", [ROWS, N], BF16) for i in range(2)]
        Q2 = [sb(f"q_exp{i}", [ROWS + PARTS, N], BF16) for i in range(2)]
        K2 = [sb(f"k_exp{i}", [ROWS + PARTS, N], BF16) for i in range(2)]
        Vs = [sb(f"v_head{i}", [128, NT, 32]) for i in range(2)]
        v_tok = sb("v_tok", [128, NT, HEADS, HD])
        o_tok = sb("o_tok", [128, NT, HEADS, HD])
        PT = sb("probs", [128, 8, 512])
        mxp = [sb(f"max_parts{i}", [128, 64]) for i in range(2)]
        nmx = sb("neg_max", [128, NT])
        nhi = sb("neg_max_hi", [NT, PARTS, 128], BF16)
        nres = sb("neg_max_rest", [NT, 2, 128])
        osb = sb("pv_copy", [128, 512])
        rec = sb("recip_sums", [128, 4, 4])
        Ld1 = [p.stream(nc.sync, f"{tag}_load_max{i}", 16) for i in range(2)]
        Ld2 = [p.stream(nc.sync, f"{tag}_load_exp{i}", 16) for i in range(2)]
        Lmx = [p.stream(nc.sync, f"{tag}_load_negmax{i}", 16) for i in range(2)]
        Lsc = p.stream(nc.sync, f"{tag}_scratch", 16)
        S1b, S2b, PVb, misc = g.ps[0:3], g.ps[3:6], g.ps[6], g.ps[7]
        qs, ks = g.q_scratch, g.k_scratch

        part = sb("qk_parts", [128, 2, PARTS, 512], BF16)
        full = sb("qk_full", [128, 2, 512])
        rest = sb("qk_rest", [128, 2, 512])
        sent = [None, None]
        unit = 0
        evac = {}
        for wT, bias, dst in ((w["wqT"], w["bq"], qs), (w["wkT"], w["bk"], ks)):
            for b in range(NB):
                k = unit % 2
                mm = T.do(nc.tensor.matmul, g.ps[k][:, :], wT, g.xnT[:, b * 512:(b + 1) * 512], start=True, stop=True,
                          after=[evac.get(k)])
                f = evac[k] = V.do(nc.vector.tensor_scalar, full[:, k, :], g.ps[k][:, :], bias, None, ALU.add, after=[mm, V.last()])
                h = A.do(nc.scalar.copy, part[:, k, 0, :], full[:, k, :], after=[f, sent[k]])
                r = V.do(nc.vector.tensor_tensor, rest[:, k, :], full[:, k, :], part[:, k, 0, :], ALU.subtract, after=[h])
                h2 = A.do(nc.scalar.copy, part[:, k, 1, :], rest[:, k, :], after=[r])
                lo = V.do(nc.vector.tensor_tensor, part[:, k, 2, :], rest[:, k, :], part[:, k, 1, :], ALU.subtract, after=[h2, sent[k]])
                s = Lsc if k == 0 else g.Lsc2
                sent[k] = s.do(nc.sync.dma_start, dst[:, :, b * 512:(b + 1) * 512].rearrange("a p n -> p a n"), part[:, k, :, :], after=[lo])
                unit += 1
        for t in range(NT):
            bank = g.ps[2 + t // 4]
            o = bank[:, (t % 4) * 128:(t % 4) * 128 + 128]
            T.do(nc.tensor.matmul, o, g.xnT[:, t * 128:(t + 1) * 128], w["wvT"], start=True, stop=False)
            mm = T.do(nc.tensor.matmul, o, g.ones_row[:, 0:128], w["bv"], start=False, stop=True)
            if t % 4 == 3:
                A.do(nc.scalar.copy, v_tok[:, t - 3:t + 1, :, :], bank[:, :].rearrange("p (t h d) -> p t h d", t=4, h=HEADS), after=[mm])
        v_ready = A.last()
        ini = []
        for i in range(2):
            ini.append(G.do(nc.gpsimd.memset, Vs[i][:, :, :], 0.0))
            ini.append(G.do(nc.gpsimd.memset, Q2[i][:, :], 1.0))
            ini.append(G.do(nc.gpsimd.memset, K2[i][:, :], 1.0))
        for i in range(2):
            G.do(nc.gpsimd.memset, Vs[i][:, :, HD:HD + 1], 1.0, after=[ini[-1]])
        inited = G.last()

        def load(stream, Q, K, h, after):
            for a in range(PARTS):
                r = slice(a * PARTS * HD, (a + 1) * PARTS * HD)
                stream.do(nc.sync.dma_start, Q[r, :], qs[a:a + 1, bass.ts(h, HD), :].broadcast_to([PARTS, HD, N]), after=after)
                d = stream.do(nc.sync.dma_start, K[r, :], ks[:, bass.ts(h, HD), :], after=after)
            return d

        def stage_v(i, h, after):
            return G.do(nc.gpsimd.tensor_copy, Vs[i][:, :, 0:HD], v_tok[:, :, h, :] if isinstance(h, int) else
                        v_tok[:, :, :, :].rearrange("p t h d -> p t (h d)")[:, :, bass.ts(h, HD)], after=after)

        scratch_done = [Lsc.last(), g.Lsc2.last()]
        st = dict(red=[None] * 3, exp=[None] * 3, maxed=None, pv=[None] * 8, evac=None, s1end=[None, None], mxred=[None, None],
                  load1=[None, None], load2=[None, None], vs=[None, None], negmax=[None, None], misc=None,
                  s2end=[None, None], pvend=[None, None], nhi=None, recm=None, tr4=None, probs=[None] * 8)
        slow = []

        def scores_max(par, u, slot):
            t, b = u // 4, u % 4
            mm = T.do(nc.tensor.matmul, S1b[slot][:, :], Q1[par][:, t * 128:(t + 1) * 128], K1[par][:, b * 512:(b + 1) * 512],
                      start=True, stop=True, after=[st["red"][slot], st["load1"][par]])
            st["red"][slot] = V.do(nc.vector.tensor_reduce, mxp[par][:, u:u + 1], S1b[slot][:, :], AX.X, ALU.max,
                                    after=[mm] + ([st["mxred"][par]] if u == 0 else []))
            st["maxed"] = st["red"][slot]
            if u == 63:
                st["s1end"][par] = mm

        def maxima(par):
            m = V.do(nc.vector.tensor_reduce, nmx[:, :], mxp[par][:, :].rearrange("p (t b) -> p t b", b=4), AX.X, ALU.max,
                     negate=True, after=[st["maxed"], st["misc"]])
            st["mxred"][par] = m
            yield
            tr = T.do(nc.tensor.transpose, misc[0:NT, 0:128], nmx[:, :], g.ident[:, :], after=[m, st["recm"]])
            yield
            m = V.do(nc.vector.tensor_copy, nhi[:, 0, :], misc[0:NT, 0:128], after=[tr, st["nhi"]])
            m = V.do(nc.vector.tensor_tensor, nres[:, 0, :], misc[0:NT, 0:128], nhi[:, 0, :], ALU.subtract, after=[m])
            st["misc"] = m
            m = V.do(nc.vector.tensor_copy, nhi[:, 1, :], nres[:, 0, :], after=[m])
            m = V.do(nc.vector.tensor_tensor, nhi[:, 2, :], nres[:, 0, :], nhi[:, 1, :], ALU.subtract, after=[m])
            for r in range(PARTS):
                d = Lmx[par].do(nc.sync.dma_start, Q2[par][ROWS + r:ROWS + r + 1, :], nhi[:, r, :], after=[m, st["s2end"][par], inited])
            st["negmax"][par] = st["nhi"] = d
            yield

        def scores_exp(par, u, slot):
            t, j = u // 4, u % 4
            mm = T.do(nc.tensor.matmul, S2b[slot][:, :], K2[par][:, t * 128:(t + 1) * 128], Q2[par][:, j * 512:(j + 1) * 512],
                      start=True, stop=True, after=[st["exp"][slot], st["load2"][par], st["negmax"][par], inited])
            st["probs"][u % 8] = st["exp"][slot] = A.do(nc.scalar.activation, PT[:, u % 8, :], S2b[slot][:, :], ACT.Exp, scale=float(HD) ** -0.5,
                                    after=[mm, st["pv"][u % 8]])
            if u == 63:
                st["s2end"][par] = mm

        def values(par, u):
            t, j = u // 4, u % 4
            st["pv"][u % 8] = T.do(nc.tensor.matmul, PVb[32 * j:32 * j + 32, :], Vs[par][:, t, :], PT[:, u % 8, :],
                                   start=(t == 0), stop=(t == NT - 1), after=[st["probs"][u % 8], st["evac"], st["vs"][par]])
            if u == 63:
                st["pvend"][par] = st["pv"][u % 8]

        def normalise(par, h):
            e = st["evac"] = A.do(nc.scalar.copy, osb[:, :], PVb[:, :], after=[st["pvend"][par], st["tr4"]])
            yield
            for c in range(4):
                tr = T.do(nc.tensor.transpose, misc[:, c * 128:(c + 1) * 128], osb[:, c * 128:(c + 1) * 128], g.ident[:, :],
                          after=[e, st["misc"], st["recm"]])
            st["tr4"] = tr
            yield
            turned = misc[:, :].rearrange("p (c j r) -> p c j r", c=4, j=4)
            m = V.do(nc.vector.reciprocal, rec[:, :, :], turned[:, :, :, HD], after=[tr, st["recm"]])
            out = o_tok[:, :, :, :].rearrange("p t h d -> p t (h d)")[:, :, bass.ts(h, HD)].rearrange("p (j c) d -> p c j d", c=4)
            st["recm"] = V.do(nc.vector.tensor_tensor, out, turned[:, :, :, 0:HD],
                              rec[:, :, :].unsqueeze(3).broadcast_to([128, 4, 4, HD]), ALU.mult, after=[m])
            yield

        def unit(h0, v, more=True, first=False):
            if v == SEAM and more:
                st["load1"][0] = load(Ld1[0], Q1[0], K1[0], h0 + 2, [st["s1end"][0]])
            ahead = v + 64 + LEAD
            if more or ahead < 128:
                scores_max((ahead // 64) % 2, ahead % 64, v % 3)
                if ahead % 64 == 63:
                    slow.append(maxima((ahead // 64) % 2))
                    if more and ahead // 64 == 1:
                        st["load1"][1] = load(Ld1[1], Q1[1], K1[1], h0 + 3, [st["s1end"][1]])
            scores_exp(v // 64, v % 64, v % 3)
            if v % 4 == 3 and not (first and v < 7):
                for y in range(v - 7, v - 3):
                    values((y // 64) % 2, y % 64)
            for chain in list(slow):
                next(chain, None)
            if v % 64 == 3 and not first:
                par = 1 - v // 64
                slow.append(normalise(par, h0 + v // 64 - 1))
                next(slow[-1])
                if more or par == 1:
                    st["load2"][par] = load(Ld2[par], Q2[par], K2[par], h0 + 2 - par, [st["s2end"][par]])
                    st["vs"][par] = stage_v(par, h0 + 2 - par, [st["pvend"][par]])

        def pair(h0):
            slow.clear()
            for v in range(SEAM, 128):
                unit(h0, v)
            for v in range(SEAM):
                unit(h0 + 2, v)

        for i in range(2):
            st["load1"][i] = load(Ld1[i], Q1[i], K1[i], i, scratch_done)
            st["load2"][i] = load(Ld2[i], Q2[i], K2[i], i, scratch_done + [inited])
            st["vs"][i] = stage_v(i, i, [v_ready, inited])
        p.wait(nc.tensor, [V.last(), v_ready])
        for u in range(64):
            scores_max(0, u, u % 3)
        for _ in maxima(0):
            pass
        for u in range(LEAD):
            scores_max(1, u, u % 3)
        for v in range(SEAM):
            unit(0, v, first=True)
        p.pipeline(HEADS // 2 - 1, lambda i: pair(2 * i), st)
        slow.clear()
        for v in range(SEAM, 128):
            unit(HEADS - 2, v, more=False)
        for u in range(60, 64):
            values(1, u)
        for _ in normalise(1, HEADS - 1):
            pass
        p.join()

        oT = sb("o_T", [128, N])
        for b in range(NB):
            for c in range(4):
                t = 4 * b + c
                tr = T.do(nc.tensor.transpose, g.ps[b][:, c * 128:(c + 1) * 128], o_tok[:, t, :, :].rearrange("p h d -> p (h d)"), g.ident[:, :])
            A.do(nc.scalar.copy, oT[:, b * 512:(b + 1) * 512], g.ps[b][:, :], after=[tr])
        for b in range(NB):
            bank = g.ps[4 + b]
            for c in range(4):
                t = 4 * b + c
                o = bank[:, c * 128:(c + 1) * 128]
                T.do(nc.tensor.matmul, o, oT[:, t * 128:(t + 1) * 128], w["woT"], start=True, stop=False, after=[A.last()])
                mm = T.do(nc.tensor.matmul, o, g.ones_row[:, 0:128], w["bo"], start=False, stop=True)
            x = g.x_tok[:, 4 * b:4 * b + 4, :]
            V.do(nc.vector.tensor_tensor, x, x, bank[:, :].rearrange("p (t f) -> p t f", t=4), ALU.add, after=[mm])
        p.join()


FH, DK = 8, 64
NEXP = 4
KD = FH * DK
ST = 1 + NEXP

ORDER = "bbbbbabcabcbcacaaacaabcbba" + "abc" * 4

def gla_ffn(g, w, tag):
    nc, p, V, A, T, G = g.nc, g.p, g.V, g.A, g.T, g.G
    with ExitStack() as mem:
        sb = lambda n, s, d=F32: mem.enter_context(nc.sbuf_tensor(f"{n}{g.uid()}", s, d))
        a1T = sb("low_rank_qk", [128, N])
        a2T = sb("low_rank_gates", [128, N])
        gate = sb("out_gate", [128, NT, KD])
        mask = sb("expert_mask", [128, NT, NEXP])
        prob = sb("expert_prob", [128, NT, NEXP])
        rw = sb("expert_weight", [128, NT])
        rws = sb("expert_weight_scaled", [128, NT])
        et = sb("expert_tmp", [128, NT])
        half = sb("half_mask", [128, NT, 2, NEXP])
        tri_s = sb("same_expert_tri", [128, NT, 128])
        cum_s = sb("same_expert_cum", [128, NT, 128])
        early = ExitStack()
        maskT = early.enter_context(nc.sbuf_tensor(f"expert_maskT{g.uid()}", [NEXP, N], F32))
        m = G.do(nc.gpsimd.memset, a2T[64:128, :], 1.0)
        for b in range(NB):
            c = slice(b * 512, (b + 1) * 512)
            m1 = T.do(nc.tensor.matmul, g.ps[b][:, :], w["Wa"][:, 0:128], g.xnT[:, c], start=True, stop=True)
            lowq = A.do(nc.scalar.copy, a1T[:, c], g.ps[b][:, :], after=[m1])
            o = g.ps[4 + b]
            T.do(nc.tensor.matmul, o[0:64, :], w["Wa"][:, 128:192], g.xnT[:, c], start=True, stop=True)
            T.do(nc.tensor.matmul, o[64:80, :], w["Wa"][:, 192:208], g.xnT[:, c], start=True, stop=True)
            m2 = T.do(nc.tensor.matmul, o[96:112, :], w["Wa"][:, 208:224], g.xnT[:, c], start=True, stop=True)
            V.do(nc.vector.tensor_copy, a2T[0:64, c], o[0:64, :], after=[m2])
            V.do(nc.vector.tensor_copy, a2T[64:80, c], o[64:80, :], after=[m])
            low = V.do(nc.vector.tensor_copy, a2T[96:112, c], o[96:112, :])
        le = g.ps[0][:, 0:NT * NEXP].rearrange("p (t e) -> p t e", e=NEXP)
        for t in range(NT):
            mm = T.do(nc.tensor.matmul, g.ps[0][:, t * NEXP:(t + 1) * NEXP], g.xnT[:, t * 128:(t + 1) * 128], w["We"], start=True, stop=True, after=[lowq])
        up = lambda ap, k: ap.unsqueeze(2).broadcast_to([128, NT, k])
        m = V.do(nc.vector.tensor_reduce, et[:, :], le, AX.X, ALU.max, after=[mm])
        m = V.do(nc.vector.tensor_tensor, prob[:, :, :], le, up(et[:, :], NEXP), ALU.subtract, after=[m])
        exped = A.do(nc.scalar.activation, prob[:, :, :], prob[:, :, :], ACT.Exp, after=[m])
        nc.scalar.preload_act_table(ACT.Silu)

        def routing():
            m = V.do(nc.vector.tensor_reduce, et[:, :], prob[:, :, :], AX.X, ALU.add, after=[exped])
            m = V.do(nc.vector.reciprocal, et[:, :], et[:, :], after=[m])
            m = V.do(nc.vector.tensor_tensor, prob[:, :, :], prob[:, :, :], up(et[:, :], NEXP), ALU.mult, after=[m])
            m = V.do(nc.vector.tensor_reduce, rw[:, :], prob[:, :, :], AX.X, ALU.max, after=[m])
            V.do(nc.vector.tensor_scalar, rws[:, :], rw[:, :], DK ** -0.5, None, ALU.mult, after=[m])
            m = V.do(nc.vector.tensor_tensor, mask[:, :, :], prob[:, :, :], up(rw[:, :], NEXP), ALU.is_equal, after=[m])
            m = V.do(nc.vector.tensor_copy, et[:, :], mask[:, :, 0], after=[m])
            for e in range(1, NEXP):
                m = V.do(nc.vector.tensor_tensor, mask[:, :, e], mask[:, :, e], et[:, :], ALU.is_gt, after=[m])
                m = V.do(nc.vector.tensor_tensor, et[:, :], et[:, :], mask[:, :, e], ALU.add, after=[m])
            for k in range(2):
                V.do(nc.vector.tensor_scalar, half[:, :, k, :], mask[:, :, :], g.half_col[:, k:k + 1], None, ALU.mult, after=[m])
            masked = V.last()
            yield
            yield
            for b in range(NB):
                for c in range(4):
                    tr = T.do(nc.tensor.transpose, g.ps[4][0:NEXP, c * 128:(c + 1) * 128], mask[:, 4 * b + c, :], g.ident[:, :], after=[masked, A.last()])
                A.do(nc.scalar.copy, maskT[:, b * 512:(b + 1) * 512], g.ps[4][0:NEXP, :], after=[tr])
                yield
            used = [None] * 2
            for b in range(NB):
                bank = g.ps[4 + b % 2]
                for c in range(4):
                    ts = slice((4 * b + c) * 128, (4 * b + c + 1) * 128)
                    mm = T.do(nc.tensor.matmul, bank[:, c * 128:(c + 1) * 128], maskT[:, ts], maskT[:, ts], start=True, stop=True, after=[A.last(), used[b % 2]])
                same = bank[:, :].rearrange("p (t k) -> p t k", t=4)
                four = lambda ap: ap.unsqueeze(1).broadcast_to([128, 4, 128])
                V.do(nc.vector.tensor_tensor, tri_s[:, 4 * b:4 * b + 4, :], same, four(g.tri[:, :]), ALU.mult, after=[mm])
                used[b % 2] = V.do(nc.vector.tensor_tensor, cum_s[:, 4 * b:4 * b + 4, :], same, four(g.cum[:, :]), ALU.mult)
                yield

        route = routing()
        used = [None] * 4
        for t in range(NT):
            k = (1, 2, 3, 6)[t % 4]
            mm = T.do(nc.tensor.matmul, g.ps[k][:, :], a2T[0:64, t * 128:(t + 1) * 128], w["Wc"][0:64, :], start=True, stop=True, after=[low, lowq, used[t % 4]])
            s = used[t % 4] = A.do(nc.scalar.activation, gate[:, t, :], g.ps[k][:, :], ACT.Silu, after=[mm])
            heads = gate[:, t, :].rearrange("p (h e) -> p h e", h=FH)
            G.do(nc.gpsimd.tensor_tensor, heads, heads, w["norm"].unsqueeze(1).broadcast_to([128, FH, DK]), ALU.mult, after=[s])
            if t >= 2:
                next(route, None)
        for _ in route:
            pass
        nc.scalar.preload_act_table_set("natural_log_exp_and_others")
        p.join()
        early.close()

        two = lambda n, s, d=F32: [sb(f"{n}{i}", s, d) for i in range(2)]
        xs, a1s, a2s, cs = two("x_tile", [128, 128]), two("qk_tile", [128, 128]), two("gate_tile", [128, 128]), two("cum_tile", [128, 128])
        v_t, vm = two("v_tile", [128, FH, DK]), two("v_experts", [128, FH, NEXP, DK])
        ms = two("mask_tile", [128, NEXP])
        qg, kg = two("q_decayed", [128, 2, KD]), two("k_decayed", [128, 2, KD])
        qT, kT = two("q_decayedT", [128, 2, 4, 128]), two("k_decayedT", [128, 2, 4, 128])
        eh = two("exp_halves", [128, 4, 2, ST])
        gk = sb("log_decay", [128, 2, KD])
        ab = sb("abs_logit", [128, 2, KD])
        eg, en = sb("exp_cum", [128, 2, KD]), sb("exp_neg_cum", [128, 2, KD])
        k2 = sb("k_softmax", [128, KD])
        ks1 = sb("k_stats", [128, FH])
        sA = sb("scores_dense", [128, 2, 4, 128])
        sB = sb("scores_expert", [128, 2, 4, 128])
        SX, SD = sb("state_experts", [128, 4, NEXP, DK]), sb("state_dense", [128, 4, 2, DK])
        U = sb("state_end", [128, 4, ST, DK])
        dec = sb("state_decay", [128, 4, ST])
        o_t, o_q = two("out_tile", [128, KD]), sb("out_square", [128, KD])
        rms = sb("out_rms", [128, FH])
        oT = sb("out_T", [128, 4, 128])
        i1 = G.do(nc.gpsimd.memset, U[:, :, :, :], 0.0)
        i3 = G.do(nc.gpsimd.memset, SD[:, :, :, :], 0.0)
        i2 = G.do(nc.gpsimd.memset, eh[1][:, :, :, :], 1.0)
        hv = lambda ap: ap.rearrange("p (h e) -> p h e", h=FH)
        P3, Abank, Obank, Ybank = g.ps[0:3], g.ps[3:5], g.ps[5], g.ps[6:8]

        st = dict(bank=[None] * 3, A=[None] * 2, O=None, Y=[None] * 2, B=[None] * 2, gk=None, eg=None, gkr=None, kgd=None, k2=None, xs=None, U=None,
                  Send=None, O_read=None, turn=[None, None], out=[None, None], out_read=[None, None], oT_read=None, rms_read=None, staged=[None, None], projected=[None, None])
        nb = [0]

        def bank(*more):
            k = nb[0] % 3
            nb[0] += 1
            return k, P3[k]

        def stage_tile(q, t):
            for dst, src in ((a2s[q], a2T[:, bass.ts(t, 128)]), (a1s[q], a1T[:, bass.ts(t, 128)]), (xs[q], g.xnT[:, bass.ts(t, 128)]),
                             (cs[q], cum_s[:, :, :].rearrange("p t k -> p (t k)")[:, bass.ts(t, 128)])):
                st["staged"][q] = G.do(nc.gpsimd.tensor_copy, dst[:, :], src, after=[st["projected"][q]])

        def stage_a(q, t, st, more):
            free, c = st["B"][q], st["staged"][q]
            zs = []
            for k, r in ((0, 64), (1, 96)):
                b, ps = bank()
                mm = T.do(nc.tensor.matmul, ps[:, :], a2s[q][r:r + 17, :], w["Wc"][r:r + 17, :], start=True, stop=True, after=[c, st["bank"][b]])
                m = A.do(nc.scalar.activation, ab[:, k, :], ps[:, :], ACT.Abs, after=[mm, st["gk"]])
                z = V.do(nc.vector.tensor_scalar, gk[:, k, :], ps[:, :], 0.0, 1 / 16.0, ALU.min, ALU.mult, after=[m, st["gkr"]])
                st["bank"][b] = z
            m = A.do(nc.scalar.activation, ab[:, :, :], ab[:, :, :], ACT.Exp, scale=-1.0, after=[m])
            m = A.do(nc.scalar.activation, ab[:, :, :], ab[:, :, :], ACT.Ln, bias=1.0, after=[m])
            mc = G.do(nc.gpsimd.tensor_copy, ms[q][:, :], mask[:, :, :].rearrange("p t e -> p (t e)")[:, bass.ts(t, NEXP)], after=[free])
            b, ps = bank()
            mm = T.do(nc.tensor.matmul, ps[:, :], xs[q][:, :], w["Wp"][:, 1024:1536], start=True, stop=True, after=[c, st["bank"][b]])
            vv = st["bank"][b] = A.do(nc.scalar.copy, v_t[q][:, :, :].rearrange("p h e -> p (h e)"), ps[:, :], after=[mm, free])
            for e in range(NEXP):
                G.do(nc.gpsimd.tensor_scalar, vm[q][:, :, e, :], v_t[q][:, :, :], ms[q][:, e:e + 1], 1.0, ALU.mult, ALU.mult, after=[vv, mc, free])
            yield
            b, ps = bank()
            mm = T.do(nc.tensor.matmul, ps[:, :], a1s[q][64:128, :], w["Wb"][64:128, :], start=True, stop=True, after=[c, st["bank"][b]])
            r = V.do(nc.vector.tensor_reduce, ks1[:, :], hv(ps[:, :]), AX.X, ALU.max, after=[mm])
            gm = st["gk"] = V.do(nc.vector.scalar_tensor_tensor, gk[:, :, :], ab[:, :, :], -1 / 16.0, gk[:, :, :], ALU.mult, ALU.add, after=[m, z])
            bc = lambda ap: ap.unsqueeze(2).broadcast_to([128, FH, DK])
            r = st["bank"][b] = V.do(nc.vector.tensor_tensor, hv(k2[:, :]), hv(ps[:, :]), bc(ks1[:, :]), ALU.subtract, after=[r])
            r = A.do(nc.scalar.activation, k2[:, :], k2[:, :], ACT.Exp, after=[r])
            es = []
            for k, lhs in ((0, g.cum), (1, cs[q])):
                b, ps = bank()
                mm = T.do(nc.tensor.matmul, ps[:, :], lhs[:, :], gk[:, k, :], start=True, stop=True, after=[gm, c, st["bank"][b]])
                A.do(nc.scalar.activation, eg[:, k, :], ps[:, :], ACT.Exp, after=[mm, st["kgd"]])
                st["bank"][b] = A.do(nc.scalar.activation, en[:, k, :], ps[:, :], ACT.Exp, scale=-1.0)
                es.append(st["bank"][b])
            yield
            b, ps = bank()
            for pr in range(4):
                o = ps[:, pr * 16:pr * 16 + 10].rearrange("p (k s) -> p k s", s=ST)
                T.do(nc.tensor.matmul, o[:, :, 0], gk[:, 0, pr * 128:(pr + 1) * 128], g.half_col[:, :], start=True, stop=True, after=[st["bank"][b]])
                mm = T.do(nc.tensor.matmul, o[:, :, 1:ST], gk[:, 1, pr * 128:(pr + 1) * 128],
                          half[:, :, :, :].rearrange("p t k e -> p t (k e)")[:, bass.ds(t, 1), :].rearrange("p t (k e) -> p (t k) e", k=2),
                          start=True, stop=True)
            st["gkr"] = mm
            st["bank"][b] = A.do(nc.scalar.activation, eh[q][:, :, :, :].rearrange("p r k s -> p r (k s)"),
                                 ps[:, 0:64].rearrange("p (r x) -> p r x", r=4)[:, :, 0:10], ACT.Exp, after=[mm, free])
            s = V.do(nc.vector.tensor_reduce, ks1[:, :], hv(k2[:, :]), AX.X, ALU.add, after=[r])
            s = V.do(nc.vector.reciprocal, ks1[:, :], ks1[:, :], after=[s])
            s = V.do(nc.vector.tensor_scalar, ks1[:, :], ks1[:, :], rw[:, bass.ds(t, 1)], None, ALU.mult, after=[s])
            s = V.do(nc.vector.tensor_tensor, hv(k2[:, :]), hv(k2[:, :]), bc(ks1[:, :]), ALU.mult, after=[s])
            s = V.do(nc.vector.tensor_tensor, kg[q][:, 1, :], k2[:, :], en[:, 1, :], ALU.mult, after=[s, es[1], free])
            yield
            def turn(src, dst, k, made):
                b, ps = bank()
                for pr in range(4):
                    tr = T.do(nc.tensor.transpose, ps[:, pr * 128:(pr + 1) * 128], src[:, k, pr * 128:(pr + 1) * 128], g.ident[:, :], after=[made, st["bank"][b]])
                eng, fn = ((A, nc.scalar.copy), (V, nc.vector.tensor_copy))[k]
                st["turn"][k] = st["bank"][b] = eng.do(fn, dst[:, k, :, :].rearrange("p r t -> p (r t)"), ps[:, :], after=[tr, free])

            b, ps = bank()
            mm = T.do(nc.tensor.matmul, ps[:, :], xs[q][:, :], w["Wp"][:, 512:1024], start=True, stop=True, after=[st["bank"][b]])
            k1 = st["bank"][b] = V.do(nc.vector.tensor_tensor, kg[q][:, 0, :], ps[:, :], en[:, 0, :], ALU.mult, after=[mm, es[0], free])
            b, ps = bank()
            mm = T.do(nc.tensor.matmul, ps[:, :], a1s[q][0:64, :], w["Wb"][0:64, :], start=True, stop=True, after=[st["bank"][b]])
            q2 = st["bank"][b] = V.do(nc.vector.scalar_tensor_tensor, qg[q][:, 1, :], ps[:, :], rws[:, bass.ds(t, 1)], eg[:, 1, :], ALU.mult, ALU.mult, after=[mm, free])
            yield
            turn(kg[q], kT[q], 1, s)
            b, ps = bank()
            mm = T.do(nc.tensor.matmul, ps[:, :], xs[q][:, :], w["Wp"][:, 0:512], start=True, stop=True, after=[st["bank"][b]])
            q1 = st["bank"][b] = st["kgd"] = V.do(nc.vector.scalar_tensor_tensor, qg[q][:, 0, :], ps[:, :], DK ** -0.5, eg[:, 0, :], ALU.mult, ALU.mult, after=[mm, free])
            st["projected"][q] = mm
            if more:
                stage_tile(q, t + 2)
            yield
            turn(kg[q], kT[q], 0, k1)
            yield
            turn(qg[q], qT[q], 1, q2)
            yield
            turn(qg[q], qT[q], 0, q1)
            yield

        def stage_b(q, t, st):
            o_s = o_t[q]
            turned = list(st["turn"])
            d = V.do(nc.vector.tensor_tensor, dec[:, :, :], eh[1 - q][:, :, 1, :], eh[q][:, :, 0, :], ALU.mult, after=turned + [st["Send"]])
            wide = lambda ap, k: ap.unsqueeze(3).broadcast_to([ap.shape[0], 4, k, DK])
            for x in range(2):
                r = slice(64 * x, 64 * x + 64)
                sd = V.do(nc.vector.tensor_tensor, SD[r, :, x, :], U[r, :, 0, :], dec[r, :, 0:1].broadcast_to([64, 4, DK]), ALU.mult,
                          after=[d, st["U"], st["Send"]])
            sm = G.do(nc.gpsimd.tensor_tensor, SX[:, :, :, :], U[:, :, 1:ST, :], wide(dec[:, :, 1:ST], NEXP), ALU.mult,
                      after=[d, st["U"], st["Send"]])
            for k, dst in ((0, sA), (1, sB)):
                for x in range(2):
                    r = slice(64 * x, 64 * x + 64)
                    for y in range(4):
                        mm = T.do(nc.tensor.matmul, Abank[x][:, y * 128:y * 128 + 128], kT[q][r, k, y, :], qT[q][r, k, y, :],
                                  start=True, stop=True, after=turned + [st["A"][x]])
                    mt = g.tri[:, :] if k == 0 else tri_s[:, :, :].rearrange("p t k -> p (t k)")[:, bass.ts(t, 128)]
                    st["A"][x] = V.do(nc.vector.tensor_tensor, dst[:, x, :, :], Abank[x][:, :].rearrange("p (h t) -> p h t", h=4),
                                      mt.unsqueeze(1).broadcast_to([128, 4, 128]), ALU.mult, after=[mm, st["O"]])
                    yield
            scored = V.last()
            ao = G.do(nc.gpsimd.tensor_tensor, sA[:, :, :, :], sA[:, :, :, :], sB[:, :, :, :], ALU.add, after=[scored])

            def on_states(z):
                x = z % 2
                r = slice(64 * x, 64 * x + 64)
                for y in (0, 1):
                    mm = T.do(nc.tensor.matmul, Ybank[x][:, y * 256:y * 256 + 256], qT[q][r, 1, 2 * (z // 2) + y, :], SX[r, 2 * (z // 2) + y, :, :],
                              start=True, stop=True, after=[sm, st["Y"][x]])
                return mm

            ys = [on_states(0), on_states(1)]
            yield
            for y in range(4):
                T.do(nc.tensor.matmul, Obank[:, y * 128:(y + 1) * 128], qT[q][:, 0, y, :], SD[:, y, :, :], start=True, stop=False, after=[sd, st["O_read"]],
                     skip_group_check=True)
                for x in range(2):
                    h = 2 * y + x
                    mm = T.do(nc.tensor.matmul, Obank[:, h * DK:(h + 1) * DK], sA[:, x, y, :], v_t[q][:, h, :], start=False, stop=True, after=[ao],
                              skip_group_check=True)
            st["O"] = mm
            oc = st["O_read"] = A.do(nc.scalar.copy, o_s[:, :], Obank[:, :], after=[mm, st["out_read"][q]])
            yield
            for z in range(4):
                x = z % 2
                if z >= 2:
                    ys.append(on_states(z))
                o2 = o_s[:, :].rearrange("p (y x e) -> p y x e", x=2, e=DK)[:, 2 * (z // 2):2 * (z // 2) + 2, x, :]
                y = Ybank[x][:, :].rearrange("p (h x e) -> p h x e", h=2, x=NEXP)
                m = oc
                for e in range(NEXP):
                    m = V.do(nc.vector.scalar_tensor_tensor, o2, y[:, :, e, :], mask[:, :, :].rearrange("p t e -> p (t e)")[:, bass.ds(t * NEXP + e, 1)], o2,
                             ALU.mult, ALU.add, after=[ys[z], m])
                st["Y"][x] = m
            st["out"][q] = m
            yield
            for x in range(3):
                bnk = (Abank[0], Abank[1], Ybank[0])[x]
                prev = (st["A"][0], st["A"][1], st["Y"][0])[x]
                if x < 2:
                    for h in range(4 * x, 4 * x + 4):
                        r = slice(64 * (h % 2), 64 * (h % 2) + 64)
                        mm = T.do(nc.tensor.matmul, bnk[r, (h // 2 % 2) * 256:(h // 2 % 2) * 256 + 256], kg[q][:, 1, h * DK:(h + 1) * DK], vm[q][:, h, :, :],
                                  start=True, stop=True, after=[prev, G.last()])
                    m = V.do(nc.vector.tensor_tensor, U[:, 2 * x:2 * x + 2, 1:ST, :], SX[:, 2 * x:2 * x + 2, :, :],
                             bnk[:, :].rearrange("p (r x e) -> p r x e", r=2, x=NEXP), ALU.add, after=[mm, sm])
                    st["A"][x] = m
                else:
                    for h in range(FH):
                        r = slice(64 * (h % 2), 64 * (h % 2) + 64)
                        mm = T.do(nc.tensor.matmul, bnk[r, (h // 2) * DK:(h // 2 + 1) * DK], kg[q][:, 0, h * DK:(h + 1) * DK], v_t[q][:, h, :],
                                  start=True, stop=True, after=[prev])
                    for y in range(2):
                        r = slice(64 * y, 64 * y + 64)
                        m = V.do(nc.vector.tensor_tensor, U[r, :, 0, :], SD[r, :, y, :], bnk[r, 0:256].rearrange("p (r e) -> p r e", r=4), ALU.add, after=[mm])
                    st["Y"][0] = m
            st["B"][q] = mm
            st["U"] = st["Send"] = m

        def stage_c(q, t, st):
            o_s = o_t[q]
            m = A.do(nc.scalar.activation, o_q[:, :], o_s[:, :], ACT.Square, after=[st["out"][q], st["rms_read"]])
            gt = G.do(nc.gpsimd.tensor_tensor, o_s[:, :], o_s[:, :], gate[:, :, :].rearrange("p t k -> p (t k)")[:, bass.ts(t, KD)], ALU.mult, after=[m])
            yield
            m = V.do(nc.vector.tensor_reduce, rms[:, :], hv(o_q[:, :]), AX.X, ALU.add, after=[m])
            st["rms_read"] = m
            m = A.do(nc.scalar.activation, rms[:, :], rms[:, :], ACT.Ln, bias=g.eps_ln[:, :], scale=1.0 / DK, after=[m])
            m = A.do(nc.scalar.activation, rms[:, :], rms[:, :], ACT.Exp, scale=-0.5, after=[m])
            yield
            m = V.do(nc.vector.tensor_tensor, hv(o_s[:, :]), hv(o_s[:, :]), rms[:, :].unsqueeze(2).broadcast_to([128, FH, DK]), ALU.mult, after=[m, gt])
            yield
            b, ps = bank()
            for c in range(4):
                tr = T.do(nc.tensor.transpose, ps[:, c * 128:(c + 1) * 128], o_s[:, c * 128:(c + 1) * 128], g.ident[:, :], after=[m, st["bank"][b]])
            st["out_read"][q] = tr
            m = st["bank"][b] = A.do(nc.scalar.copy, oT[:, :, :].rearrange("p c t -> p (c t)"), ps[:, :], after=[tr, st["oT_read"]])
            yield
            b, ps = bank()
            for c in range(4):
                mm = T.do(nc.tensor.matmul, ps[:, 0:128], oT[:, c, :], w["Wo"][:, c * 128:(c + 1) * 128], start=(c == 0), stop=(c == 3), after=[m, st["bank"][b]])
            st["oT_read"] = mm
            x = g.x_tok[:, :, :].rearrange("p t d -> p (t d)")[:, bass.ts(t, 128)]
            st["bank"][b] = V.do(nc.vector.tensor_tensor, x, x, ps[:, 0:128], ALU.add, after=[mm])
            yield

        def together(*gens):
            gens = list(gens)
            while gens:
                for x in list(gens):
                    if next(x, "end") == "end":
                        gens.remove(x)

        p.join()
        stage_tile(0, 0)
        stage_tile(1, 1)
        together(stage_a(0, 0, st, True))

        def step(t, par, after, before, more=True):
            stages = dict(b=stage_b(par, t, st), a=stage_a(1 - par, t + 1, st, more) if after else iter(()),
                          c=stage_c(1 - par, t - 1, st) if before else iter(()))
            for name in ORDER:
                next(stages[name], None)

        def tiles(t):
            nb[0] = 0
            step(t, 1, True, True)
            step(t + 1, 0, True, True)

        step(0, 0, True, False)
        p.pipeline(NT // 2 - 2, lambda i: tiles(2 * i + 1), st)
        step(NT - 3, 1, True, True, False)
        step(NT - 2, 0, True, True, False)
        step(NT - 1, 1, False, True)
        together(stage_c(1, NT - 1, st))
        p.join()


DI, NS, RANK, CONV = 256, 16, 8, 4
CHK = 1024

def mamba(g, w, tag):
    nc, p, V, A, T, G = g.nc, g.p, g.V, g.A, g.T, g.G
    with ExitStack() as mem:
        sb = lambda n, s, d=F32: mem.enter_context(nc.sbuf_tensor(f"{n}{g.uid()}", s, d))
        res, xi = sb("silu_res", [128, 2, N]), sb("conv_out", [128, 2, N])
        dt, dtx = sb("dt", [128, 2, N]), sb("dt_x", [128, 2, N])
        BC = sb("bc_parts", [96, N], BF16)
        sel = sb("row_select", [96, 2 * NS, 128], BF16)
        negA = sb("neg_A", [128, 2, NS])
        with ExitStack() as early:
            sbe = lambda n, s, d=F32: early.enter_context(nc.sbuf_tensor(f"{n}{g.uid()}", s, d))
            xp = sbe("conv_in", [128, 2, CONV - 1 + N])
            bcf = sbe("bc_full", [32, 2, N])
            dlt = sbe("delta", [RANK, N])
            z = G.do(nc.gpsimd.memset, xp[:, :, 0:CONV - 1], 0.0)
            m = G.do(nc.gpsimd.memset, sel[:, :, :], 0.0)
            for k in range(3):
                m = G.do(nc.gpsimd.affine_select, out=sel[:, :, :], in_=sel[:, :, :], compare_op=ALU.not_equal, fill=1.0, base=-32 * k,
                         pattern=[[-1, 2 * NS], [0, 128]], channel_multiplier=1, after=[m])
            m = A.do(nc.scalar.activation, negA[:, :, :], w["A_log"], ACT.Exp)
            V.do(nc.vector.tensor_scalar, negA[:, :, :], negA[:, :, :], -1.0, None, ALU.mult, after=[m])
            nc.scalar.preload_act_table(ACT.Silu)
            free = [None] * 8
            conv = []
            for c in range(4):
                for b in range(NB):
                    k = (c * NB + b) % 8
                    ts = slice(b * 512, (b + 1) * 512)
                    mm = T.do(nc.tensor.matmul, g.ps[k][:, :], w["in_proj"][:, c * 128:(c + 1) * 128], g.xnT[:, ts], start=True, stop=True, after=[free[k]])
                    if c < 2:
                        free[k] = A.do(nc.scalar.copy, xp[:, c, CONV - 1 + b * 512:CONV - 1 + (b + 1) * 512], g.ps[k][:, :], after=[mm])
                    else:
                        free[k] = A.do(nc.scalar.activation, res[:, c - 2, ts], g.ps[k][:, :], ACT.Silu, after=[mm])
                if c < 2:
                    m = V.do(nc.vector.tensor_scalar, xi[:, c, :], xp[:, c, 0:N], w["conv_w"][:, c, 0:1], w["conv_b"][:, c:c + 1], ALU.mult, ALU.add,
                             after=[free[k], z])
                    for q in range(1, CONV):
                        m = V.do(nc.vector.scalar_tensor_tensor, xi[:, c, :], xp[:, c, q:q + N], w["conv_w"][:, c, q:q + 1], xi[:, c, :], ALU.mult, ALU.add, after=[m])
                    conv.append(m)
            for c in range(2):
                a = A.do(nc.scalar.activation, xi[:, c, :], xi[:, c, :], ACT.Silu, after=[conv[c]])
            for b in range(NB):
                ts = slice(b * 512, (b + 1) * 512)
                k0, k1 = 2 * (b % 2), 2 * (b % 2) + 1
                for c in range(2):
                    mb = T.do(nc.tensor.matmul, g.ps[k0][0:32, :], w["x_proj"][:, c, RANK:RANK + 32], xi[:, c, ts], start=(c == 0), stop=(c == 1), after=[a, free[k0], free[k1]])
                for c in range(2):
                    md = T.do(nc.tensor.matmul, g.ps[k1][0:RANK, :], w["x_proj"][:, c, 0:RANK], xi[:, c, ts], start=(c == 0), stop=(c == 1))
                f0 = V.do(nc.vector.tensor_copy, bcf[:, 0, ts], g.ps[k0][0:32, :], after=[mb])
                f1 = V.do(nc.vector.tensor_copy, dlt[:, ts], g.ps[k1][0:RANK, :], after=[md])
                free[k0], free[k1] = f0, f1
            m = V.do(nc.vector.tensor_copy, BC[0:32, :], bcf[:, 0, :], after=[f0])
            m = V.do(nc.vector.tensor_tensor, bcf[:, 1, :], bcf[:, 0, :], BC[0:32, :], ALU.subtract, after=[m])
            m = V.do(nc.vector.tensor_copy, BC[32:64, :], bcf[:, 1, :], after=[m])
            m = A.do(nc.scalar.copy, bcf[:, 0, :], BC[32:64, :], after=[m])
            m = V.do(nc.vector.tensor_tensor, BC[64:96, :], bcf[:, 1, :], bcf[:, 0, :], ALU.subtract, after=[m])
            nc.scalar.preload_act_table_set("natural_log_exp_and_others")
            zb = xp[:, :, 0:N]
            ee, uu = dtx, sbe("one_plus_e", [128, N])
            for c in range(2):
                for b in range(NB):
                    k = 4 + (c * NB + b) % 4
                    ts = slice(b * 512, (b + 1) * 512)
                    mm = T.do(nc.tensor.matmul, g.ps[k][:, :], w["dt_w"][0:RANK, c * 128:(c + 1) * 128], dlt[:, ts], start=True, stop=True, after=[f1, free[k]])
                    free[k] = A.do(nc.scalar.activation, zb[:, c, ts], g.ps[k][:, :], ACT.Identity, bias=w["dt_b"][:, c:c + 1], after=[mm, V.last()])
                m = A.do(nc.scalar.activation, ee[:, c, :], zb[:, c, :], ACT.Abs, after=[free[k]])
                m = A.do(nc.scalar.activation, ee[:, c, :], ee[:, c, :], ACT.Exp, scale=-1.0, after=[m])
                u = V.do(nc.vector.tensor_scalar, uu[:, :], ee[:, c, :], 1.0, None, ALU.add, after=[m])
                ln = A.do(nc.scalar.activation, dt[:, c, :], uu[:, :], ACT.Ln, after=[u])
                m = V.do(nc.vector.scalar_tensor_tensor, ee[:, c, :], uu[:, :], 1.0, ee[:, c, :], ALU.subtract, ALU.subtract, after=[u])
                m = V.do(nc.vector.tensor_tensor, dt[:, c, :], dt[:, c, :], ee[:, c, :], ALU.subtract, after=[ln, m])
                m = V.do(nc.vector.scalar_tensor_tensor, dt[:, c, :], zb[:, c, :], 0.0, dt[:, c, :], ALU.max, ALU.add, after=[m])
                V.do(nc.vector.tensor_tensor, dtx[:, c, :], dt[:, c, :], xi[:, c, :], ALU.mult, after=[m])
            p.join()
        nc.scalar.preload_act_table_set("natural_log_exp_and_others")
        E = [[sb(f"decay{i}{c}", [128, CHK]) for c in range(2)] for i in range(2)]
        F = [[sb(f"state{i}{c}", [128, CHK]) for c in range(2)] for i in range(2)]
        Cs = [sb(f"c_row{i}", [128, CHK]) for i in range(2)]
        carry = sb("state_carry", [128, 2, NS])
        zero = sb("zero_row", [1, 512], BF16)
        y = sb("scan_out", [128, 2, N])
        G.do(nc.gpsimd.memset, carry[:, :, :], 0.0)
        zz = G.do(nc.gpsimd.memset, zero[:, :], 0.0)
        Bb, Cb, Yb = g.ps[0:2], g.ps[2:4], g.ps[4:8]
        for chunk in range(N // CHK):
            t0 = chunk * CHK
            st = dict(B=[None, None], C=None, E=[[None, None], [None, None]], Cs=[None, None], Fh=[[None, None], [None, None]], car=[[None, None], [None, None]])
            for k in range(4):
                T.do(nc.tensor.matmul, Yb[k][:, :], zero[:, 0:128], zero[:, :], start=True, stop=True, after=[zz, V.last()], skip_group_check=True)

            def front(n, i):
                for b in range(2):
                    ts = slice(t0 + b * 512, t0 + (b + 1) * 512)
                    mb = T.do(nc.tensor.matmul, Bb[b][:, :], sel[:, bass.ds(n, 1), :].rearrange("p a b -> p (a b)"), BC[:, ts], start=True, stop=True, after=[st["B"][1]])
                for b in range(2):
                    ts = slice(t0 + b * 512, t0 + (b + 1) * 512)
                    mc = T.do(nc.tensor.matmul, Cb[b][:, :], sel[:, bass.ds(n + NS, 1), :].rearrange("p a b -> p (a b)"), BC[:, ts], start=True, stop=True, after=[st["C"]])
                dec = []
                for c in range(2):
                    dec.append(A.do(nc.scalar.activation, E[i][c][:, :], dt[:, c, t0:t0 + CHK], ACT.Exp, scale=negA[:, c, bass.ds(n, 1)], after=[st["E"][i][c]]))
                cb = st["C"] = A.do(nc.scalar.copy, Cs[i][:, :], g.wide(2)[:, :], after=[mc, st["Cs"][i]])
                for c in range(2):
                    st["B"][c] = V.do(nc.vector.tensor_tensor, F[i][c][:, :], dtx[:, c, t0:t0 + CHK], g.wide(0)[:, :], ALU.mult, after=[mb, st["Fh"][i][c], st["car"][i][c]])
                for c in range(2):
                    h = V.do(nc.vector.tensor_tensor_scan, F[i][c][:, :], E[i][c][:, :], F[i][c][:, :], carry[:, c, bass.ds(n, 1)], ALU.mult, ALU.add,
                             after=[dec[c], st["B"][c]])
                    st["car"][i][c] = A.do(nc.scalar.copy, carry[:, c, bass.ds(n, 1)], F[i][c][:, CHK - 1:CHK], after=[h])
                    st["Cs"][i] = st["Fh"][i][c] = G.do(nc.gpsimd.tensor_tensor, E[i][c][:, :], F[i][c][:, :], Cs[i][:, :], ALU.mult, after=[h, cb])

            def back(i):
                for c in range(2):
                    for b in range(2):
                        st["E"][i][c] = T.do(nc.tensor.matmul, Yb[2 * c + b][:, :], g.ident[:, :], E[i][c][:, b * 512:(b + 1) * 512], start=False, stop=True,
                                             after=[st["Fh"][i][c]], skip_group_check=True)

            def pair(n0):
                front(n0 + 1, 1)
                back(0)
                front(n0 + 2, 0)
                back(1)

            p.join()
            front(0, 0)
            p.pipeline(NS // 2 - 1, lambda i: pair(2 * i), st)
            front(NS - 1, 1)
            back(0)
            back(1)
            p.join()
            for c in range(2):
                for b in range(2):
                    ts = slice(t0 + b * 512, t0 + (b + 1) * 512)
                    m = V.do(nc.vector.scalar_tensor_tensor, y[:, c, ts], xi[:, c, ts], w["Dp"][:, c:c + 1], Yb[2 * c + b][:, :], ALU.mult, ALU.add)
                G.do(nc.gpsimd.tensor_tensor, y[:, c, t0:t0 + CHK], y[:, c, t0:t0 + CHK], res[:, c, t0:t0 + CHK], ALU.mult, after=[m])
        gm = G.last()
        for b in range(NB):
            for q in range(4):
                t = 4 * b + q
                for c in range(2):
                    mm = T.do(nc.tensor.matmul, g.ps[b][:, q * 128:(q + 1) * 128], y[:, c, t * 128:(t + 1) * 128], w["out_proj"][:, c, :], start=(c == 0), stop=(c == 1), after=[gm, V.last()])
            xx = g.x_tok[:, 4 * b:4 * b + 4, :]
            V.do(nc.vector.tensor_tensor, xx, xx, g.ps[b][:, :].rearrange("p (t f) -> p t f", t=4), ALU.add, after=[mm])
        p.join()


EXPERTS, SHARED = 8, 2
UNITS = EXPERTS + SHARED

def first_of(g, V, mask, count, one, after):
    nc = g.nc
    m = V.do(nc.vector.tensor_copy, count, mask[:, :, 0], after=after)
    for e in range(1, one):
        m = V.do(nc.vector.tensor_tensor, mask[:, :, e], mask[:, :, e], count, ALU.is_gt, after=[m])
        m = V.do(nc.vector.tensor_tensor, count, count, mask[:, :, e], ALU.add, after=[m])
    return m

def moe(g, w, beside=None):
    nc, p, V, A, T, G = g.nc, g.p, g.V, g.A, g.T, g.G
    with ExitStack() as mem:
        sb = lambda n, s, d=F32: mem.enter_context(nc.sbuf_tensor(f"{n}{g.uid()}", s, d))
        sc, bs, m1, m2 = (sb(f"route{i}", [128, NT, EXPERTS]) for i in range(4))
        et = sb("route_tmp", [128, NT])
        GT = sb("gate_parts", [96, N], BF16)
        gf = sb("gate_full", [EXPERTS, 3, N])
        sel = sb("gate_select", [96, EXPERTS, 128], BF16)
        sa = sb("silu_a", [128, 3, 512])
        hs = sb("hidden", [128, 3, 512])
        cleared = G.do(nc.gpsimd.memset, GT[:, :], 0.0)
        m = G.do(nc.gpsimd.memset, sel[:, :, :], 0.0)
        for k in range(3):
            m = G.do(nc.gpsimd.affine_select, out=sel[:, :, :], in_=sel[:, :, :], compare_op=ALU.not_equal, fill=1.0, base=-32 * k,
                     pattern=[[-1, EXPERTS], [0, 128]], channel_multiplier=1, after=[m])
        selects = m
        up = lambda ap: ap.unsqueeze(2).broadcast_to([128, NT, EXPERTS])
        turn_banks = (g.ps[0], g.ps[6], g.ps[7])
        st = dict(a=[None] * 2, b=[None] * 2, gb=None, h=[None] * 3, y=None, sa=[None] * 3)
        Ab, Bb, Gb, Yb = g.ps[1:3], g.ps[3:5], g.ps[6], g.ps[5]

        le = g.ps[0][:, 0:NT * EXPERTS].rearrange("p (t e) -> p t e", e=EXPERTS)
        for t in range(NT):
            mm = T.do(nc.tensor.matmul, g.ps[0][:, t * EXPERTS:(t + 1) * EXPERTS], g.xnT[:, t * 128:(t + 1) * 128], w["gate"], start=True, stop=True)
        m = V.do(nc.vector.tensor_reduce, et[:, :], le, AX.X, ALU.max, after=[mm])
        m = V.do(nc.vector.tensor_tensor, sc[:, :, :], le, up(et[:, :]), ALU.subtract, after=[m])
        exped = A.do(nc.scalar.activation, sc[:, :, :], sc[:, :, :], ACT.Exp, after=[m])
        nc.scalar.preload_act_table(ACT.Silu)

        def routing():
            m = V.do(nc.vector.tensor_reduce, et[:, :], sc[:, :, :], AX.X, ALU.add, after=[exped])
            m = V.do(nc.vector.reciprocal, et[:, :], et[:, :], after=[m])
            m = V.do(nc.vector.tensor_tensor, sc[:, :, :], sc[:, :, :], up(et[:, :]), ALU.mult, after=[m])
            m = V.do(nc.vector.tensor_tensor, bs[:, :, :], sc[:, :, :], w["gate_bias"].unsqueeze(1).broadcast_to([128, NT, EXPERTS]), ALU.add, after=[m])
            for mk in (m1, m2):
                yield
                m = V.do(nc.vector.tensor_reduce, et[:, :], bs[:, :, :], AX.X, ALU.max, after=[m])
                m = V.do(nc.vector.tensor_tensor, mk[:, :, :], bs[:, :, :], up(et[:, :]), ALU.is_equal, after=[m])
                m = first_of(g, V, mk, et[:, :], EXPERTS, [m])
                if mk is m1:
                    m = V.do(nc.vector.scalar_tensor_tensor, bs[:, :, :], m1[:, :, :], -1e30, bs[:, :, :], ALU.mult, ALU.add, after=[m])
            m = V.do(nc.vector.tensor_tensor, m1[:, :, :], m1[:, :, :], m2[:, :, :], ALU.add, after=[m])
            m = V.do(nc.vector.tensor_tensor, m1[:, :, :], m1[:, :, :], sc[:, :, :], ALU.mult, after=[m])
            yield
            read = [None] * 3
            for b in range(NB):
                ts = slice(b * 512, (b + 1) * 512)
                bank = turn_banks[b % 3]
                for c in range(4):
                    tr = T.do(nc.tensor.transpose, bank[0:EXPERTS, c * 128:(c + 1) * 128], m1[:, 4 * b + c, :], g.ident[:, :], after=[m, read[b % 3]])
                cp = read[b % 3] = A.do(nc.scalar.copy, gf[:, 0, ts], bank[0:EXPERTS, :], after=[tr])
                v = V.do(nc.vector.tensor_copy, GT[0:8, ts], gf[:, 0, ts], after=[cp, cleared])
                v = V.do(nc.vector.tensor_tensor, gf[:, 1, ts], gf[:, 0, ts], GT[0:8, ts], ALU.subtract, after=[v])
                v = V.do(nc.vector.tensor_copy, GT[32:40, ts], gf[:, 1, ts], after=[v])
                a = A.do(nc.scalar.copy, gf[:, 2, ts], GT[32:40, ts], after=[v])
                yield
                V.do(nc.vector.tensor_tensor, GT[64:72, ts], gf[:, 1, ts], gf[:, 2, ts], ALU.subtract, after=[a])

        def experts(ts, units):
            hid = {}

            def front(u):
                k = u % 2
                ma = T.do(nc.tensor.matmul, Ab[k], w["w1"][:, u, :], g.xnT[:, ts], start=True, stop=True, after=[st["a"][k]])
                mb = T.do(nc.tensor.matmul, Bb[k], w["w3"][:, u, :], g.xnT[:, ts], start=True, stop=True, after=[st["b"][k]])
                if u < EXPERTS:
                    mg = T.do(nc.tensor.matmul, Gb, sel[:, u, :], GT[:, ts], start=True, stop=True, after=[st["gb"]])
                s = st["a"][k] = A.do(nc.scalar.activation, sa[:, u % 3, :], Ab[k], ACT.Silu, after=[ma, st["sa"][u % 3]])
                h = st["b"][k] = V.do(nc.vector.tensor_tensor, hs[:, u % 3, :], sa[:, u % 3, :], Bb[k], ALU.mult, after=[mb, s, st["h"][u % 3]])
                st["sa"][u % 3] = h
                if u < EXPERTS:
                    h = st["gb"] = V.do(nc.vector.tensor_tensor, hs[:, u % 3, :], hs[:, u % 3, :], Gb, ALU.mult, after=[mg, h])
                hid[u] = h

            def back(u):
                for c in range(4):
                    mm = T.do(nc.tensor.matmul, Yb[:, c * 128:(c + 1) * 128], hs[:, u % 3, c * 128:(c + 1) * 128], w["w2"][:, u, :],
                              start=(u == units[0] and c == 0), stop=(u == units[-1]), after=[hid[u], st["y"]], skip_group_check=True)
                st["h"][u % 3] = mm
                return mm

            front(units[0])
            yield
            for u in units[1:]:
                front(u)
                yield
                back(u - 1)
            mm = back(units[-1])
            x = g.x_tok[:, :, :].rearrange("p t d -> p (t d)")[:, ts]
            st["y"] = V.do(nc.vector.tensor_tensor, x, x, Yb, ALU.add, after=[mm])
            yield

        route = routing()
        for b in range(NB):
            for _ in experts(slice(b * 512, (b + 1) * 512), range(EXPERTS, UNITS)):
                next(route, None)
        for _ in route:
            pass
        p.wait(nc.tensor, [selects])
        left = []
        if beside:
            p.wait(nc.gpsimd, [V.last(), A.last()])
            beside()
            left = [G]

        def block(b):
            for _ in experts(bass.ts(b, 512), range(EXPERTS)):
                pass

        p.pipeline(NB, block, st, left)
        p.join(left)
        nc.scalar.preload_act_table_set("natural_log_exp_and_others")


TAPS = 4
SEG = 32
STEPS = N // SEG
GRP = 8
SPREADS = 4
EPS_R = 1e-6

def rotation_columns(g, theta, decay_log, col):
    nc, V, A = g.nc, g.V, g.A
    with ExitStack() as mem:
        ki = mem.enter_context(nc.sbuf_tensor(f"turns{g.uid()}", [128, 1], mybir.dt.int32))
        cc = lambda k: col[:, k:k + 1]
        vs = lambda o, i, a, b, o1, o2=ALU.bypass, **kw: V.do(nc.vector.tensor_scalar, o, i, a, b, o1, o2, after=[V.last(), A.last()])
        vt = lambda o, a, b, op: V.do(nc.vector.tensor_tensor, o, a, b, op, after=[V.last(), A.last()])
        TWO_PI = 2 * math.pi
        hi = 6.28125
        vs(cc(0), theta, 1 / TWO_PI, None, ALU.mult)
        V.do(nc.vector.tensor_copy, ki[:, :], cc(0), after=[V.last()])
        V.do(nc.vector.tensor_copy, cc(0), ki[:, :], after=[V.last()])
        V.do(nc.vector.scalar_tensor_tensor, cc(1), cc(0), -hi, theta, ALU.mult, ALU.add, after=[V.last()])
        V.do(nc.vector.scalar_tensor_tensor, cc(1), cc(0), -(TWO_PI - hi), cc(1), ALU.mult, ALU.add, after=[V.last()])
        vs(cc(1), cc(1), 0.5, None, ALU.mult)
        vs(cc(2), cc(1), -1.0, None, ALU.mult)
        vt(cc(2), cc(1), cc(2), ALU.max)
        vs(cc(2), cc(2), -1.0, math.pi / 2, ALU.mult, ALU.add)
        nc.scalar.preload_act_table(ACT.Sin)
        A.do(nc.scalar.activation, cc(3), cc(1), ACT.Sin, after=[V.last()])
        A.do(nc.scalar.activation, cc(4), cc(2), ACT.Sin)
        nc.scalar.preload_act_table_set("natural_log_exp_and_others")
        vt(cc(6), cc(3), cc(4), ALU.mult)
        vs(cc(6), cc(6), 2.0, None, ALU.mult)
        vt(cc(5), cc(3), cc(3), ALU.mult)
        vs(cc(5), cc(5), -2.0, 1.0, ALU.mult, ALU.add)
        A.do(nc.scalar.activation, cc(8), decay_log, ACT.Exp, after=[V.last()])
        A.do(nc.scalar.activation, cc(9), cc(8), ACT.Exp, scale=-1.0, after=[A.last()])
        vs(cc(10), cc(8), 0.25, None, ALU.min)
        vs(cc(11), cc(10), -1 / 7.0, 1.0, ALU.mult, ALU.add)
        for k in range(6, 0, -1):
            V.do(nc.vector.scalar_tensor_tensor, cc(11), cc(11), -1.0 / k, cc(10), ALU.mult, ALU.mult, after=[V.last()])
            vs(cc(11), cc(11), 1.0, None, ALU.add)
        vs(cc(12), cc(8), 0.25, None, ALU.is_lt)
        vt(cc(11), cc(11), cc(9), ALU.subtract)
        V.do(nc.vector.scalar_tensor_tensor, cc(7), cc(11), cc(12), cc(9), ALU.mult, ALU.add, after=[V.last()])


def rotation_tables(g, col, CT, ST, inv, s1, s2):
    nc, G = g.nc, g.G
    cc = lambda k: col[:, k:k + 1]
    gs = lambda o, i, a: G.do(nc.gpsimd.tensor_scalar, o, i, a, 1.0, ALU.mult, ALU.mult, after=[G.last()])
    gt = lambda o, a, b, op: G.do(nc.gpsimd.tensor_tensor, o, a, b, op, after=[G.last()])
    G.do(nc.gpsimd.memset, CT[:, 0:1], 1.0)
    G.do(nc.gpsimd.memset, ST[:, 0:1], 0.0)
    n = 1
    while n < N:
        gs(s1[:, 0:n], ST[:, 0:n], cc(6))
        gs(CT[:, n:2 * n], CT[:, 0:n], cc(5))
        gs(s2[:, 0:n], CT[:, 0:n], cc(6))
        gs(ST[:, n:2 * n], ST[:, 0:n], cc(5))
        gt(CT[:, n:2 * n], CT[:, n:2 * n], s1[:, 0:n], ALU.subtract)
        gt(ST[:, n:2 * n], ST[:, n:2 * n], s2[:, 0:n], ALU.add)
        gs(cc(14), cc(5), cc(6))
        gs(cc(15), cc(6), cc(6))
        gt(cc(6), cc(14), cc(14), ALU.add)
        gs(cc(14), cc(5), cc(5))
        gt(cc(5), cc(14), cc(15), ALU.subtract)
        n *= 2
    gt(s1[:, :], CT[:, :], CT[:, :], ALU.mult)
    gt(s2[:, :], ST[:, :], ST[:, :], ALU.mult)
    gt(inv[:, :], s1[:, :], s2[:, :], ALU.add)
    G.do(nc.gpsimd.tensor_scalar, inv[:, :], inv[:, :], -1.0, 2.0, ALU.mult, ALU.add, after=[G.last()])


def delta(g, w, tables):
    nc, p, V, A, T, G = g.nc, g.p, g.V, g.A, g.T, g.G
    with ExitStack() as mem:
        sb = lambda n, s, d=F32: mem.enter_context(nc.sbuf_tensor(f"{n}{g.uid()}", s, d))
        blk = lambda b: slice(b * 512, (b + 1) * 512)
        npT = sb("normed_p20", [128, N])
        swap = sb("swap", [128, 128])
        ones = sb("ones", [128, 128])
        bd = sb("head_ones", [128, HEADS, HD])
        selk = sb("key_select", [128, HD, HEADS, HD])
        z = G.do(nc.gpsimd.memset, swap[:, :], 0.0)
        v = swap[:, :].rearrange("p (m r) -> p m r", r=2)
        z = G.do(nc.gpsimd.affine_select, out=v[:, :, 0], in_=v[:, :, 0], compare_op=ALU.not_equal, fill=1.0, base=-1, pattern=[[-2, 64]], channel_multiplier=1, after=[z])
        z = G.do(nc.gpsimd.affine_select, out=v[:, :, 1], in_=v[:, :, 1], compare_op=ALU.not_equal, fill=-1.0, base=0, pattern=[[-2, 64]], channel_multiplier=1, after=[z])
        G.do(nc.gpsimd.memset, ones[:, :], 1.0)
        z = G.do(nc.gpsimd.memset, bd[:, :, :], 1.0)
        z = G.do(nc.gpsimd.affine_select, out=bd[:, :, :], in_=bd[:, :, :], compare_op=ALU.is_ge, fill=0.0, base=0, pattern=[[-HD, HEADS], [0, HD]], channel_multiplier=1, after=[z])
        z = G.do(nc.gpsimd.affine_select, out=bd[:, :, :], in_=bd[:, :, :], compare_op=ALU.is_ge, fill=0.0, base=HD - 1, pattern=[[HD, HEADS], [0, HD]], channel_multiplier=-1, after=[z])
        z = G.do(nc.gpsimd.memset, selk[:, :, :, :], 0.0)
        for k in range(HD):
            G.do(nc.gpsimd.affine_select, out=selk[:, k, :, :], in_=selk[:, k, :, :], compare_op=ALU.not_equal, fill=1.0, base=-k, pattern=[[-HD, HEADS], [0, HD]],
                 channel_multiplier=1, after=[z])
        made = G.last()

        q, k, bv = sb("queries", [128, N]), sb("keys", [128, N]), sb("beta_values", [128, N])
        dec, nb = sb("decay", [128, N]), sb("neg_beta_decay", [128, N])
        gt = sb("gate", [128, NT, D])
        ramp = sb("ramp", [128, 1])
        with ExitStack() as early:
            sbe = lambda n, s, d=F32: early.enter_context(nc.sbuf_tensor(f"{n}{g.uid()}", s, d))
            CT, ST, inv, r = tables
            x1, x2 = sbe("p20_a", [128, N]), sbe("p20_b", [128, N])
            pads = [sbe(f"conv_in{i}", [128, TAPS - 1 + N]) for i in range(3)]
            free = [None] * 8

            def turned(src, after):
                for b in range(NB):
                    T.do(nc.tensor.matmul, g.ps[b], swap[:, :], src[:, blk(b)], start=True, stop=True, after=[made, free[b]] + after)
                    yield T.last()

            def sine_part(marks, after):
                for b, mm in enumerate(marks):
                    free[b] = V.do(nc.vector.tensor_tensor, x2[:, blk(b)], ST[:, blk(b)], g.ps[b], ALU.mult, after=[mm] + after)
                return free[NB - 1]

            def projection(i):
                z = V.do(nc.vector.memset, pads[i][:, 0:TAPS - 1], 0.0)
                for b in range(NB):
                    c = 4 + b
                    mm = T.do(nc.tensor.matmul, g.ps[c], w["ctrl"][:, i * 128:(i + 1) * 128], g.xnT[:, blk(b)], start=True, stop=True, after=[free[c]])
                    free[c] = A.do(nc.scalar.activation, pads[i][:, TAPS - 1 + b * 512:TAPS - 1 + (b + 1) * 512], g.ps[c], ACT.Identity,
                                   bias=w["ctrl_b"][:, i:i + 1], after=[mm])
                return [free[7], z]

            def convolve(i, dst, m):
                m = V.do(nc.vector.tensor_scalar, dst[:, :], pads[i][:, 0:N], w["convs"][:, i, 0:1], None, ALU.mult, after=m)
                for c in range(1, TAPS):
                    m = V.do(nc.vector.scalar_tensor_tensor, dst[:, :], pads[i][:, c:c + N], w["convs"][:, i, c:c + 1], dst[:, :], ALU.mult, ALU.add, after=[m])
                return m

            marks = list(turned(g.xnT, []))
            zc = G.do(nc.gpsimd.tensor_tensor, npT[:, :], g.xnT[:, :], CT[:, :], ALU.mult, after=[made])
            projected = [projection(i) for i in range(3)]
            zs = sine_part(marks, [])
            cv = convolve(0, q, projected[0])
            m = V.do(nc.vector.tensor_tensor, npT[:, :], npT[:, :], x2[:, :], ALU.add, after=[zs, zc])
            m = V.do(nc.vector.tensor_tensor, x1[:, :], npT[:, :], inv[:, :], ALU.mult, after=[m])
            scan = V.do(nc.vector.tensor_tensor_scan, inv[:, :], r.broadcast_to([128, N]), x1[:, :], 0.0, ALU.mult, ALU.add, after=[m])
            marks = list(turned(inv, [scan]))
            yc = G.do(nc.gpsimd.tensor_tensor, CT[:, :], CT[:, :], inv[:, :], ALU.mult, after=[scan])
            nc.scalar.preload_act_table(ACT.Silu)
            silud = [A.do(nc.scalar.activation, q[:, :], q[:, :], ACT.Silu, after=[cv])]
            cv = convolve(1, k, projected[1])
            silud.append(A.do(nc.scalar.activation, k[:, :], k[:, :], ACT.Silu, after=[cv]))
            m = sine_part(marks, [])
            y = V.do(nc.vector.tensor_tensor, x1[:, :], CT[:, :], x2[:, :], ALU.subtract, after=[yc, m])
            cv = convolve(2, bv, projected[2])
            sq = G.do(nc.gpsimd.tensor_tensor, x2[:, :], x1[:, :], x1[:, :], ALU.mult, after=[y])
            silud.append(A.do(nc.scalar.activation, bv[:, :], bv[:, :], ACT.Silu, after=[cv]))
            nc.scalar.preload_act_table(ACT.Sigmoid)
            rm = A.do(nc.scalar.activation, ramp[:, :], w["ramp_logit"], ACT.Sigmoid)
            for i, dst in ((0, dec), (1, nb)):
                for b in range(NB):
                    c = 4 + b
                    mm = T.do(nc.tensor.matmul, g.ps[c], w["dec_beta"][:, i * 128:(i + 1) * 128], g.xnT[:, blk(b)], start=True, stop=True, after=[free[c]])
                    free[c] = A.do(nc.scalar.activation, dst[:, blk(b)], g.ps[c], ACT.Sigmoid, bias=w["ctrl_b"][:, 3 + i:4 + i], after=[mm])
            sig = A.last()
            for b in range(NB):
                for c in range(4):
                    t = 4 * b + c
                    o = g.ps[b][:, c * 128:(c + 1) * 128]
                    T.do(nc.tensor.matmul, o, g.xnT[:, t * 128:(t + 1) * 128], w["ctrl"][:, 384:512], start=True, stop=False, after=[free[b]])
                    mm = T.do(nc.tensor.matmul, o, g.ones_row[:, 0:128], w["gate_b"], start=False, stop=True)
                free[b] = A.do(nc.scalar.activation, gt[:, 4 * b:4 * b + 4, :].rearrange("p t d -> p (t d)"), g.ps[b], ACT.Sigmoid, after=[mm])
            nc.scalar.preload_act_table_set("natural_log_exp_and_others")
            for b in range(NB):
                c = 4 + b
                mm = T.do(nc.tensor.matmul, g.ps[c], ones[:, :], x2[:, blk(b)], start=True, stop=True, after=[sq, free[c]])
                m = A.do(nc.scalar.activation, CT[:, blk(b)], g.ps[c], ACT.Ln, bias=g.eps_rms[:, :], scale=1.0 / D, after=[mm, y])
                free[c] = m
                m = A.do(nc.scalar.activation, CT[:, blk(b)], CT[:, blk(b)], ACT.Exp, scale=-0.5, after=[m])
                npd = V.do(nc.vector.scalar_tensor_tensor, npT[:, blk(b)], x1[:, blk(b)], w["vnorm"], CT[:, blk(b)], ALU.mult, ALU.mult, after=[m, scan])
            n = 0
            for i, dst in enumerate((q, k, bv)):
                for b in range(NB):
                    c = n % 8
                    n += 1
                    mm = T.do(nc.tensor.matmul, g.ps[c], w["p20c"][:, i * 128:(i + 1) * 128], npT[:, blk(b)], start=True, stop=True, after=[npd, free[c]])
                    m = free[c] = V.do(nc.vector.scalar_tensor_tensor, dst[:, blk(b)], g.ps[c], ramp[:, :], dst[:, blk(b)], ALU.mult, ALU.add, after=[mm, silud[i], rm])
                if i < 2:
                    squares, norm = ((x2, pads[0]), (x1, pads[1]))[i]
                    s = A.do(nc.scalar.activation, squares[:, :], dst[:, :], ACT.Square, after=[m, npd, T.last()])
                    for b in range(NB):
                        c = n % 8
                        n += 1
                        mm = T.do(nc.tensor.matmul, g.ps[c], bd[:, :, :].rearrange("p h d -> p (h d)"), squares[:, blk(b)], start=True, stop=True, after=[s, free[c]])
                        a = free[c] = A.do(nc.scalar.activation, norm[:, blk(b)], g.ps[c], ACT.Ln, bias=g.eps_rms[:, :], after=[mm, cv])
                    a = A.do(nc.scalar.activation, norm[:, 0:N], norm[:, 0:N], ACT.Exp, scale=-0.5, after=[a])
                    unit = G.do(nc.gpsimd.tensor_tensor, dst[:, :], dst[:, :], norm[:, 0:N], ALU.mult, after=[a])
            m = V.do(nc.vector.tensor_tensor, bv[:, :], bv[:, :], nb[:, :], ALU.mult, after=[m, sig])
            m = V.do(nc.vector.scalar_tensor_tensor, nb[:, :], nb[:, :], -1.0, dec[:, :], ALU.mult, ALU.mult, after=[m])
            kn = nb
            V.do(nc.vector.tensor_tensor, kn[:, :], nb[:, :], k[:, :], ALU.mult, after=[m, unit])
            p.join()

        KB = [sb(f"keys_spread{i}", [128, GRP, SEG, HD]) for i in range(2)]
        QB = [sb(f"queries_spread{i}", [128, GRP, SEG, HD]) for i in range(2)]
        KN = [sb(f"keys_scaled{i}", [128, GRP, SEG, HD + 1]) for i in range(2)]
        S = [sb(f"state{i}", [128, 2, SEG, HD + 1]) for i in range(2)]
        SD = sb("state_decayed", [128, 2, SEG, HD])
        M, X = sb("state_keys", [128, 2, SEG, HD + 1]), sb("update", [128, 2, SEG, HD])
        MQ = [sb(f"state_queries{i}", [128, 2, SEG, HD]) for i in range(2)]
        pr = sb("predicted", [128, 2, SEG])
        ou = sb("outs", [128, 2, N])
        seg = lambda ap: ap.rearrange("p (g s) -> p g s", s=STEPS)
        for i in range(2):
            z = G.do(nc.gpsimd.memset, S[i][:, :, :, :], 0.0)
            z = G.do(nc.gpsimd.memset, S[i][:, 0, :, HD:HD + 1], 1.0, after=[z])
        z = V.do(nc.vector.tensor_reduce, pr[:, 0, 0:HD], selk[:, :, :, 0], AX.X, ALU.add, after=[z])
        z = V.do(nc.vector.tensor_copy, S[1][:, 1, :, 0:HD], pr[:, 0, 0:HD].unsqueeze(1).broadcast_to([128, SEG, HD]), after=[z])
        st = dict(bank=[None] * 6, kb=[None, None], use=[None, None], S=None, X=None, MQ=[None, None], summed=[None, None], outs=[None, None])
        held = []

        def spread(i, s0):
            n = 0
            st["kb"][i] = A.do(nc.scalar.copy, KN[i][:, :, :, HD], seg(bv[:, :])[:, :, bass.ds(s0, GRP)].rearrange("p g s -> p s g"), after=[st["use"][i]])
            for src, dst in ((kn, KN[i]), (k, KB[i]), (q, QB[i])):
                cols = seg(src[:, :])[:, :, bass.ds(s0, GRP)].rearrange("p g s -> p s g")
                for kk in range(HD):
                    b = n % 6
                    n += 1
                    o = g.ps[b][:, 0:GRP * SEG]
                    mm = T.do(nc.tensor.matmul, o, selk[:, kk, :, :].rearrange("p h v -> p (h v)"), cols, start=True, stop=True, after=[st["bank"][b]])
                    st["bank"][b] = A.do(nc.scalar.copy, dst[:, :, :, kk], o.rearrange("p (s g) -> p s g", s=GRP), after=[mm, st["use"][i]])
                    st["kb"][i] = st["bank"][b]
                    yield

        def outputs():
            if not held:
                return
            i, j, s0 = held.pop()
            a = j % 2
            m = st["MQ"][a] = st["use"][i] = G.do(nc.gpsimd.tensor_tensor, MQ[a][:, :, :, :], S[a][:, :, :, 0:HD], kinds(QB[i][:, j, :, :]), ALU.mult,
                                                  after=[st["S"], st["summed"][a]])
            bank = g.ps[6 + i].rearrange("p (j x g) -> p j x g", j=GRP, x=2)
            for kk in range(HD):
                m2 = T.do(nc.tensor.matmul, bank[:, j, :, :], g.ident[:, :], MQ[a][:, :, :, kk], start=(kk == 0), stop=(kk == HD - 1),
                          after=[m, st["outs"][i]], skip_group_check=True)
            st["summed"][a] = m2
            if j == GRP - 1:
                for x in range(2):
                    o = ou[:, x, :].rearrange("p (g s) -> p g s", s=STEPS)[:, :, bass.ds(s0, GRP)]
                    st["outs"][i] = A.do(nc.scalar.copy, o, bank[:, :, x, :].rearrange("p j g -> p g j"), after=[m2])

        kinds = lambda ap: ap.unsqueeze(1).broadcast_to([128, 2] + list(ap.shape[1:]))

        def step(i, j, s0):
            s = s0 + j
            a, b = j % 2, 1 - j % 2
            m = V.do(nc.vector.tensor_tensor, M[:, :, :, :], S[b][:, :, :, :], kinds(KN[i][:, j, :, :]), ALU.mult, after=[st["S"], st["kb"][i]])
            decay = seg(dec[:, :])[:, :, bass.ds(s, 1)].rearrange("p g o -> p (g o)").unsqueeze(1).unsqueeze(3).broadcast_to([128, 2, SEG, HD])
            d = G.do(nc.gpsimd.tensor_tensor, SD[:, :, :, :], S[b][:, :, :, 0:HD], decay, ALU.mult,
                     after=[st["S"]])
            outputs()
            m = V.do(nc.vector.tensor_reduce, pr[:, :, :], M[:, :, :, :], AX.X, ALU.add, after=[m])
            m = st["X"] = V.do(nc.vector.tensor_tensor, X[:, :, :, :], pr[:, :, :].unsqueeze(3).broadcast_to([128, 2, SEG, HD]),
                               kinds(KB[i][:, j, :, :]), ALU.mult, after=[m])
            st["S"] = V.do(nc.vector.tensor_tensor, S[a][:, :, :, 0:HD], SD[:, :, :, :], X[:, :, :, :], ALU.add, after=[m, d, st["MQ"][a]])
            held.append((i, j, s0))

        for _ in spread(0, 0):
            pass

        def groups(s0, more):
            nxt = spread(1, s0 + GRP)
            for i in range(2):
                for j in range(GRP):
                    step(i, j, s0 + GRP * i)
                    for _ in range(SPREADS):
                        next(nxt, None)
                if i == 0 and more:
                    nxt = spread(0, s0 + 2 * GRP)
            outputs()
        p.pipeline(STEPS // (2 * GRP) - 1, lambda i: groups(i * 2 * GRP, True), st)
        groups(STEPS - 2 * GRP, False)
        p.join()

        fin = S[1][:, :, :, 0:HD]
        diagonal = lambda pair, n: pair[n // 16][:, :, :, :].rearrange("p a b c -> p (a b c)")[:, (n % 16) * 128:(n % 16 + 1) * 128]
        spread_out = []
        for n in range(SEG - 1):
            two_ends = []
            for eng, f, kind, pair in ((V, nc.vector, 1, KB), (G, nc.gpsimd, 0, QB)):
                out = diagonal(pair, n).rearrange("p (h k) -> p h k", h=HEADS)
                two_ends.append((eng, f.tensor_tensor, out, fin[:, kind, n, :].unsqueeze(1).broadcast_to([128, HEADS, HD]), bd[:, :, :], ALU.mult))
            spread_out.append(two_ends)

        def build(n):
            return [eng.do(*rest) for eng, *rest in spread_out[n]] if n < SEG - 1 else None

        o_, t1, t2 = ou[:, 0, :], ou[:, 1, :], q
        scale = float(HD) ** -0.5
        mn = V.do(nc.vector.tensor_scalar, ramp[:, :], w["mnorm"], scale, None, ALU.mult)
        free = {2: None, 3: None}

        def finish(b, cm):
            m = V.do(nc.vector.tensor_tensor, o_[:, blk(b)], o_[:, blk(b)], g.ps[4 + b], ALU.add, after=[cm])
            yield
            s = A.do(nc.scalar.activation, t1[:, blk(b)], o_[:, blk(b)], ACT.Square, scale=scale, after=[m, cm])
            yield
            mm = T.do(nc.tensor.matmul, g.ps[2], bd[:, :, :].rearrange("p h d -> p (h d)"), t1[:, blk(b)], start=True, stop=True, after=[s, free[2]])
            a = free[2] = A.do(nc.scalar.activation, t2[:, blk(b)], g.ps[2], ACT.Ln, bias=g.eps_rms[:, :], scale=1.0 / HD, after=[mm])
            a = A.do(nc.scalar.activation, t2[:, blk(b)], t2[:, blk(b)], ACT.Exp, scale=-0.5, after=[a])
            yield
            m = V.do(nc.vector.scalar_tensor_tensor, o_[:, blk(b)], o_[:, blk(b)], ramp[:, :], t2[:, blk(b)], ALU.mult, ALU.mult, after=[a, m, mn])
            yield
            for c in range(4):
                t = 4 * b + c
                o = g.ps[3][:, c * 128:(c + 1) * 128]
                ts = slice(t * 128, (t + 1) * 128)
                T.do(nc.tensor.matmul, o, o_[:, ts], w["out"][:, 0, :], start=True, stop=False, after=[m, free[3]])
                T.do(nc.tensor.matmul, o, npT[:, ts], w["out"][:, 1, :], start=False, stop=False)
                mm = T.do(nc.tensor.matmul, o, g.ones_row[:, 0:128], w["out_b"], start=False, stop=True)
                if c % 2:
                    yield
            ge = gt[:, 4 * b:4 * b + 4, :]
            xx = g.x_tok[:, 4 * b:4 * b + 4, :]
            m = free[3] = V.do(nc.vector.tensor_tensor, ge, ge, g.ps[3].rearrange("p (t f) -> p t f", t=4), ALU.mult, after=[mm])
            G.do(nc.gpsimd.tensor_tensor, xx, xx, ge, ALU.add, after=[m])
            yield

        S0 = [sb(f"start_state{i}", [128, 128]) for i in range(2)]
        z = V.do(nc.vector.memset, S0[0][:, :], 0.0)
        cor, finishing = None, []
        ends = {n: build(n) for n in range(3)}
        for n in range(SEG):
            cur, nx = S0[n % 2], S0[(n + 1) % 2]
            ends[n + 3] = build(n + 3)
            if n + 1 < SEG:
                bank = g.ps[n % 2][:, 0:128]
                T.do(nc.tensor.matmul, bank, diagonal(QB, n), g.ident[:, :], start=True, stop=False, after=ends[n] + [z])
                mm = T.do(nc.tensor.matmul, bank, diagonal(KB, n), cur[:, :], start=False, stop=True, after=[z])
            ob = g.ps[4 + n // 8][:, (n % 8) * STEPS:(n % 8 + 1) * STEPS]
            cm = T.do(nc.tensor.matmul, ob, cur[:, :], ou[:, 1, n * STEPS:(n + 1) * STEPS], start=True, stop=True, after=[z])
            if n + 1 < SEG:
                z = V.do(nc.vector.tensor_copy, nx[:, :], bank, after=[mm, cor])
            cor = cm
            for block in finishing:
                next(block, None)
            if n % 8 == 7:
                finishing.append(finish(n // 8, cm))
        for block in finishing:
            for _ in block:
                pass
        p.join()


ATTN_COLS = (("wqT", 128), ("wkT", 128), ("wvT", 128), ("woT", 128), ("bq", 1), ("bk", 1))
GLA_COLS = (("Wp", 3 * KD), ("Wa", 224), ("Wb", KD), ("Wc", KD), ("Wo", KD), ("We", NEXP), ("norm", DK))
MAMBA_COLS = (("in_proj", 512), ("x_proj", 80), ("out_proj", 256), ("dt_w", 256), ("conv_w", 8), ("conv_b", 2),
              ("dt_b", 2), ("A_log", 32), ("Dp", 2))
MOE_COLS = (("w1", UNITS * 128), ("w3", UNITS * 128), ("w2", UNITS * 128), ("gate", EXPERTS), ("gate_bias", EXPERTS))
DELTA_COLS = (("ctrl", 512), ("dec_beta", 256), ("ctrl_b", 5), ("p20c", 384), ("convs", 12), ("out", 256),
              ("theta", 1), ("decay_log", 1), ("ramp_logit", 1), ("vnorm", 1), ("mnorm", 1))
BLOCKS = {"x_proj": 2, "out_proj": 2, "conv_w": 2, "A_log": 2, "w1": UNITS, "w3": UNITS, "w2": UNITS, "convs": 3, "out": 2}
ROW_PAIRS = 3


def width(cols):
    return sum(k for _, k in cols)


def views(sbuf, cols):
    out, at = {}, 0
    for name, k in cols:
        v = sbuf[:, at:at + k]
        out[name] = v.rearrange("p (i c) -> p i c", i=BLOCKS[name]) if name in BLOCKS else v
        at += k
    return out


class Context:
    pass


def build(nc):
    dram = lambda n, s: nc.dram_tensor(n, s, F32, kind="ExternalInput").ap()
    x = dram("x", (N, D))
    src = {n: dram(n, (128, width(c))) for n, c in
           (("attn_a", ATTN_COLS), ("attn_b", ATTN_COLS), ("gla", GLA_COLS), ("mamba", MAMBA_COLS), ("moe", MOE_COLS), ("delta", DELTA_COLS))}
    row_src = dram("row_biases", (ROW_PAIRS, 2 * D))
    out = nc.dram_tensor("out", (1, N, D), F32, kind="ExternalOutput").ap()

    g = Context()
    g.nc, g.p = nc, Program(nc)
    p = g.p
    g.V, g.A, g.T, g.G = p.stream(nc.vector, "vec"), p.stream(nc.scalar, "act"), p.stream(nc.tensor, "pe"), p.stream(nc.gpsimd, "pool")
    g.L, g.Lsc2 = p.stream(nc.sync, "load", 16), p.stream(nc.sync, "scratch_2", 16)
    names = []

    def uid():
        names.append(None)
        return f"_{len(names)}"

    g.uid = uid
    keep = lambda n, s, d=F32: nc.alloc_sbuf_tensor(n, s, d)
    g.x_tok, g.xnT = keep("x_tok", [128, NT, D]), keep("xnT", [128, N])
    g.ident, g.tri, g.cum = keep("ident", [128, 128]), keep("tri", [128, 128]), keep("cum", [128, 128])
    g.half_col, g.eps_ln, g.eps_rms = keep("half_col", [128, 2]), keep("eps_ln", [128, 1]), keep("eps_rms", [128, 1])
    g.ones_row, rows = keep("ones_row", [1, 128]), keep("row_biases_sb", [1, 2 * D])
    rotation, given = keep("rotation_columns", [128, 16]), keep("theta_decay", [128, 2])
    mixer_w = keep("mixer_weights", [128, max(width(c) for c in (ATTN_COLS, MAMBA_COLS, DELTA_COLS))])
    ffn_w = keep("ffn_weights", [128, max(width(GLA_COLS), width(MOE_COLS))])
    whole = nc.alloc_psum_tensor("banks", [128, 8 * 512], F32)
    g.ps = [whole[:, i * 512:(i + 1) * 512] for i in range(8)]
    g.wide = lambda i: whole[:, i * 512:(i + 2) * 512]
    g.q_scratch = nc.dram_tensor("q_scratch", (PARTS, 128, N), BF16, kind="Internal").ap()
    g.k_scratch = nc.dram_tensor("k_scratch", (PARTS, 128, N), BF16, kind="Internal").ap()

    def load(sbuf, name):
        a = src[name]
        return g.L.do(nc.sync.dma_start, sbuf[:, 0:a.shape[1]], a)

    def load_rows(k):
        return g.L.do(nc.sync.dma_start, rows[:, :], row_src[k:k + 1, :])

    for b in range(NB):
        xb = g.L.do(nc.sync.dma_start, g.x_tok[:, 4 * b:4 * b + 4, :], x[b * 512:(b + 1) * 512, :].rearrange("(t p) d -> p t d", p=128))
    at = sum(k for _, k in DELTA_COLS[:[n for n, _ in DELTA_COLS].index("theta")])
    g.L.do(nc.sync.dma_start, given[:, :], src["delta"][:, at:at + 2])
    load(mixer_w, "attn_a")
    load_rows(0)
    first = g.L.last()
    ffn_loads = p.stream(nc.sync, "load_gla", 16)
    ffn_loads.do(nc.sync.dma_start, ffn_w[:, 0:width(GLA_COLS)], src["gla"])

    G = g.G
    m = G.do(nc.gpsimd.memset, g.ident[:, :], 0.0)
    G.do(nc.gpsimd.affine_select, out=g.ident[:, :], in_=g.ident[:, :], compare_op=ALU.not_equal, fill=1.0, base=0,
         pattern=[[-1, 128]], channel_multiplier=1, after=[m])
    G.do(nc.gpsimd.memset, g.ones_row[:, :], 1.0)
    G.do(nc.gpsimd.memset, g.eps_ln[:, :], EPS_LN)
    G.do(nc.gpsimd.memset, g.eps_rms[:, :], EPS_R)
    m = G.do(nc.gpsimd.memset, g.tri[:, :], 1.0)
    m = G.do(nc.gpsimd.affine_select, out=g.tri[:, :], in_=g.tri[:, :], compare_op=ALU.is_ge, fill=0.0, base=0,
             pattern=[[1, 128]], channel_multiplier=-1, after=[m])
    m = G.do(nc.gpsimd.memset, g.half_col[:, :], 1.0)
    m = G.do(nc.gpsimd.affine_select, out=g.half_col[:, 0:1], in_=g.half_col[:, 0:1], compare_op=ALU.is_ge, fill=0.0,
             base=63, pattern=[[0, 1]], channel_multiplier=-1, after=[m])
    m = G.do(nc.gpsimd.affine_select, out=g.half_col[:, 1:2], in_=g.half_col[:, 1:2], compare_op=ALU.is_ge, fill=0.0,
             base=-64, pattern=[[0, 1]], channel_multiplier=1, after=[m])
    g.V.do(nc.vector.tensor_scalar, g.cum[:, :], g.tri[:, :], g.half_col[:, 0:1], None, ALU.subtract, after=[m])
    nc.scalar.preload_act_table_set("natural_log_exp_and_others")

    row_1, row_2 = rows[:, 0:D], rows[:, D:2 * D]
    for e in (nc.tensor, nc.vector, nc.scalar, nc.gpsimd):
        p.wait(e, [first, G.last(), g.V.last()])
    rotation_columns(g, given[:, 0:1], given[:, 1:2], rotation)
    layer_norm_T(g)
    attention(g, dict(views(mixer_w, ATTN_COLS), bv=row_1, bo=row_2), "a")
    load(mixer_w, "attn_b")
    load_rows(1)
    layer_norm_T(g)
    gla_ffn(g, views(ffn_w, GLA_COLS), "f1")
    layer_norm_T(g)
    attention(g, dict(views(mixer_w, ATTN_COLS), bv=row_1, bo=row_2), "b")
    load(mixer_w, "mamba")
    load_rows(2)
    layer_norm_T(g)
    gla_ffn(g, views(ffn_w, GLA_COLS), "f2")
    load(ffn_w, "moe")
    layer_norm_T(g)
    mamba(g, views(mixer_w, MAMBA_COLS), "m")
    load(mixer_w, "delta")
    with ExitStack() as mem:
        tables = [mem.enter_context(nc.sbuf_tensor(f"{n}_table", [128, N], F32)) for n in ("cosine", "sine", "inverse")]
        with ExitStack() as scratch:
            beside = [scratch.enter_context(nc.sbuf_tensor(f"table_scratch{i}", [128, N], F32)) for i in range(2)]
            layer_norm_T(g)
            moe(g, views(ffn_w, MOE_COLS), lambda: rotation_tables(g, rotation, *tables, *beside))
            p.join()
        layer_norm_T(g)
        delta(g, dict(views(mixer_w, DELTA_COLS), gate_b=row_1, out_b=row_2), (*tables, rotation[:, 7:8]))
    layer_norm_T(g)
    moe(g, views(ffn_w, MOE_COLS))
    stored = g.L.do(nc.sync.dma_start, out[0].rearrange("(t p) d -> p t d", p=128), g.x_tok[:, :, :])
    p.wait(nc.sync, [stored])


def kernel(**a):
    import concourse.bacc as _bacc
    import numpy as np
    from concourse.bass_utils import run_bass_kernel_spmd as _run

    a = {k: np.asarray(v) for k, v in a.items()}
    w, b = a["L0_attn_a_qkv_w"], a["L0_attn_a_qkv_b"]
    attn_a = np.concatenate([w[0:128].T, w[128:256].T, w[256:384].T, a["L0_attn_a_out_w"].T, b[0:128, None], b[128:256, None]], 1)
    rows = [b[256:384], a["L0_attn_a_out_b"]]
    f = lambda n: a["L0_attn_b_" + n]
    kv_heads = f("wk").shape[0] // HD
    grp = HEADS // kv_heads
    again = lambda v: np.repeat(v.reshape((kv_heads, HD) + v.shape[1:]), grp, 0).reshape((HEADS * HD,) + v.shape[1:])
    attn_b = np.concatenate([f("wq").T, again(f("wk")).T, again(f("wv")).T, f("wo").T, f("bq")[:, None],
                             again(f("bk"))[:, None]], 1)
    rows += [again(f("bv")), f("bo")]
    f = lambda n: a["L0_ffn_" + n]
    blocks = lambda v: v.reshape(v.shape[0] // 128, 128, -1).transpose(1, 0, 2).reshape(128, -1)
    wc = np.zeros((128, f("Wgb").shape[1]), np.float32)
    wc[0:64], wc[64:80], wc[80], wc[96:112], wc[112] = f("Wgb"), f("Wg1b"), f("bg1"), f("Wg2b"), f("bg2")
    gla = np.concatenate([f("Wq"), f("Wk"), f("Wv"), f("Wqa"), f("Wka"), f("Wga"), f("Wg1a"), f("Wg2a"),
                          np.concatenate([f("Wqb"), f("Wkb")], 0), wc, blocks(f("Wo")), f("We"), np.tile(f("norm_w")[None], (128, 1))], 1)
    f = lambda n: a["L1_attn_a_" + n]
    dt_w = np.zeros((128, f("dt_proj_w").shape[1]), np.float32)
    dt_w[0:f("dt_proj_w").shape[0]] = f("dt_proj_w")
    mamba_w = np.concatenate([f("in_proj_w"), blocks(f("x_proj_w")), blocks(f("out_proj_w")), dt_w, blocks(f("conv_w")[:, 0, :]),
                              blocks(f("conv_b")[:, None]), blocks(f("dt_proj_b")[:, None]), blocks(f("A_log")), blocks(f("Dparam")[:, None])], 1)
    f = lambda n: a["L1_ffn_" + n]
    up = lambda r, s: np.concatenate([f(r), f(s).reshape(-1, 128, 128)], 0).transpose(2, 0, 1).reshape(128, -1)
    down = np.concatenate([f("w2").transpose(0, 2, 1), f("sw2").T.reshape(-1, 128, 128)], 0).transpose(1, 0, 2).reshape(128, -1)
    moe_w = np.concatenate([up("w1", "sw1"), up("w3", "sw3"), down, f("gate_w").T, np.tile(f("gate_bias")[None], (128, 1))], 1)
    f = lambda n: a["L1_attn_b_" + n]
    w, b = f("ctrl_W"), f("ctrl_b")
    cols = [b[0:128], b[128:256], b[256:384], np.repeat(b[384:400], HD), np.repeat(b[400:416], HD)]
    delta_w = np.concatenate([w[:, 0:384], w[:, 416:544], np.repeat(w[:, 384:416], HD, 1), np.stack(cols, 1), f("p20c_W"),
                              f("qconv_w"), f("kconv_w"), f("vconv_w"), blocks(f("out_W")), np.repeat(f("p20_theta"), 2)[:, None],
                              np.repeat(f("p20_decay_log"), 2)[:, None], f("ramp_logit")[:, None], f("vnorm_scale")[:, None],
                              np.tile(f("mnorm_scale"), HEADS)[:, None]], 1)
    rows += [b[416:544], f("out_b")]
    inputs = dict(x=a["L0_attn_a_x"][0], attn_a=attn_a, attn_b=attn_b, gla=gla, mamba=mamba_w, moe=moe_w, delta=delta_w,
                  row_biases=np.concatenate(rows).reshape(-1, 256))
    inputs = {k: np.ascontiguousarray(v) for k, v in inputs.items()}
    nc = _bacc.Bacc("TRN2", target_bir_lowering=False, num_devices=1)
    build(nc)
    nc.compile()
    return _run(nc, [inputs], core_ids=[0]).results[0]["out"]
```

```python
import math
from contextlib import ExitStack

import concourse.bass as bass
from concourse import mybir

F32 = mybir.dt.float32
BF16 = mybir.dt.bfloat16
ALU = mybir.AluOpType
ACT = mybir.ActivationFunctionType
AX = mybir.AxisListType

N = 2048
D = 128
NT = N // 128
NB = N // 512
EPS_LN = 1e-5
BIAS = 1024


class Mark:

    def __init__(self, stream, loop, value):
        self.stream, self.loop, self.value = stream, loop, value

    def before(self):
        return Mark(self.stream, self.loop, self.value - self.loop.per[self.stream])


class Loop:
    def __init__(self, times):
        self.times, self.per, self.base, self.index = times, {}, {}, 0


class Stream:

    def __init__(self, prog, engine, sem, step=1):
        self.prog, self.engine, self.sem, self.step, self.count = prog, engine, sem, step, 0
        prog.streams.append(self)

    def do(self, make, *args, after=(), **kw):
        self.prog.wait(self.engine, after)
        if not self.prog.counting:
            make(*args, **kw).then_inc(self.sem, self.step)
        self.count += self.step
        return Mark(self, self.prog.loop, self.count)

    def last(self):
        return Mark(self, self.prog.loop, self.count)


class Program:

    def __init__(self, nc):
        self.nc, self.streams, self.loop, self.counting = nc, [], None, False
        self.waited = {}
        self.held_waits = {id(e): nc.alloc_semaphore(f"held_waits_{n}") for n, e in
                           (("pool", nc.gpsimd), ("sync", nc.sync), ("pe", nc.tensor))}

    def stream(self, engine, name, step=1):
        s = Stream(self, engine, self.nc.alloc_semaphore(name), step)
        engine.sem_inc(s.sem, BIAS)
        s.count = BIAS
        return s

    def value(self, mark):
        loop = mark.loop
        if loop is None:
            return mark.value
        per, base = loop.per.get(mark.stream, 0), loop.base.get(mark.stream, 0)
        if loop is self.loop:
            return base + mark.value + loop.index * per
        return base + (loop.times - 1) * per + mark.value

    def hold(self, engine, marks):
        self.wait(engine, marks, True)

    def wait(self, engine, marks, own=False):
        if self.counting:
            return
        for mark in marks:
            if mark is None:
                continue
            key = (id(engine), id(mark.stream), id(mark.loop if mark.loop is self.loop else None))
            least = mark.value if mark.loop is self.loop else self.value(mark)
            if self.waited.get(key, -10**9) >= least:
                continue
            self.waited[key] = least
            engine.wait_ge(mark.stream.sem, self.value(mark))
            if self.loop is not None and (own or engine in (self.nc.sync, self.nc.gpsimd)):
                engine.sem_inc(self.held_waits[id(engine)], 1)

    def repeat(self, times, body):
        loop = Loop(times)
        at = {s: s.count for s in self.streams}
        for s in self.streams:
            s.count = 0
        outer_loop = self.loop
        assert outer_loop is None
        self.loop, self.counting = loop, True
        for s in self.streams:
            loop.per[s] = 0
        body(0)
        loop.per = {s: s.count for s in self.streams}
        for s in self.streams:
            s.count = 0
        loop.base = at
        self.counting = False
        self.waited = {}
        with self.nc.Fori(0, times) as index:
            loop.index = index
            body(index)
        self.waited = {}
        self.loop = None
        for s in self.streams:
            s.count = at[s] + times * loop.per[s]

    def pipeline(self, times, body, state, leave=()):
        def age(x):
            if isinstance(x, (list, tuple)):
                return [age(y) for y in x]
            return x.before() if x is not None else None

        def blank(x):
            return [blank(y) for y in x] if isinstance(x, (list, tuple)) else None

        ends = {}

        def traced(i):
            if self.counting:
                state.update({k: blank(x) for k, x in state.items()})
            else:
                state.update({k: age(x) for k, x in ends.items()})
            body(i)
            if self.counting:
                ends.update(state)

        self.join(leave)
        self.repeat(times, traced)

    def join(self, leave=()):
        left = [s.engine for s in leave]
        for engine in (self.nc.tensor, self.nc.vector, self.nc.scalar, self.nc.gpsimd, self.nc.sync):
            if engine not in left:
                self.wait(engine, [s.last() for s in self.streams if s not in leave])


HEADS, HD = 16, 8
PARTS = 3
ROWS = PARTS * PARTS * HD
SEAM = 8
LEAD = 16

def layer_norm_T(g):
    nc, V, A, T = g.nc, g.V, g.A, g.T
    with ExitStack() as mem:
        sb = lambda n, s, d=F32: mem.enter_context(nc.sbuf_tensor(f"{n}{g.uid()}", s, d))
        xn = sb("ln_normed", [128, NT, D])
        stats, mv, rstd = sb("ln_stats", [128, NT, 6]), sb("ln_mean_var", [128, NT, 2]), sb("ln_rstd", [128, NT])
        scaled = {}

        def statistics(b):
            for t in range(4 * b, 4 * b + 4):
                V.do(nc.vector.bn_stats, stats[:, t, :], g.x_tok[:, t, :])
            m = V.last()
            for t in range(4 * b, 4 * b + 4):
                v = V.do(nc.vector.bn_aggr, mv[:, t, :], stats[:, t, :], after=[m])
            r = rstd[:, 4 * b:4 * b + 4]
            m = A.do(nc.scalar.activation, r, mv[:, 4 * b:4 * b + 4, 1], ACT.Ln, bias=g.eps_ln[:, :], after=[v])
            scaled[b] = A.do(nc.scalar.activation, r, r, ACT.Exp, scale=-0.5, after=[m])

        def apply(b):
            for c in range(4):
                t = 4 * b + c
                m = V.do(nc.vector.tensor_scalar, xn[:, t, :], g.x_tok[:, t, :], mv[:, t, 0:1], rstd[:, t:t + 1], ALU.subtract, ALU.mult, after=[scaled[b]])
                tr = T.do(nc.tensor.transpose, g.ps[b][:, c * 128:(c + 1) * 128], xn[:, t, :], g.ident[:, :], after=[m])
            A.do(nc.scalar.copy, g.xnT[:, b * 512:(b + 1) * 512], g.ps[b][:, :], after=[tr])

        statistics(0)
        for b in range(1, NB):
            statistics(b)
            apply(b - 1)
        apply(NB - 1)
        g.p.join()

def attention(g, w, tag):
    nc, p, V, A, T, G = g.nc, g.p, g.V, g.A, g.T, g.G
    with ExitStack() as mem:
        sb = lambda n, s, d=F32: mem.enter_context(nc.sbuf_tensor(f"{n}{g.uid()}", s, d))
        Q1 = [sb(f"q_max{i}", [ROWS, N], BF16) for i in range(2)]
        K1 = [sb(f"k_max{i}", [ROWS, N], BF16) for i in range(2)]
        Q2 = [sb(f"q_exp{i}", [ROWS + PARTS, N], BF16) for i in range(2)]
        K2 = [sb(f"k_exp{i}", [ROWS + PARTS, N], BF16) for i in range(2)]
        Vs = [sb(f"v_head{i}", [128, NT, 32]) for i in range(2)]
        v_tok = sb("v_tok", [128, NT, HEADS, HD])
        o_tok = sb("o_tok", [128, NT, HEADS, HD])
        PT = sb("probs", [128, 8, 512])
        mxp = [sb(f"max_parts{i}", [128, 64]) for i in range(2)]
        nmx = sb("neg_max", [128, NT])
        nhi = sb("neg_max_hi", [NT, PARTS, 128], BF16)
        nres = sb("neg_max_rest", [NT, 2, 128])
        osb = sb("pv_copy", [128, 512])
        rec = sb("recip_sums", [128, 4, 4])
        Ld1 = [p.stream(nc.sync, f"{tag}_load_max{i}", 16) for i in range(2)]
        Ld2 = [p.stream(nc.sync, f"{tag}_load_exp{i}", 16) for i in range(2)]
        Lmx = [p.stream(nc.sync, f"{tag}_load_negmax{i}", 16) for i in range(2)]
        Lsc = p.stream(nc.sync, f"{tag}_scratch", 16)
        S1b, S2b, PVb, misc = g.ps[0:3], g.ps[3:6], g.ps[6], g.ps[7]
        qs, ks = g.q_scratch, g.k_scratch

        part = sb("qk_parts", [128, 2, PARTS, 512], BF16)
        full = sb("qk_full", [128, 2, 512])
        rest = sb("qk_rest", [128, 2, 512])
        sent = [None, None]
        unit = 0
        evac = {}
        for wT, bias, dst in ((w["wqT"], w["bq"], qs), (w["wkT"], w["bk"], ks)):
            for b in range(NB):
                k = unit % 2
                mm = T.do(nc.tensor.matmul, g.ps[k][:, :], wT, g.xnT[:, b * 512:(b + 1) * 512], start=True, stop=True,
                          after=[evac.get(k)])
                f = evac[k] = V.do(nc.vector.tensor_scalar, full[:, k, :], g.ps[k][:, :], bias, None, ALU.add, after=[mm, V.last()])
                h = A.do(nc.scalar.copy, part[:, k, 0, :], full[:, k, :], after=[f, sent[k]])
                r = V.do(nc.vector.tensor_tensor, rest[:, k, :], full[:, k, :], part[:, k, 0, :], ALU.subtract, after=[h])
                h2 = A.do(nc.scalar.copy, part[:, k, 1, :], rest[:, k, :], after=[r])
                lo = V.do(nc.vector.tensor_tensor, part[:, k, 2, :], rest[:, k, :], part[:, k, 1, :], ALU.subtract, after=[h2, sent[k]])
                s = Lsc if k == 0 else g.Lsc2
                sent[k] = s.do(nc.sync.dma_start, dst[:, :, b * 512:(b + 1) * 512].rearrange("a p n -> p a n"), part[:, k, :, :], after=[lo])
                unit += 1
        for t in range(NT):
            bank = g.ps[2 + t // 4]
            o = bank[:, (t % 4) * 128:(t % 4) * 128 + 128]
            T.do(nc.tensor.matmul, o, g.xnT[:, t * 128:(t + 1) * 128], w["wvT"], start=True, stop=False)
            mm = T.do(nc.tensor.matmul, o, g.ones_row[:, 0:128], w["bv"], start=False, stop=True)
            if t % 4 == 3:
                A.do(nc.scalar.copy, v_tok[:, t - 3:t + 1, :, :], bank[:, :].rearrange("p (t h d) -> p t h d", t=4, h=HEADS), after=[mm])
        v_ready = A.last()
        ini = []
        for i in range(2):
            ini.append(G.do(nc.gpsimd.memset, Vs[i][:, :, :], 0.0))
            ini.append(G.do(nc.gpsimd.memset, Q2[i][:, :], 1.0))
            ini.append(G.do(nc.gpsimd.memset, K2[i][:, :], 1.0))
        for i in range(2):
            G.do(nc.gpsimd.memset, Vs[i][:, :, HD:HD + 1], 1.0, after=[ini[-1]])
        inited = G.last()

        def load(stream, Q, K, h, after):
            for a in range(PARTS):
                r = slice(a * PARTS * HD, (a + 1) * PARTS * HD)
                stream.do(nc.sync.dma_start, Q[r, :], qs[a:a + 1, bass.ts(h, HD), :].broadcast_to([PARTS, HD, N]), after=after)
                d = stream.do(nc.sync.dma_start, K[r, :], ks[:, bass.ts(h, HD), :], after=after)
            return d

        def stage_v(i, h, after):
            return G.do(nc.gpsimd.tensor_copy, Vs[i][:, :, 0:HD], v_tok[:, :, h, :] if isinstance(h, int) else
                        v_tok[:, :, :, :].rearrange("p t h d -> p t (h d)")[:, :, bass.ts(h, HD)], after=after)

        scratch_done = [Lsc.last(), g.Lsc2.last()]
        st = dict(red=[None] * 3, exp=[None] * 3, maxed=None, pv=[None] * 8, evac=None, s1end=[None, None], mxred=[None, None],
                  load1=[None, None], load2=[None, None], vs=[None, None], negmax=[None, None], misc=None,
                  s2end=[None, None], pvend=[None, None], nhi=None, recm=None, tr4=None, probs=[None] * 8)
        slow = []

        def scores_max(par, u, slot):
            t, b = u // 4, u % 4
            mm = T.do(nc.tensor.matmul, S1b[slot][:, :], Q1[par][:, t * 128:(t + 1) * 128], K1[par][:, b * 512:(b + 1) * 512],
                      start=True, stop=True, after=[st["red"][slot], st["load1"][par]])
            st["red"][slot] = V.do(nc.vector.tensor_reduce, mxp[par][:, u:u + 1], S1b[slot][:, :], AX.X, ALU.max,
                                    after=[mm] + ([st["mxred"][par]] if u == 0 else []))
            st["maxed"] = st["red"][slot]
            if u == 63:
                st["s1end"][par] = mm

        def maxima(par):
            m = V.do(nc.vector.tensor_reduce, nmx[:, :], mxp[par][:, :].rearrange("p (t b) -> p t b", b=4), AX.X, ALU.max,
                     negate=True, after=[st["maxed"], st["misc"]])
            st["mxred"][par] = m
            yield
            tr = T.do(nc.tensor.transpose, misc[0:NT, 0:128], nmx[:, :], g.ident[:, :], after=[m, st["recm"]])
            yield
            m = V.do(nc.vector.tensor_copy, nhi[:, 0, :], misc[0:NT, 0:128], after=[tr, st["nhi"]])
            m = V.do(nc.vector.tensor_tensor, nres[:, 0, :], misc[0:NT, 0:128], nhi[:, 0, :], ALU.subtract, after=[m])
            st["misc"] = m
            m = V.do(nc.vector.tensor_copy, nhi[:, 1, :], nres[:, 0, :], after=[m])
            m = V.do(nc.vector.tensor_tensor, nhi[:, 2, :], nres[:, 0, :], nhi[:, 1, :], ALU.subtract, after=[m])
            for r in range(PARTS):
                d = Lmx[par].do(nc.sync.dma_start, Q2[par][ROWS + r:ROWS + r + 1, :], nhi[:, r, :], after=[m, st["s2end"][par], inited])
            st["negmax"][par] = st["nhi"] = d
            yield

        def scores_exp(par, u, slot):
            t, j = u // 4, u % 4
            mm = T.do(nc.tensor.matmul, S2b[slot][:, :], K2[par][:, t * 128:(t + 1) * 128], Q2[par][:, j * 512:(j + 1) * 512],
                      start=True, stop=True, after=[st["exp"][slot], st["load2"][par], st["negmax"][par], inited])
            st["probs"][u % 8] = st["exp"][slot] = A.do(nc.scalar.activation, PT[:, u % 8, :], S2b[slot][:, :], ACT.Exp, scale=float(HD) ** -0.5,
                                    after=[mm, st["pv"][u % 8]])
            if u == 63:
                st["s2end"][par] = mm

        def values(par, u):
            t, j = u // 4, u % 4
            st["pv"][u % 8] = T.do(nc.tensor.matmul, PVb[32 * j:32 * j + 32, :], Vs[par][:, t, :], PT[:, u % 8, :],
                                   start=(t == 0), stop=(t == NT - 1), after=[st["probs"][u % 8], st["evac"], st["vs"][par]])
            if u == 63:
                st["pvend"][par] = st["pv"][u % 8]

        def normalise(par, h):
            e = st["evac"] = A.do(nc.scalar.copy, osb[:, :], PVb[:, :], after=[st["pvend"][par], st["tr4"]])
            yield
            for c in range(4):
                tr = T.do(nc.tensor.transpose, misc[:, c * 128:(c + 1) * 128], osb[:, c * 128:(c + 1) * 128], g.ident[:, :],
                          after=[e, st["misc"], st["recm"]])
            st["tr4"] = tr
            yield
            turned = misc[:, :].rearrange("p (c j r) -> p c j r", c=4, j=4)
            m = V.do(nc.vector.reciprocal, rec[:, :, :], turned[:, :, :, HD], after=[tr, st["recm"]])
            out = o_tok[:, :, :, :].rearrange("p t h d -> p t (h d)")[:, :, bass.ts(h, HD)].rearrange("p (j c) d -> p c j d", c=4)
            st["recm"] = V.do(nc.vector.tensor_tensor, out, turned[:, :, :, 0:HD],
                              rec[:, :, :].unsqueeze(3).broadcast_to([128, 4, 4, HD]), ALU.mult, after=[m])
            yield

        def unit(h0, v, more=True, first=False):
            if v == SEAM and more:
                st["load1"][0] = load(Ld1[0], Q1[0], K1[0], h0 + 2, [st["s1end"][0]])
            ahead = v + 64 + LEAD
            if more or ahead < 128:
                scores_max((ahead // 64) % 2, ahead % 64, v % 3)
                if ahead % 64 == 63:
                    slow.append(maxima((ahead // 64) % 2))
                    if more and ahead // 64 == 1:
                        st["load1"][1] = load(Ld1[1], Q1[1], K1[1], h0 + 3, [st["s1end"][1]])
            scores_exp(v // 64, v % 64, v % 3)
            if v % 4 == 3 and not (first and v < 7):
                for y in range(v - 7, v - 3):
                    values((y // 64) % 2, y % 64)
            for chain in list(slow):
                next(chain, None)
            if v % 64 == 3 and not first:
                par = 1 - v // 64
                slow.append(normalise(par, h0 + v // 64 - 1))
                next(slow[-1])
                if more or par == 1:
                    st["load2"][par] = load(Ld2[par], Q2[par], K2[par], h0 + 2 - par, [st["s2end"][par]])
                    st["vs"][par] = stage_v(par, h0 + 2 - par, [st["pvend"][par]])

        def pair(h0):
            slow.clear()
            for v in range(SEAM, 128):
                unit(h0, v)
            for v in range(SEAM):
                unit(h0 + 2, v)

        for i in range(2):
            st["load1"][i] = load(Ld1[i], Q1[i], K1[i], i, scratch_done)
            st["load2"][i] = load(Ld2[i], Q2[i], K2[i], i, scratch_done + [inited])
            st["vs"][i] = stage_v(i, i, [v_ready, inited])
        p.wait(nc.tensor, [V.last(), v_ready])
        for u in range(64):
            scores_max(0, u, u % 3)
        for _ in maxima(0):
            pass
        for u in range(LEAD):
            scores_max(1, u, u % 3)
        for v in range(SEAM):
            unit(0, v, first=True)
        p.pipeline(HEADS // 2 - 1, lambda i: pair(2 * i), st)
        slow.clear()
        for v in range(SEAM, 128):
            unit(HEADS - 2, v, more=False)
        for u in range(60, 64):
            values(1, u)
        for _ in normalise(1, HEADS - 1):
            pass
        p.join()

        oT = sb("o_T", [128, N])
        for b in range(NB):
            for c in range(4):
                t = 4 * b + c
                tr = T.do(nc.tensor.transpose, g.ps[b][:, c * 128:(c + 1) * 128], o_tok[:, t, :, :].rearrange("p h d -> p (h d)"), g.ident[:, :])
            A.do(nc.scalar.copy, oT[:, b * 512:(b + 1) * 512], g.ps[b][:, :], after=[tr])
        for b in range(NB):
            bank = g.ps[4 + b]
            for c in range(4):
                t = 4 * b + c
                o = bank[:, c * 128:(c + 1) * 128]
                T.do(nc.tensor.matmul, o, oT[:, t * 128:(t + 1) * 128], w["woT"], start=True, stop=False, after=[A.last()])
                mm = T.do(nc.tensor.matmul, o, g.ones_row[:, 0:128], w["bo"], start=False, stop=True)
            x = g.x_tok[:, 4 * b:4 * b + 4, :]
            V.do(nc.vector.tensor_tensor, x, x, bank[:, :].rearrange("p (t f) -> p t f", t=4), ALU.add, after=[mm])
        p.join()


FH, DK = 8, 64
NEXP = 4
KD = FH * DK
ST = 1 + NEXP

ORDER = "bbbbbb" + "acb" * 10

def gla_ffn(g, w):
    nc, p, V, A, T, G = g.nc, g.p, g.V, g.A, g.T, g.G
    with ExitStack() as mem:
        sb = lambda n, s, d=F32: mem.enter_context(nc.sbuf_tensor(f"{n}{g.uid()}", s, d))
        a1T = sb("low_rank_qk", [128, N])
        a2T = sb("low_rank_gates", [128, N])
        gate = sb("out_gateT", [128, 4, N])
        maskR = sb("expert_mask_rows", [NEXP, N], BF16)
        selR = sb("expert_select", [NEXP, NEXP, 128], BF16)
        head_ones = sb("head_ones", [128, 2, DK])
        mask = sb("expert_mask", [128, NT, NEXP])
        prob = sb("expert_prob", [128, NT, NEXP])
        rw = sb("expert_weight", [128, NT])
        rws = sb("expert_weight_scaled", [128, NT])
        et = sb("expert_tmp", [128, NT])
        half = sb("half_mask", [128, NT, 2, NEXP])
        tri_s = sb("same_expert_tri", [128, NT, 128], BF16)
        cum_s = sb("same_expert_cum", [128, NT, 128], BF16)
        early = ExitStack()
        maskT = early.enter_context(nc.sbuf_tensor(f"expert_maskT{g.uid()}", [NEXP, N], F32))
        z = G.do(nc.gpsimd.memset, selR[:, :, :], 0.0)
        z = G.do(nc.gpsimd.affine_select, out=selR[:, :, :], in_=selR[:, :, :], compare_op=ALU.not_equal, fill=1.0, base=0,
                 pattern=[[-1, NEXP], [0, 128]], channel_multiplier=1, after=[z])
        z = G.do(nc.gpsimd.memset, head_ones[:, :, :], 1.0)
        z = G.do(nc.gpsimd.affine_select, out=head_ones[:, 0, :], in_=head_ones[:, 0, :], compare_op=ALU.is_ge, fill=0.0, base=63,
                 pattern=[[0, DK]], channel_multiplier=-1, after=[z])
        z = G.do(nc.gpsimd.affine_select, out=head_ones[:, 1, :], in_=head_ones[:, 1, :], compare_op=ALU.is_ge, fill=0.0, base=-64,
                 pattern=[[0, DK]], channel_multiplier=1, after=[z])
        m = G.do(nc.gpsimd.memset, a2T[64:128, :], 1.0, after=[z])
        for b in range(NB):
            c = slice(b * 512, (b + 1) * 512)
            m1 = T.do(nc.tensor.matmul, g.ps[b][:, :], w["Wa"][:, 0:128], g.xnT[:, c], start=True, stop=True)
            lowq = A.do(nc.scalar.copy, a1T[:, c], g.ps[b][:, :], after=[m1])
            o = g.ps[4 + b]
            T.do(nc.tensor.matmul, o[0:64, :], w["Wa"][:, 128:192], g.xnT[:, c], start=True, stop=True)
            T.do(nc.tensor.matmul, o[64:80, :], w["Wa"][:, 192:208], g.xnT[:, c], start=True, stop=True)
            m2 = T.do(nc.tensor.matmul, o[96:112, :], w["Wa"][:, 208:224], g.xnT[:, c], start=True, stop=True)
            V.do(nc.vector.tensor_copy, a2T[0:64, c], o[0:64, :], after=[m2])
            V.do(nc.vector.tensor_copy, a2T[64:80, c], o[64:80, :], after=[m])
            low = V.do(nc.vector.tensor_copy, a2T[96:112, c], o[96:112, :])
        le = g.ps[0][:, 0:NT * NEXP].rearrange("p (t e) -> p t e", e=NEXP)
        for t in range(NT):
            mm = T.do(nc.tensor.matmul, g.ps[0][:, t * NEXP:(t + 1) * NEXP], g.xnT[:, t * 128:(t + 1) * 128], w["We"], start=True, stop=True, after=[lowq])
        up = lambda ap, k: ap.unsqueeze(2).broadcast_to([128, NT, k])
        m = V.do(nc.vector.tensor_reduce, et[:, :], le, AX.X, ALU.max, after=[mm])
        m = V.do(nc.vector.tensor_tensor, prob[:, :, :], le, up(et[:, :], NEXP), ALU.subtract, after=[m])
        exped = A.do(nc.scalar.activation, prob[:, :, :], prob[:, :, :], ACT.Exp, after=[m])
        nc.scalar.preload_act_table(ACT.Silu)

        def routing():
            m = V.do(nc.vector.tensor_reduce, et[:, :], prob[:, :, :], AX.X, ALU.add, after=[exped])
            m = V.do(nc.vector.reciprocal, et[:, :], et[:, :], after=[m])
            m = V.do(nc.vector.tensor_tensor, prob[:, :, :], prob[:, :, :], up(et[:, :], NEXP), ALU.mult, after=[m])
            m = V.do(nc.vector.tensor_reduce, rw[:, :], prob[:, :, :], AX.X, ALU.max, after=[m])
            V.do(nc.vector.tensor_scalar, rws[:, :], rw[:, :], DK ** -0.5, None, ALU.mult, after=[m])
            m = V.do(nc.vector.tensor_tensor, mask[:, :, :], prob[:, :, :], up(rw[:, :], NEXP), ALU.is_equal, after=[m])
            m = V.do(nc.vector.tensor_copy, et[:, :], mask[:, :, 0], after=[m])
            for e in range(1, NEXP):
                m = V.do(nc.vector.tensor_tensor, mask[:, :, e], mask[:, :, e], et[:, :], ALU.is_gt, after=[m])
                m = V.do(nc.vector.tensor_tensor, et[:, :], et[:, :], mask[:, :, e], ALU.add, after=[m])
            for k in range(2):
                V.do(nc.vector.tensor_scalar, half[:, :, k, :], mask[:, :, :], g.half_col[:, k:k + 1], None, ALU.mult, after=[m])
            masked = V.last()
            yield
            yield
            for b in range(NB):
                for c in range(4):
                    tr = T.do(nc.tensor.transpose, g.ps[4][0:NEXP, c * 128:(c + 1) * 128], mask[:, 4 * b + c, :], g.ident[:, :], after=[masked, A.last()])
                A.do(nc.scalar.copy, maskT[:, b * 512:(b + 1) * 512], g.ps[4][0:NEXP, :], after=[tr])
                yield
            used = [None] * 2
            for b in range(NB):
                bank = g.ps[4 + b % 2]
                for c in range(4):
                    ts = slice((4 * b + c) * 128, (4 * b + c + 1) * 128)
                    mm = T.do(nc.tensor.matmul, bank[:, c * 128:(c + 1) * 128], maskT[:, ts], maskT[:, ts], start=True, stop=True, after=[A.last(), used[b % 2]])
                same = bank[:, :].rearrange("p (t k) -> p t k", t=4)
                four = lambda ap: ap.unsqueeze(1).broadcast_to([128, 4, 128])
                V.do(nc.vector.tensor_tensor, tri_s[:, 4 * b:4 * b + 4, :], same, four(g.tri[:, :]), ALU.mult, after=[mm])
                used[b % 2] = V.do(nc.vector.tensor_tensor, cum_s[:, 4 * b:4 * b + 4, :], same, four(g.cum[:, :]), ALU.mult)
                yield

        route = routing()
        used = [None] * 4
        for t in range(NT):
            k = (1, 2, 3, 6)[t % 4]
            r, c = t // NB, slice((t % NB) * 512, (t % NB + 1) * 512)
            mm = T.do(nc.tensor.matmul, g.ps[k][:, :], w["Wc"][0:64, r * 128:(r + 1) * 128], a2T[0:64, c], start=True, stop=True, after=[low, lowq, used[t % 4]])
            s = used[t % 4] = A.do(nc.scalar.activation, gate[:, r, c], g.ps[k][:, :], ACT.Silu, after=[mm])
            G.do(nc.gpsimd.tensor_scalar, gate[:, r, c], gate[:, r, c], w["norm"], 1.0, ALU.mult, ALU.mult, after=[s])
            if t >= 2:
                next(route, None)
        for _ in route:
            pass
        V.do(nc.vector.tensor_copy, maskR[:, :], maskT[:, :], after=[A.last()])
        nc.scalar.preload_act_table_set("natural_log_exp_and_others")
        p.join()
        early.close()

        two = lambda n, s, d=F32: [sb(f"{n}{i}", s, d) for i in range(2)]
        xs, a1s, a2s, cs = two("x_tile", [128, 128]), two("qk_tile", [128, 128]), two("gate_tile", [128, 128]), two("cum_tile", [128, 128])
        v_t, vm = two("v_tile", [128, FH, DK]), two("v_experts", [128, FH, NEXP, DK])
        ms = two("mask_tile", [128, NEXP])
        qg, kg = two("q_decayed", [128, 2, KD]), two("k_decayed", [128, 2, KD])
        qT, kT = two("q_decayedT", [128, 2, 4, 128]), two("k_decayedT", [128, 2, 4, 128])
        eh = two("exp_halves", [128, 4, 2, ST])
        gk = sb("log_decay", [128, 2, KD])
        ab = sb("abs_logit", [128, 2, KD])
        eg, en = sb("exp_cum", [128, 2, KD]), sb("exp_neg_cum", [128, 2, KD])
        ks1 = sb("k_stats", [128, FH])
        sA = sb("scores_dense", [128, 2, 4, 128])
        sB = sb("scores_expert", [128, 2, 4, 128])
        SS, U = sb("state_middle", [128, 4, ST, DK]), sb("state_end", [128, 4, ST, DK])
        dec = sb("state_decay", [128, 4, ST])
        qm = sb("q_experts", [128, NEXP, 4, 128])
        o_t, o_q = two("outT_tile", [128, 4, 128]), sb("out_square", [128, 4, 128])
        G.do(nc.gpsimd.memset, U[:, :, :, :], 0.0)
        G.do(nc.gpsimd.memset, eh[1][:, :, :, :], 1.0)
        hv = lambda ap: ap.rearrange("p (h e) -> p h e", h=FH)
        P3, Abank, Obank, Dbank = g.ps[0:3], g.ps[3:5], g.ps[5:7], g.ps[7]

        pair = lambda: [None, None]
        st = dict(bank=[None] * 3, A=pair(), O=None, O_read=pair(), D=None, B=pair(), gk=None, gkr=None, kgd=None, U=None, SS_read=None, qm_read=None,
                  vm=pair(), turn=pair(), out=pair(), out_read=pair(), rs_read=None, SS=None, staged=pair(), projected=pair())
        nb = [0]

        def bank():
            k = nb[0] % 3
            nb[0] += 1
            return k, P3[k]

        def stage_tile(q, t):
            for dst, src in ((a2s[q], a2T[:, bass.ts(t, 128)]), (a1s[q], a1T[:, bass.ts(t, 128)]), (xs[q], g.xnT[:, bass.ts(t, 128)]),
                             (cs[q], cum_s[:, :, :].rearrange("p t k -> p (t k)")[:, bass.ts(t, 128)])):
                st["staged"][q] = G.do(nc.gpsimd.tensor_copy, dst[:, :], src, after=[st["projected"][q]])

        def stage_a(q, t, st, more):
            free, c = st["B"][q], st["staged"][q]
            zs = []
            for k, r in ((0, 64), (1, 96)):
                b, ps = bank()
                mm = T.do(nc.tensor.matmul, ps[:, :], a2s[q][r:r + 17, :], w["Wc"][r:r + 17, :], start=True, stop=True, after=[c, st["bank"][b]])
                m = A.do(nc.scalar.activation, ab[:, k, :], ps[:, :], ACT.Abs, after=[mm, st["gk"]])
                z = V.do(nc.vector.tensor_scalar, gk[:, k, :], ps[:, :], 0.0, 1 / 16.0, ALU.min, ALU.mult, after=[m, st["gkr"]])
                st["bank"][b] = z
            m = A.do(nc.scalar.activation, ab[:, :, :], ab[:, :, :], ACT.Exp, scale=-1.0, after=[m])
            m = A.do(nc.scalar.activation, ab[:, :, :], ab[:, :, :], ACT.Ln, bias=1.0, after=[m])
            mc = G.do(nc.gpsimd.tensor_copy, ms[q][:, :], mask[:, :, :].rearrange("p t e -> p (t e)")[:, bass.ts(t, NEXP)], after=[free])
            b, ps = bank()
            mm = T.do(nc.tensor.matmul, ps[:, :], xs[q][:, :], w["Wp"][:, 1024:1536], start=True, stop=True, after=[c, st["bank"][b]])
            vv = st["bank"][b] = A.do(nc.scalar.copy, v_t[q][:, :, :].rearrange("p h e -> p (h e)"), ps[:, :], after=[mm, free])
            for e in range(NEXP):
                st["vm"][q] = G.do(nc.gpsimd.tensor_scalar, vm[q][:, :, e, :], v_t[q][:, :, :], ms[q][:, e:e + 1], 1.0, ALU.mult, ALU.mult, after=[vv, mc, free])
            gm = st["gk"] = V.do(nc.vector.scalar_tensor_tensor, gk[:, :, :], ab[:, :, :], -1 / 16.0, gk[:, :, :], ALU.mult, ALU.add, after=[m, z])
            yield
            b, ps = bank()
            mm = T.do(nc.tensor.matmul, ps[:, :], a1s[q][64:128, :], w["Wb"][64:128, :], start=True, stop=True, after=[c, st["bank"][b]])
            r = V.do(nc.vector.tensor_reduce, ks1[:, :], hv(ps[:, :]), AX.X, ALU.max, after=[mm])
            bc = lambda ap: ap.unsqueeze(2).broadcast_to([128, FH, DK])
            r = st["bank"][b] = V.do(nc.vector.tensor_tensor, hv(kg[q][:, 1, :]), hv(ps[:, :]), bc(ks1[:, :]), ALU.subtract, after=[r, free])
            r = A.do(nc.scalar.activation, kg[q][:, 1, :], kg[q][:, 1, :], ACT.Exp, after=[r])
            yield
            es = []
            for k, lhs in ((0, g.cum), (1, cs[q])):
                b, ps = bank()
                mm = T.do(nc.tensor.matmul, ps[:, :], lhs[:, :], gk[:, k, :], start=True, stop=True, after=[gm, c, st["bank"][b]])
                A.do(nc.scalar.activation, eg[:, k, :], ps[:, :], ACT.Exp, after=[mm, st["kgd"]])
                st["bank"][b] = A.do(nc.scalar.activation, en[:, k, :], ps[:, :], ACT.Exp, scale=-1.0)
                es.append(st["bank"][b])
            yield
            b, ps = bank()
            for pr in range(4):
                o = ps[:, pr * 16:pr * 16 + 10].rearrange("p (k s) -> p k s", s=ST)
                T.do(nc.tensor.matmul, o[:, :, 0], gk[:, 0, pr * 128:(pr + 1) * 128], g.half_col[:, :], start=True, stop=True, after=[st["bank"][b]])
                mm = T.do(nc.tensor.matmul, o[:, :, 1:ST], gk[:, 1, pr * 128:(pr + 1) * 128],
                          half[:, :, :, :].rearrange("p t k e -> p t (k e)")[:, bass.ds(t, 1), :].rearrange("p t (k e) -> p (t k) e", k=2),
                          start=True, stop=True)
            st["gkr"] = mm
            st["bank"][b] = A.do(nc.scalar.activation, eh[q][:, :, :, :].rearrange("p r k s -> p r (k s)"),
                                 ps[:, 0:64].rearrange("p (r x) -> p r x", r=4)[:, :, 0:10], ACT.Exp, after=[mm, free])
            s = V.do(nc.vector.tensor_reduce, ks1[:, :], hv(kg[q][:, 1, :]), AX.X, ALU.add, after=[r])
            s = V.do(nc.vector.reciprocal, ks1[:, :], ks1[:, :], after=[s])
            s = V.do(nc.vector.tensor_scalar, ks1[:, :], ks1[:, :], rw[:, bass.ds(t, 1)], None, ALU.mult, after=[s])
            s = V.do(nc.vector.tensor_tensor, hv(kg[q][:, 1, :]), hv(kg[q][:, 1, :]), bc(ks1[:, :]), ALU.mult, after=[s])
            s = V.do(nc.vector.tensor_tensor, kg[q][:, 1, :], kg[q][:, 1, :], en[:, 1, :], ALU.mult, after=[s, es[1], free])
            yield
            def turn(src, dst, k, made):
                b, ps = bank()
                for pr in range(4):
                    tr = T.do(nc.tensor.transpose, ps[:, pr * 128:(pr + 1) * 128], src[:, k, pr * 128:(pr + 1) * 128], g.ident[:, :], after=[made, st["bank"][b]])
                eng, fn = ((A, nc.scalar.copy), (V, nc.vector.tensor_copy))[k]
                st["turn"][k] = st["bank"][b] = eng.do(fn, dst[:, k, :, :].rearrange("p r t -> p (r t)"), ps[:, :], after=[tr, free])

            b, ps = bank()
            mm = T.do(nc.tensor.matmul, ps[:, :], xs[q][:, :], w["Wp"][:, 512:1024], start=True, stop=True, after=[st["bank"][b]])
            k1 = st["bank"][b] = V.do(nc.vector.tensor_tensor, kg[q][:, 0, :], ps[:, :], en[:, 0, :], ALU.mult, after=[mm, es[0], free])
            b, ps = bank()
            mm = T.do(nc.tensor.matmul, ps[:, :], a1s[q][0:64, :], w["Wb"][0:64, :], start=True, stop=True, after=[st["bank"][b]])
            q2 = st["bank"][b] = V.do(nc.vector.scalar_tensor_tensor, qg[q][:, 1, :], ps[:, :], rws[:, bass.ds(t, 1)], eg[:, 1, :], ALU.mult, ALU.mult, after=[mm, free])
            yield
            turn(kg[q], kT[q], 1, s)
            b, ps = bank()
            mm = T.do(nc.tensor.matmul, ps[:, :], xs[q][:, :], w["Wp"][:, 0:512], start=True, stop=True, after=[st["bank"][b]])
            q1 = st["bank"][b] = st["kgd"] = V.do(nc.vector.scalar_tensor_tensor, qg[q][:, 0, :], ps[:, :], DK ** -0.5, eg[:, 0, :], ALU.mult, ALU.mult, after=[mm, free])
            st["projected"][q] = mm
            if more:
                stage_tile(q, t + 2)
            yield
            turn(kg[q], kT[q], 0, k1)
            yield
            turn(qg[q], qT[q], 1, q2)
            yield
            turn(qg[q], qT[q], 0, q1)
            yield

        def stage_b(q, t, st):
            o_s = o_t[q]
            turned = list(st["turn"])
            half_of = lambda x: slice(64 * x, 64 * x + 64)
            d = V.do(nc.vector.tensor_tensor, dec[:, :, :], eh[1 - q][:, :, 1, :], eh[q][:, :, 0, :], ALU.mult, after=turned + [st["SS"]])
            sm = st["SS"] = G.do(nc.gpsimd.tensor_tensor, SS[:, :, :, :].rearrange("p r s e -> p (r s) e"), U[:, :, :, :].rearrange("p r s e -> p (r s) e"),
                                 dec[:, :, :].rearrange("p r s -> p (r s)").unsqueeze(2).broadcast_to([128, 4 * ST, DK]), ALU.mult,
                                 after=[d, st["U"], st["SS_read"]])
            for k, dst in ((0, sA), (1, sB)):
                for x in range(2):
                    for y in range(4):
                        mm = T.do(nc.tensor.matmul, Abank[x][:, y * 128:y * 128 + 128], kT[q][half_of(x), k, y, :], qT[q][half_of(x), k, y, :],
                                  start=True, stop=True, after=turned + [st["A"][x]])
                    mt = g.tri[:, :] if k == 0 else tri_s[:, :, :].rearrange("p t k -> p (t k)")[:, bass.ts(t, 128)]
                    st["A"][x] = V.do(nc.vector.tensor_tensor, dst[:, x, :, :], Abank[x][:, :].rearrange("p (h t) -> p h t", h=4),
                                      mt.unsqueeze(1).broadcast_to([128, 4, 128]), ALU.mult, after=[mm, st["O"]])
                    yield
            scored = V.last()
            ao = G.do(nc.gpsimd.tensor_tensor, sA[:, :, :, :], sA[:, :, :, :], sB[:, :, :, :], ALU.add, after=[scored])
            b, ps = bank()
            for e in range(NEXP):
                mm = T.do(nc.tensor.matmul, ps[:, e * 128:(e + 1) * 128], selR[:, e, :], maskR[:, bass.ts(t, 128)], start=True, stop=True, after=[st["bank"][b]])
            qd = st["bank"][b] = V.do(nc.vector.tensor_tensor, qm[:, :, :, :], qT[q][:, 1, :, :].unsqueeze(1).broadcast_to([128, NEXP, 4, 128]),
                                      ps[:, :].rearrange("p (e t) -> p e t", e=NEXP).unsqueeze(2).broadcast_to([128, NEXP, 4, 128]), ALU.mult,
                                      after=[mm, st["qm_read"]])
            yield
            p.hold(nc.tensor, [sm, st["O_read"][0], st["O_read"][1]])
            for s in range(ST):
                if s == 1:
                    p.hold(nc.tensor, [qd])
                for y in range(4):
                    for x in range(2):
                        mm = T.do(nc.tensor.matmul, Obank[x][half_of(x), y * 128:(y + 1) * 128], SS[half_of(x), y, s, :],
                                  qT[q][half_of(x), 0, y, :] if s == 0 else qm[half_of(x), s - 1, y, :], start=(s == 0 and y == 0), stop=False,
                                  skip_group_check=True)
                if s % 2 == 0:
                    yield
            st["qm_read"] = st["SS_read"] = mm
            for y in range(4):
                for x in range(2):
                    mm = T.do(nc.tensor.matmul, Obank[x][half_of(x), y * 128:(y + 1) * 128], v_t[q][:, 2 * y + x, :], sA[:, x, y, :], start=False, stop=(y == 3),
                              after=[ao, st["qm_read"]], skip_group_check=True)
            st["O"] = mm
            for x in range(2):
                st["O_read"][x] = A.do(nc.scalar.copy, o_s[half_of(x), :, :].rearrange("p y t -> p (y t)"), Obank[x][half_of(x), :], after=[mm, st["out_read"][q]])
            st["out"][q] = A.last()
            yield
            for x in range(2):
                for h in range(4 * x, 4 * x + 4):
                    mm = T.do(nc.tensor.matmul, Abank[x][half_of(h % 2), (h // 2 % 2) * 256:(h // 2 % 2) * 256 + 256], kg[q][:, 1, h * DK:(h + 1) * DK], vm[q][:, h, :, :],
                              start=True, stop=True, after=[st["A"][x], st["vm"][q]])
                st["A"][x] = V.do(nc.vector.tensor_tensor, U[:, 2 * x:2 * x + 2, 1:ST, :], SS[:, 2 * x:2 * x + 2, 1:ST, :],
                                  Abank[x][:, :].rearrange("p (r x e) -> p r x e", r=2, x=NEXP), ALU.add, after=[mm, sm])
                yield
            for h in range(FH):
                mm = T.do(nc.tensor.matmul, Dbank[half_of(h % 2), (h // 2) * DK:(h // 2 + 1) * DK], kg[q][:, 0, h * DK:(h + 1) * DK], v_t[q][:, h, :],
                          start=True, stop=True, after=[st["D"]])
            st["D"] = st["U"] = V.do(nc.vector.tensor_tensor, U[:, :, 0, :], SS[:, :, 0, :], Dbank[:, 0:256].rearrange("p (r e) -> p r e", r=4), ALU.add, after=[mm])
            st["SS_read"] = st["U"]
            st["B"][q] = mm
            yield

        def stage_c(q, t, st):
            o_s = o_t[q]
            flat = lambda ap: ap[:, :, :].rearrange("p y t -> p (y t)")
            m = A.do(nc.scalar.activation, flat(o_q), flat(o_s), ACT.Square, after=[st["out"][q], st["rs_read"]])
            gt = G.do(nc.gpsimd.tensor_tensor, o_s[:, :, :], o_s[:, :, :], gate[:, :, bass.ts(t, 128)], ALU.mult, after=[m])
            yield
            b, ps = bank()
            mm = T.do(nc.tensor.matmul, ps[:, :], head_ones[:, :, :].rearrange("p x e -> p (x e)"), flat(o_q), start=True, stop=True,
                                      after=[m, st["bank"][b]])
            m = st["bank"][b] = A.do(nc.scalar.activation, flat(o_q), ps[:, :], ACT.Ln, bias=g.eps_ln[:, :], scale=1.0 / DK, after=[mm])
            m = A.do(nc.scalar.activation, flat(o_q), flat(o_q), ACT.Exp, scale=-0.5, after=[m])
            yield
            m = st["rs_read"] = V.do(nc.vector.tensor_tensor, flat(o_s), flat(o_s), flat(o_q), ALU.mult, after=[m, gt])
            yield
            b, ps = bank()
            for c in range(4):
                mm = T.do(nc.tensor.matmul, ps[:, 0:128], o_s[:, c, :], w["Wo"][:, c * 128:(c + 1) * 128], start=(c == 0), stop=(c == 3), after=[m, st["bank"][b]])
            st["out_read"][q] = mm
            x = g.x_tok[:, :, :].rearrange("p t d -> p (t d)")[:, bass.ts(t, 128)]
            st["bank"][b] = V.do(nc.vector.tensor_tensor, x, x, ps[:, 0:128], ALU.add, after=[mm])
            yield

        def together(*gens):
            gens = list(gens)
            while gens:
                for x in list(gens):
                    if next(x, "end") == "end":
                        gens.remove(x)

        p.join()
        stage_tile(0, 0)
        stage_tile(1, 1)
        together(stage_a(0, 0, st, True))

        def step(t, par, after, before, more=True):
            stages = dict(b=stage_b(par, t, st), a=stage_a(1 - par, t + 1, st, more) if after else iter(()),
                          c=stage_c(1 - par, t - 1, st) if before else iter(()))
            for name in ORDER:
                next(stages[name], None)

        def tiles(t):
            nb[0] = 0
            step(t, 1, True, True)
            step(t + 1, 0, True, True)

        step(0, 0, True, False)
        p.pipeline(NT // 2 - 2, lambda i: tiles(2 * i + 1), st)
        step(NT - 3, 1, True, True, False)
        step(NT - 2, 0, True, True, False)
        step(NT - 1, 1, False, True)
        together(stage_c(1, NT - 1, st))
        p.join()


DI, NS, RANK, CONV = 256, 16, 8, 4
CHK = 1024

def mamba(g, w):
    nc, p, V, A, T, G = g.nc, g.p, g.V, g.A, g.T, g.G
    with ExitStack() as mem:
        sb = lambda n, s, d=F32: mem.enter_context(nc.sbuf_tensor(f"{n}{g.uid()}", s, d))
        res, xi = sb("silu_res", [128, 2, N]), sb("conv_out", [128, 2, N])
        dt, dtx = sb("dt", [128, 2, N]), sb("dt_x", [128, 2, N])
        BC = sb("bc_parts", [96, N], BF16)
        sel = sb("row_select", [96, 2 * NS, 128], BF16)
        negA = sb("neg_A", [128, 2, NS])
        with ExitStack() as early:
            sbe = lambda n, s, d=F32: early.enter_context(nc.sbuf_tensor(f"{n}{g.uid()}", s, d))
            xp = sbe("conv_in", [128, 2, CONV - 1 + N])
            bcf = sbe("bc_full", [32, 2, N])
            dlt = sbe("delta", [RANK, N])
            z = G.do(nc.gpsimd.memset, xp[:, :, 0:CONV - 1], 0.0)
            m = G.do(nc.gpsimd.memset, sel[:, :, :], 0.0)
            for k in range(3):
                m = G.do(nc.gpsimd.affine_select, out=sel[:, :, :], in_=sel[:, :, :], compare_op=ALU.not_equal, fill=1.0, base=-32 * k,
                         pattern=[[-1, 2 * NS], [0, 128]], channel_multiplier=1, after=[m])
            m = A.do(nc.scalar.activation, negA[:, :, :], w["A_log"], ACT.Exp)
            V.do(nc.vector.tensor_scalar, negA[:, :, :], negA[:, :, :], -1.0, None, ALU.mult, after=[m])
            nc.scalar.preload_act_table(ACT.Silu)
            free = [None] * 8
            blk = lambda b: slice(b * 512, (b + 1) * 512)
            conv, split_in, low = {}, [], []

            def project(b):
                for c in range(4):
                    mm = T.do(nc.tensor.matmul, g.ps[c], w["in_proj"][:, c * 128:(c + 1) * 128], g.xnT[:, blk(b)], start=True, stop=True, after=[free[c]])
                    if c < 2:
                        free[c] = A.do(nc.scalar.copy, xp[:, c, CONV - 1 + b * 512:CONV - 1 + (b + 1) * 512], g.ps[c], after=[mm])
                    else:
                        free[c] = A.do(nc.scalar.activation, res[:, c - 2, blk(b)], g.ps[c], ACT.Silu, after=[mm])

            def convolve(b):
                ms = [V.do(nc.vector.tensor_scalar, xi[:, c, blk(b)], xp[:, c, b * 512:(b + 1) * 512], w["conv_w"][:, c, 0:1], w["conv_b"][:, c:c + 1],
                           ALU.mult, ALU.add, after=[free[c], z]) for c in range(2)]
                for q in range(1, CONV):
                    ms = [V.do(nc.vector.scalar_tensor_tensor, xi[:, c, blk(b)], xp[:, c, b * 512 + q:(b + 1) * 512 + q], w["conv_w"][:, c, q:q + 1], xi[:, c, blk(b)],
                               ALU.mult, ALU.add, after=[ms[c]]) for c in range(2)]
                conv[b] = ms

            def rows(b):
                for c in range(2):
                    a = A.do(nc.scalar.activation, xi[:, c, blk(b)], xi[:, c, blk(b)], ACT.Silu, after=[conv[b][c]])
                k0, k1 = 4 + 2 * (b % 2), 5 + 2 * (b % 2)
                for c in range(2):
                    mb = T.do(nc.tensor.matmul, g.ps[k0][0:32, :], w["x_proj"][:, c, RANK:RANK + 32], xi[:, c, blk(b)], start=(c == 0), stop=(c == 1), after=[a, free[k0]])
                for c in range(2):
                    md = T.do(nc.tensor.matmul, g.ps[k1][0:RANK, :], w["x_proj"][:, c, 0:RANK], xi[:, c, blk(b)], start=(c == 0), stop=(c == 1), after=[free[k1]])
                free[k0] = V.do(nc.vector.tensor_copy, bcf[:, 0, blk(b)], g.ps[k0][0:32, :], after=[mb])
                free[k1] = V.do(nc.vector.tensor_copy, dlt[:, blk(b)], g.ps[k1][0:RANK, :], after=[md])
                split_in.append(free[k0])
                low.append(free[k1])

            for b in range(NB + 1):
                if b < NB:
                    project(b)
                    convolve(b)
                if b:
                    rows(b - 1)
            f0 = split_in[-1]

            def split():
                m = A.do(nc.scalar.copy, BC[0:32, :], bcf[:, 0, :], after=[f0])
                m = G.do(nc.gpsimd.tensor_tensor, bcf[:, 1, :], bcf[:, 0, :], BC[0:32, :], ALU.subtract, after=[m])
                yield
                m = A.do(nc.scalar.copy, BC[32:64, :], bcf[:, 1, :], after=[m])
                m = A.do(nc.scalar.copy, bcf[:, 0, :], BC[32:64, :], after=[m])
                G.do(nc.gpsimd.tensor_tensor, BC[64:96, :], bcf[:, 1, :], bcf[:, 0, :], ALU.subtract, after=[m])
                yield

            parts = split()
            next(parts)
            nc.scalar.preload_act_table_set("natural_log_exp_and_others")
            zb = xp[:, :, 0:N]
            ee, uu = dtx, sbe("one_plus_e", [128, 2, 512])
            units = [(c, b) for c in range(2) for b in range(NB)]
            made, logs, used, sub = {}, {}, [None] * 2, {}
            for n in range(len(units) + 2):
                if n < len(units):
                    c, b = units[n]
                    k = n % 4
                    mm = T.do(nc.tensor.matmul, g.ps[k], w["dt_w"][0:RANK, c * 128:(c + 1) * 128], dlt[:, blk(b)], start=True, stop=True, after=[low[b], free[k]])
                    m = free[k] = A.do(nc.scalar.activation, zb[:, c, blk(b)], g.ps[k], ACT.Identity, bias=w["dt_b"][:, c:c + 1], after=[mm, f0])
                    m = A.do(nc.scalar.activation, ee[:, c, blk(b)], zb[:, c, blk(b)], ACT.Abs, after=[m])
                    made[n] = A.do(nc.scalar.activation, ee[:, c, blk(b)], ee[:, c, blk(b)], ACT.Exp, scale=-1.0, after=[m])
                if n in (2, 6):
                    next(parts, None)
                if 1 <= n <= len(units):
                    c, b = units[n - 1]
                    u = V.do(nc.vector.tensor_scalar, uu[:, n % 2, :], ee[:, c, blk(b)], 1.0, None, ALU.add, after=[made[n - 1], used[n % 2], logs.get(n - 3)])
                    logs[n - 1] = A.do(nc.scalar.activation, dt[:, c, blk(b)], uu[:, n % 2, :], ACT.Ln, after=[u])
                    sub[n - 1] = V.do(nc.vector.scalar_tensor_tensor, ee[:, c, blk(b)], uu[:, n % 2, :], 1.0, ee[:, c, blk(b)], ALU.subtract, ALU.subtract, after=[u])
                    used[n % 2] = sub[n - 1]
                if n >= 2:
                    c, b = units[n - 2]
                    m = V.do(nc.vector.tensor_tensor, dt[:, c, blk(b)], dt[:, c, blk(b)], ee[:, c, blk(b)], ALU.subtract, after=[logs[n - 2], sub[n - 2]])
                    m = V.do(nc.vector.scalar_tensor_tensor, dt[:, c, blk(b)], zb[:, c, blk(b)], 0.0, dt[:, c, blk(b)], ALU.max, ALU.add, after=[m])
                    G.do(nc.gpsimd.tensor_tensor, dtx[:, c, blk(b)], dt[:, c, blk(b)], xi[:, c, blk(b)], ALU.mult, after=[m, G.last()])
            p.join()
        nc.scalar.preload_act_table_set("natural_log_exp_and_others")
        E = [[sb(f"decay{i}{c}", [128, CHK]) for c in range(2)] for i in range(2)]
        F = [[sb(f"state{i}{c}", [128, CHK]) for c in range(2)] for i in range(2)]
        Cs = [sb(f"c_row{i}", [128, CHK]) for i in range(2)]
        carry = sb("state_carry", [128, 2, NS])
        zero = sb("zero_row", [1, 512], BF16)
        y = sb("scan_out", [128, 2, N])
        G.do(nc.gpsimd.memset, carry[:, :, :], 0.0)
        zz = G.do(nc.gpsimd.memset, zero[:, :], 0.0)
        Bb, Cb, Yb = g.ps[0:2], g.ps[2:4], g.ps[4:8]
        for chunk in range(N // CHK):
            t0 = chunk * CHK
            st = dict(B=[None, None], C=None, E=[[None, None], [None, None]], Cs=[None, None], Fh=[[None, None], [None, None]], car=[[None, None], [None, None]])
            for k in range(4):
                T.do(nc.tensor.matmul, Yb[k][:, :], zero[:, 0:128], zero[:, :], start=True, stop=True, after=[zz, V.last()], skip_group_check=True)

            def front(n, i):
                for b in range(2):
                    ts = slice(t0 + b * 512, t0 + (b + 1) * 512)
                    mb = T.do(nc.tensor.matmul, Bb[b][:, :], sel[:, bass.ds(n, 1), :].rearrange("p a b -> p (a b)"), BC[:, ts], start=True, stop=True, after=[st["B"][1]])
                for b in range(2):
                    ts = slice(t0 + b * 512, t0 + (b + 1) * 512)
                    mc = T.do(nc.tensor.matmul, Cb[b][:, :], sel[:, bass.ds(n + NS, 1), :].rearrange("p a b -> p (a b)"), BC[:, ts], start=True, stop=True, after=[st["C"]])
                dec = []
                for c in range(2):
                    dec.append(A.do(nc.scalar.activation, E[i][c][:, :], dt[:, c, t0:t0 + CHK], ACT.Exp, scale=negA[:, c, bass.ds(n, 1)], after=[st["E"][i][c]]))
                cb = st["C"] = A.do(nc.scalar.copy, Cs[i][:, :], g.wide(2)[:, :], after=[mc, st["Cs"][i]])
                for c in range(2):
                    st["B"][c] = V.do(nc.vector.tensor_tensor, F[i][c][:, :], dtx[:, c, t0:t0 + CHK], g.wide(0)[:, :], ALU.mult, after=[mb, st["Fh"][i][c], st["car"][i][c]])
                for c in range(2):
                    h = V.do(nc.vector.tensor_tensor_scan, F[i][c][:, :], E[i][c][:, :], F[i][c][:, :], carry[:, c, bass.ds(n, 1)], ALU.mult, ALU.add,
                             after=[dec[c], st["B"][c]])
                    st["car"][i][c] = A.do(nc.scalar.copy, carry[:, c, bass.ds(n, 1)], F[i][c][:, CHK - 1:CHK], after=[h])
                    st["Cs"][i] = st["Fh"][i][c] = G.do(nc.gpsimd.tensor_tensor, E[i][c][:, :], F[i][c][:, :], Cs[i][:, :], ALU.mult, after=[h, cb])

            def back(i):
                for c in range(2):
                    for b in range(2):
                        st["E"][i][c] = T.do(nc.tensor.matmul, Yb[2 * c + b][:, :], g.ident[:, :], E[i][c][:, b * 512:(b + 1) * 512], start=False, stop=True,
                                             after=[st["Fh"][i][c]], skip_group_check=True)

            def pair(n0):
                front(n0 + 1, 1)
                back(0)
                front(n0 + 2, 0)
                back(1)

            p.join()
            front(0, 0)
            p.pipeline(NS // 2 - 1, lambda i: pair(2 * i), st)
            front(NS - 1, 1)
            back(0)
            back(1)
            p.join()
            for c in range(2):
                for b in range(2):
                    ts = slice(t0 + b * 512, t0 + (b + 1) * 512)
                    m = V.do(nc.vector.scalar_tensor_tensor, y[:, c, ts], xi[:, c, ts], w["Dp"][:, c:c + 1], Yb[2 * c + b][:, :], ALU.mult, ALU.add)
                G.do(nc.gpsimd.tensor_tensor, y[:, c, t0:t0 + CHK], y[:, c, t0:t0 + CHK], res[:, c, t0:t0 + CHK], ALU.mult, after=[m])
        gm = G.last()
        for b in range(NB):
            for q in range(4):
                t = 4 * b + q
                for c in range(2):
                    mm = T.do(nc.tensor.matmul, g.ps[b][:, q * 128:(q + 1) * 128], y[:, c, t * 128:(t + 1) * 128], w["out_proj"][:, c, :], start=(c == 0), stop=(c == 1), after=[gm, V.last()])
            xx = g.x_tok[:, 4 * b:4 * b + 4, :]
            V.do(nc.vector.tensor_tensor, xx, xx, g.ps[b][:, :].rearrange("p (t f) -> p t f", t=4), ALU.add, after=[mm])
        p.join()


EXPERTS, SHARED = 8, 2
UNITS = EXPERTS + SHARED

def first_of(g, V, mask, count, one, after):
    nc = g.nc
    m = V.do(nc.vector.tensor_copy, count, mask[:, :, 0], after=after)
    for e in range(1, one):
        m = V.do(nc.vector.tensor_tensor, mask[:, :, e], mask[:, :, e], count, ALU.is_gt, after=[m])
        m = V.do(nc.vector.tensor_tensor, count, count, mask[:, :, e], ALU.add, after=[m])
    return m

def moe(g, w, beside=None):
    nc, p, V, A, T, G = g.nc, g.p, g.V, g.A, g.T, g.G
    with ExitStack() as mem:
        sb = lambda n, s, d=F32: mem.enter_context(nc.sbuf_tensor(f"{n}{g.uid()}", s, d))
        sc, bs, m1, m2 = (sb(f"route{i}", [128, NT, EXPERTS]) for i in range(4))
        et = sb("route_tmp", [128, NT])
        GT = sb("gate_parts", [96, N], BF16)
        gf = sb("gate_full", [EXPERTS, 3, N])
        sel = sb("gate_select", [96, EXPERTS, 128], BF16)
        sa = sb("silu_a", [128, 3, 512])
        hs = sb("hidden", [128, 3, 512])
        cleared = G.do(nc.gpsimd.memset, GT[:, :], 0.0)
        m = G.do(nc.gpsimd.memset, sel[:, :, :], 0.0)
        for k in range(3):
            m = G.do(nc.gpsimd.affine_select, out=sel[:, :, :], in_=sel[:, :, :], compare_op=ALU.not_equal, fill=1.0, base=-32 * k,
                     pattern=[[-1, EXPERTS], [0, 128]], channel_multiplier=1, after=[m])
        selects = m
        up = lambda ap: ap.unsqueeze(2).broadcast_to([128, NT, EXPERTS])
        turn_banks = (g.ps[0], g.ps[6], g.ps[7])
        st = dict(a=[None] * 2, b=[None] * 2, gb=None, h=[None] * 3, y=None, sa=[None] * 3)
        Ab, Bb, Gb, Yb = g.ps[1:3], g.ps[3:5], g.ps[6], g.ps[5]

        le = g.ps[0][:, 0:NT * EXPERTS].rearrange("p (t e) -> p t e", e=EXPERTS)
        for t in range(NT):
            mm = T.do(nc.tensor.matmul, g.ps[0][:, t * EXPERTS:(t + 1) * EXPERTS], g.xnT[:, t * 128:(t + 1) * 128], w["gate"], start=True, stop=True)
        m = V.do(nc.vector.tensor_reduce, et[:, :], le, AX.X, ALU.max, after=[mm])
        m = V.do(nc.vector.tensor_tensor, sc[:, :, :], le, up(et[:, :]), ALU.subtract, after=[m])
        exped = A.do(nc.scalar.activation, sc[:, :, :], sc[:, :, :], ACT.Exp, after=[m])
        nc.scalar.preload_act_table(ACT.Silu)

        def routing():
            m = V.do(nc.vector.tensor_reduce, et[:, :], sc[:, :, :], AX.X, ALU.add, after=[exped])
            m = V.do(nc.vector.reciprocal, et[:, :], et[:, :], after=[m])
            m = V.do(nc.vector.tensor_tensor, sc[:, :, :], sc[:, :, :], up(et[:, :]), ALU.mult, after=[m])
            m = V.do(nc.vector.tensor_tensor, bs[:, :, :], sc[:, :, :], w["gate_bias"].unsqueeze(1).broadcast_to([128, NT, EXPERTS]), ALU.add, after=[m])
            for mk in (m1, m2):
                yield
                m = V.do(nc.vector.tensor_reduce, et[:, :], bs[:, :, :], AX.X, ALU.max, after=[m])
                m = V.do(nc.vector.tensor_tensor, mk[:, :, :], bs[:, :, :], up(et[:, :]), ALU.is_equal, after=[m])
                m = first_of(g, V, mk, et[:, :], EXPERTS, [m])
                if mk is m1:
                    m = V.do(nc.vector.scalar_tensor_tensor, bs[:, :, :], m1[:, :, :], -1e30, bs[:, :, :], ALU.mult, ALU.add, after=[m])
            m = V.do(nc.vector.tensor_tensor, m1[:, :, :], m1[:, :, :], m2[:, :, :], ALU.add, after=[m])
            m = V.do(nc.vector.tensor_tensor, m1[:, :, :], m1[:, :, :], sc[:, :, :], ALU.mult, after=[m])
            yield
            read = [None] * 3
            for b in range(NB):
                ts = slice(b * 512, (b + 1) * 512)
                bank = turn_banks[b % 3]
                for c in range(4):
                    tr = T.do(nc.tensor.transpose, bank[0:EXPERTS, c * 128:(c + 1) * 128], m1[:, 4 * b + c, :], g.ident[:, :], after=[m, read[b % 3]])
                cp = read[b % 3] = A.do(nc.scalar.copy, gf[:, 0, ts], bank[0:EXPERTS, :], after=[tr])
                v = V.do(nc.vector.tensor_copy, GT[0:8, ts], gf[:, 0, ts], after=[cp, cleared])
                v = V.do(nc.vector.tensor_tensor, gf[:, 1, ts], gf[:, 0, ts], GT[0:8, ts], ALU.subtract, after=[v])
                v = V.do(nc.vector.tensor_copy, GT[32:40, ts], gf[:, 1, ts], after=[v])
                a = A.do(nc.scalar.copy, gf[:, 2, ts], GT[32:40, ts], after=[v])
                yield
                V.do(nc.vector.tensor_tensor, GT[64:72, ts], gf[:, 1, ts], gf[:, 2, ts], ALU.subtract, after=[a])

        def experts(ts, units):
            hid = {}

            def front(u):
                k = u % 2
                ma = T.do(nc.tensor.matmul, Ab[k], w["w1"][:, u, :], g.xnT[:, ts], start=True, stop=True, after=[st["a"][k]])
                mb = T.do(nc.tensor.matmul, Bb[k], w["w3"][:, u, :], g.xnT[:, ts], start=True, stop=True, after=[st["b"][k]])
                if u < EXPERTS:
                    mg = T.do(nc.tensor.matmul, Gb, sel[:, u, :], GT[:, ts], start=True, stop=True, after=[st["gb"]])
                s = st["a"][k] = A.do(nc.scalar.activation, sa[:, u % 3, :], Ab[k], ACT.Silu, after=[ma, st["sa"][u % 3]])
                h = st["b"][k] = V.do(nc.vector.tensor_tensor, hs[:, u % 3, :], sa[:, u % 3, :], Bb[k], ALU.mult, after=[mb, s, st["h"][u % 3]])
                st["sa"][u % 3] = h
                if u < EXPERTS:
                    h = st["gb"] = V.do(nc.vector.tensor_tensor, hs[:, u % 3, :], hs[:, u % 3, :], Gb, ALU.mult, after=[mg, h])
                hid[u] = h

            def back(u):
                for c in range(4):
                    mm = T.do(nc.tensor.matmul, Yb[:, c * 128:(c + 1) * 128], hs[:, u % 3, c * 128:(c + 1) * 128], w["w2"][:, u, :],
                              start=(u == units[0] and c == 0), stop=(u == units[-1]), after=[hid[u], st["y"]], skip_group_check=True)
                st["h"][u % 3] = mm
                return mm

            front(units[0])
            yield
            for u in units[1:]:
                front(u)
                yield
                back(u - 1)
            mm = back(units[-1])
            x = g.x_tok[:, :, :].rearrange("p t d -> p (t d)")[:, ts]
            st["y"] = V.do(nc.vector.tensor_tensor, x, x, Yb, ALU.add, after=[mm])
            yield

        route = routing()
        for b in range(NB):
            for _ in experts(slice(b * 512, (b + 1) * 512), range(EXPERTS, UNITS)):
                next(route, None)
        for _ in route:
            pass
        p.wait(nc.tensor, [selects])
        left = []
        if beside:
            p.wait(nc.gpsimd, [V.last(), A.last()])
            beside()
            left = [G]

        def block(b):
            for _ in experts(bass.ts(b, 512), range(EXPERTS)):
                pass

        p.pipeline(NB, block, st, left)
        p.join(left)
        nc.scalar.preload_act_table_set("natural_log_exp_and_others")


TAPS = 4
SEG = 32
STEPS = N // SEG
GRP = 8
SPREADS = 4
EPS_R = 1e-6

def rotation_columns(g, theta, decay_log, col):
    nc, V, A = g.nc, g.V, g.A
    with ExitStack() as mem:
        ki = mem.enter_context(nc.sbuf_tensor(f"turns{g.uid()}", [128, 1], mybir.dt.int32))
        cc = lambda k: col[:, k:k + 1]
        vs = lambda o, i, a, b, o1, o2=ALU.bypass, **kw: V.do(nc.vector.tensor_scalar, o, i, a, b, o1, o2, after=[V.last(), A.last()])
        vt = lambda o, a, b, op: V.do(nc.vector.tensor_tensor, o, a, b, op, after=[V.last(), A.last()])
        TWO_PI = 2 * math.pi
        hi = 6.28125
        vs(cc(0), theta, 1 / TWO_PI, None, ALU.mult)
        V.do(nc.vector.tensor_copy, ki[:, :], cc(0), after=[V.last()])
        V.do(nc.vector.tensor_copy, cc(0), ki[:, :], after=[V.last()])
        V.do(nc.vector.scalar_tensor_tensor, cc(1), cc(0), -hi, theta, ALU.mult, ALU.add, after=[V.last()])
        V.do(nc.vector.scalar_tensor_tensor, cc(1), cc(0), -(TWO_PI - hi), cc(1), ALU.mult, ALU.add, after=[V.last()])
        vs(cc(1), cc(1), 0.5, None, ALU.mult)
        vs(cc(2), cc(1), -1.0, None, ALU.mult)
        vt(cc(2), cc(1), cc(2), ALU.max)
        vs(cc(2), cc(2), -1.0, math.pi / 2, ALU.mult, ALU.add)
        nc.scalar.preload_act_table(ACT.Sin)
        A.do(nc.scalar.activation, cc(3), cc(1), ACT.Sin, after=[V.last()])
        A.do(nc.scalar.activation, cc(4), cc(2), ACT.Sin)
        nc.scalar.preload_act_table_set("natural_log_exp_and_others")
        vt(cc(6), cc(3), cc(4), ALU.mult)
        vs(cc(6), cc(6), 2.0, None, ALU.mult)
        vt(cc(5), cc(3), cc(3), ALU.mult)
        vs(cc(5), cc(5), -2.0, 1.0, ALU.mult, ALU.add)
        A.do(nc.scalar.activation, cc(8), decay_log, ACT.Exp, after=[V.last()])
        A.do(nc.scalar.activation, cc(9), cc(8), ACT.Exp, scale=-1.0, after=[A.last()])
        vs(cc(10), cc(8), 0.25, None, ALU.min)
        vs(cc(11), cc(10), -1 / 7.0, 1.0, ALU.mult, ALU.add)
        for k in range(6, 0, -1):
            V.do(nc.vector.scalar_tensor_tensor, cc(11), cc(11), -1.0 / k, cc(10), ALU.mult, ALU.mult, after=[V.last()])
            vs(cc(11), cc(11), 1.0, None, ALU.add)
        vs(cc(12), cc(8), 0.25, None, ALU.is_lt)
        vt(cc(11), cc(11), cc(9), ALU.subtract)
        V.do(nc.vector.scalar_tensor_tensor, cc(7), cc(11), cc(12), cc(9), ALU.mult, ALU.add, after=[V.last()])


def rotation_tables(g, col, CT, ST, inv, s1, s2):
    nc, G = g.nc, g.G
    cc = lambda k: col[:, k:k + 1]
    gs = lambda o, i, a: G.do(nc.gpsimd.tensor_scalar, o, i, a, 1.0, ALU.mult, ALU.mult, after=[G.last()])
    gt = lambda o, a, b, op: G.do(nc.gpsimd.tensor_tensor, o, a, b, op, after=[G.last()])
    G.do(nc.gpsimd.memset, CT[:, 0:1], 1.0)
    G.do(nc.gpsimd.memset, ST[:, 0:1], 0.0)
    n = 1
    while n < N:
        gs(s1[:, 0:n], ST[:, 0:n], cc(6))
        gs(CT[:, n:2 * n], CT[:, 0:n], cc(5))
        gs(s2[:, 0:n], CT[:, 0:n], cc(6))
        gs(ST[:, n:2 * n], ST[:, 0:n], cc(5))
        gt(CT[:, n:2 * n], CT[:, n:2 * n], s1[:, 0:n], ALU.subtract)
        gt(ST[:, n:2 * n], ST[:, n:2 * n], s2[:, 0:n], ALU.add)
        gs(cc(14), cc(5), cc(6))
        gs(cc(15), cc(6), cc(6))
        gt(cc(6), cc(14), cc(14), ALU.add)
        gs(cc(14), cc(5), cc(5))
        gt(cc(5), cc(14), cc(15), ALU.subtract)
        n *= 2
    gt(s1[:, :], CT[:, :], CT[:, :], ALU.mult)
    gt(s2[:, :], ST[:, :], ST[:, :], ALU.mult)
    gt(inv[:, :], s1[:, :], s2[:, :], ALU.add)
    G.do(nc.gpsimd.tensor_scalar, inv[:, :], inv[:, :], -1.0, 2.0, ALU.mult, ALU.add, after=[G.last()])


def delta(g, w, tables):
    nc, p, V, A, T, G = g.nc, g.p, g.V, g.A, g.T, g.G
    with ExitStack() as mem:
        sb = lambda n, s, d=F32: mem.enter_context(nc.sbuf_tensor(f"{n}{g.uid()}", s, d))
        blk = lambda b: slice(b * 512, (b + 1) * 512)
        npT = sb("normed_p20", [128, N])
        swap = sb("swap", [128, 128])
        ones = sb("ones", [128, 128])
        bd = sb("head_ones", [128, HEADS, HD])
        selk = sb("key_select", [128, HD, HEADS, HD])
        z = G.do(nc.gpsimd.memset, swap[:, :], 0.0)
        v = swap[:, :].rearrange("p (m r) -> p m r", r=2)
        z = G.do(nc.gpsimd.affine_select, out=v[:, :, 0], in_=v[:, :, 0], compare_op=ALU.not_equal, fill=1.0, base=-1, pattern=[[-2, 64]], channel_multiplier=1, after=[z])
        z = G.do(nc.gpsimd.affine_select, out=v[:, :, 1], in_=v[:, :, 1], compare_op=ALU.not_equal, fill=-1.0, base=0, pattern=[[-2, 64]], channel_multiplier=1, after=[z])
        G.do(nc.gpsimd.memset, ones[:, :], 1.0)
        z = G.do(nc.gpsimd.memset, bd[:, :, :], 1.0)
        z = G.do(nc.gpsimd.affine_select, out=bd[:, :, :], in_=bd[:, :, :], compare_op=ALU.is_ge, fill=0.0, base=0, pattern=[[-HD, HEADS], [0, HD]], channel_multiplier=1, after=[z])
        z = G.do(nc.gpsimd.affine_select, out=bd[:, :, :], in_=bd[:, :, :], compare_op=ALU.is_ge, fill=0.0, base=HD - 1, pattern=[[HD, HEADS], [0, HD]], channel_multiplier=-1, after=[z])
        z = G.do(nc.gpsimd.memset, selk[:, :, :, :], 0.0)
        for k in range(HD):
            G.do(nc.gpsimd.affine_select, out=selk[:, k, :, :], in_=selk[:, k, :, :], compare_op=ALU.not_equal, fill=1.0, base=-k, pattern=[[-HD, HEADS], [0, HD]],
                 channel_multiplier=1, after=[z])
        made = G.last()

        q, k, bv = sb("queries", [128, N]), sb("keys", [128, N]), sb("beta_values", [128, N])
        dec, nb = sb("decay", [128, N]), sb("neg_beta_decay", [128, N])
        gt = sb("gate", [128, NT, D])
        ramp = sb("ramp", [128, 1])
        with ExitStack() as early:
            sbe = lambda n, s, d=F32: early.enter_context(nc.sbuf_tensor(f"{n}{g.uid()}", s, d))
            CT, ST, inv, r = tables
            kn = nb
            x1, x2 = sbe("p20_a", [128, N]), sbe("p20_b", [128, N])
            pads = [sbe(f"conv_in{i}", [128, TAPS - 1 + N]) for i in range(3)]
            free = [None] * 8

            def turned(src, after):
                for b in range(NB):
                    T.do(nc.tensor.matmul, g.ps[b], swap[:, :], src[:, blk(b)], start=True, stop=True, after=[made, free[b]] + after)
                    yield T.last()

            def sine_part(marks, after):
                for b, mm in enumerate(marks):
                    free[b] = V.do(nc.vector.tensor_tensor, x2[:, blk(b)], ST[:, blk(b)], g.ps[b], ALU.mult, after=[mm] + after)
                return free[NB - 1]

            def projection(i):
                z = V.do(nc.vector.memset, pads[i][:, 0:TAPS - 1], 0.0)
                for b in range(NB):
                    c = 4 + b
                    mm = T.do(nc.tensor.matmul, g.ps[c], w["ctrl"][:, i * 128:(i + 1) * 128], g.xnT[:, blk(b)], start=True, stop=True, after=[free[c]])
                    free[c] = A.do(nc.scalar.activation, pads[i][:, TAPS - 1 + b * 512:TAPS - 1 + (b + 1) * 512], g.ps[c], ACT.Identity,
                                   bias=w["ctrl_b"][:, i:i + 1], after=[mm])
                return [free[7], z]

            def convolve(i, dst, m):
                m = V.do(nc.vector.tensor_scalar, dst[:, :], pads[i][:, 0:N], w["convs"][:, i, 0:1], None, ALU.mult, after=m)
                for c in range(1, TAPS):
                    m = V.do(nc.vector.scalar_tensor_tensor, dst[:, :], pads[i][:, c:c + N], w["convs"][:, i, c:c + 1], dst[:, :], ALU.mult, ALU.add, after=[m])
                return m

            marks = list(turned(g.xnT, []))
            zc = G.do(nc.gpsimd.tensor_tensor, npT[:, :], g.xnT[:, :], CT[:, :], ALU.mult, after=[made])
            projected = [projection(i) for i in range(3)]
            nc.scalar.preload_act_table(ACT.Sigmoid)
            rm = A.do(nc.scalar.activation, ramp[:, :], w["ramp_logit"], ACT.Sigmoid)
            for i, dst in ((0, dec), (1, nb)):
                for b in range(NB):
                    c = 4 + b
                    mm = T.do(nc.tensor.matmul, g.ps[c], w["dec_beta"][:, i * 128:(i + 1) * 128], g.xnT[:, blk(b)], start=True, stop=True, after=[free[c]])
                    free[c] = A.do(nc.scalar.activation, dst[:, blk(b)], g.ps[c], ACT.Sigmoid, bias=w["ctrl_b"][:, 3 + i:4 + i], after=[mm])
            sig = A.last()
            zs = sine_part(marks, [])
            cv = convolve(0, q, projected[0])
            m = V.do(nc.vector.tensor_tensor, npT[:, :], npT[:, :], x2[:, :], ALU.add, after=[zs, zc])
            m = V.do(nc.vector.tensor_tensor, x1[:, :], npT[:, :], inv[:, :], ALU.mult, after=[m])
            scan = V.do(nc.vector.tensor_tensor_scan, inv[:, :], r.broadcast_to([128, N]), x1[:, :], 0.0, ALU.mult, ALU.add, after=[m])
            marks = list(turned(inv, [scan]))
            yc = G.do(nc.gpsimd.tensor_tensor, CT[:, :], CT[:, :], inv[:, :], ALU.mult, after=[scan])
            for b in range(NB):
                for c in range(4):
                    t = 4 * b + c
                    o = g.ps[4 + b][:, c * 128:(c + 1) * 128]
                    T.do(nc.tensor.matmul, o, g.xnT[:, t * 128:(t + 1) * 128], w["ctrl"][:, 384:512], start=True, stop=False, after=[free[4 + b]])
                    mm = T.do(nc.tensor.matmul, o, g.ones_row[:, 0:128], w["gate_b"], start=False, stop=True)
                free[4 + b] = A.do(nc.scalar.activation, gt[:, 4 * b:4 * b + 4, :].rearrange("p t d -> p (t d)"), g.ps[4 + b], ACT.Sigmoid, after=[mm])
            nc.scalar.preload_act_table(ACT.Silu)
            silud = [A.do(nc.scalar.activation, q[:, :], q[:, :], ACT.Silu, after=[cv])]
            cv = convolve(1, k, projected[1])
            silud.append(A.do(nc.scalar.activation, k[:, :], k[:, :], ACT.Silu, after=[cv]))
            m = sine_part(marks, [])
            y = V.do(nc.vector.tensor_tensor, x1[:, :], CT[:, :], x2[:, :], ALU.subtract, after=[yc, m])
            cv = convolve(2, bv, projected[2])
            sq = A.do(nc.scalar.activation, x2[:, :], x1[:, :], ACT.Square, after=[y])
            silud.append(A.do(nc.scalar.activation, bv[:, :], bv[:, :], ACT.Silu, after=[cv]))
            nc.scalar.preload_act_table_set("natural_log_exp_and_others")
            npd = {}
            for b in range(NB):
                c = 4 + b
                mm = T.do(nc.tensor.matmul, g.ps[c], ones[:, :], x2[:, blk(b)], start=True, stop=True, after=[sq, free[c]])
                m = free[c] = A.do(nc.scalar.activation, CT[:, blk(b)], g.ps[c], ACT.Ln, bias=g.eps_rms[:, :], scale=1.0 / D, after=[mm, y])
                m = A.do(nc.scalar.activation, CT[:, blk(b)], CT[:, blk(b)], ACT.Exp, scale=-0.5, after=[m])
                npd[b] = V.do(nc.vector.scalar_tensor_tensor, npT[:, blk(b)], x1[:, blk(b)], w["vnorm"], CT[:, blk(b)], ALU.mult, ALU.mult, after=[m, scan])
            units = [(1, b) for b in range(NB)] + [(0, b) for b in range(NB)] + [(2, b) for b in range(NB)]
            dsts, added, normed = (q, k, bv), {}, {}
            squares, norm = (x2, x1), (pads[0], pads[1])
            for n in range(len(units) + 2):
                if n < len(units):
                    i, b = units[n]
                    c = n % 4
                    mm = T.do(nc.tensor.matmul, g.ps[c], w["p20c"][:, i * 128:(i + 1) * 128], npT[:, blk(b)], start=True, stop=True, after=[npd[b], free[c]])
                    m = free[c] = V.do(nc.vector.scalar_tensor_tensor, dsts[i][:, blk(b)], g.ps[c], ramp[:, :], dsts[i][:, blk(b)], ALU.mult, ALU.add,
                                       after=[mm, silud[i], rm])
                    if i < 2:
                        added[n] = A.do(nc.scalar.activation, squares[i][:, blk(b)], dsts[i][:, blk(b)], ACT.Square, after=[m, npd[NB - 1]])
                    else:
                        m = V.do(nc.vector.tensor_tensor, bv[:, blk(b)], bv[:, blk(b)], nb[:, blk(b)], ALU.mult, after=[m, sig])
                        m = V.do(nc.vector.scalar_tensor_tensor, nb[:, blk(b)], nb[:, blk(b)], -1.0, dec[:, blk(b)], ALU.mult, ALU.mult, after=[m])
                        V.do(nc.vector.tensor_tensor, kn[:, blk(b)], nb[:, blk(b)], k[:, blk(b)], ALU.mult, after=[m, normed[b]])
                if 1 <= n <= 2 * NB:
                    i, b = units[n - 1]
                    c = 4 + n % 4
                    mm = T.do(nc.tensor.matmul, g.ps[c], bd[:, :, :].rearrange("p h d -> p (h d)"), squares[i][:, blk(b)], start=True, stop=True, after=[added[n - 1], free[c]])
                    a = free[c] = A.do(nc.scalar.activation, norm[i][:, blk(b)], g.ps[c], ACT.Ln, bias=g.eps_rms[:, :], after=[mm, cv])
                    added[n - 1] = A.do(nc.scalar.activation, norm[i][:, blk(b)], norm[i][:, blk(b)], ACT.Exp, scale=-0.5, after=[a])
                if 2 <= n <= 2 * NB + 1:
                    i, b = units[n - 2]
                    normed[n - 2] = V.do(nc.vector.tensor_tensor, dsts[i][:, blk(b)], dsts[i][:, blk(b)], norm[i][:, blk(b)], ALU.mult, after=[added[n - 2]])
            p.join()

        KB = [sb(f"keys_spread{i}", [128, GRP, SEG, HD]) for i in range(2)]
        QB = [sb(f"queries_spread{i}", [128, GRP, SEG, HD]) for i in range(2)]
        KN = [sb(f"keys_scaled{i}", [128, GRP, SEG, HD + 1]) for i in range(2)]
        S = [sb(f"state{i}", [128, 2, SEG, HD + 1]) for i in range(2)]
        SD = sb("state_decayed", [128, 2, SEG, HD])
        M, X = sb("state_keys", [128, 2, SEG, HD + 1]), sb("update", [128, 2, SEG, HD])
        MQ = [sb(f"state_queries{i}", [128, 2, SEG, HD]) for i in range(2)]
        pr = sb("predicted", [128, 2, SEG])
        ou = sb("outs", [128, 2, N])
        seg = lambda ap: ap.rearrange("p (g s) -> p g s", s=STEPS)
        for i in range(2):
            z = G.do(nc.gpsimd.memset, S[i][:, :, :, :], 0.0)
            z = G.do(nc.gpsimd.memset, S[i][:, 0, :, HD:HD + 1], 1.0, after=[z])
        z = V.do(nc.vector.tensor_reduce, pr[:, 0, 0:HD], selk[:, :, :, 0], AX.X, ALU.add, after=[z])
        z = V.do(nc.vector.tensor_copy, S[1][:, 1, :, 0:HD], pr[:, 0, 0:HD].unsqueeze(1).broadcast_to([128, SEG, HD]), after=[z])
        st = dict(bank=[None] * 6, kb=[None, None], use=[None, None], S=None, X=None, MQ=[None, None], summed=[None, None], outs=[None, None])
        held = []

        def spread(i, s0):
            n = 0
            st["kb"][i] = A.do(nc.scalar.copy, KN[i][:, :, :, HD], seg(bv[:, :])[:, :, bass.ds(s0, GRP)].rearrange("p g s -> p s g"), after=[st["use"][i]])
            for src, dst in ((kn, KN[i]), (k, KB[i]), (q, QB[i])):
                cols = seg(src[:, :])[:, :, bass.ds(s0, GRP)].rearrange("p g s -> p s g")
                for kk in range(HD):
                    b = n % 6
                    n += 1
                    o = g.ps[b][:, 0:GRP * SEG]
                    mm = T.do(nc.tensor.matmul, o, selk[:, kk, :, :].rearrange("p h v -> p (h v)"), cols, start=True, stop=True, after=[st["bank"][b]])
                    st["bank"][b] = A.do(nc.scalar.copy, dst[:, :, :, kk], o.rearrange("p (s g) -> p s g", s=GRP), after=[mm, st["use"][i]])
                    st["kb"][i] = st["bank"][b]
                    yield

        def outputs():
            if not held:
                return
            i, j, s0 = held.pop()
            a = j % 2
            m = st["MQ"][a] = st["use"][i] = G.do(nc.gpsimd.tensor_tensor, MQ[a][:, :, :, :], S[a][:, :, :, 0:HD], kinds(QB[i][:, j, :, :]), ALU.mult,
                                                  after=[st["S"], st["summed"][a]])
            bank = g.ps[6 + i].rearrange("p (j x g) -> p j x g", j=GRP, x=2)
            for kk in range(HD):
                m2 = T.do(nc.tensor.matmul, bank[:, j, :, :], g.ident[:, :], MQ[a][:, :, :, kk], start=(kk == 0), stop=(kk == HD - 1),
                          after=[m, st["outs"][i]], skip_group_check=True)
            st["summed"][a] = m2
            if j == GRP - 1:
                for x in range(2):
                    o = ou[:, x, :].rearrange("p (g s) -> p g s", s=STEPS)[:, :, bass.ds(s0, GRP)]
                    st["outs"][i] = A.do(nc.scalar.copy, o, bank[:, :, x, :].rearrange("p j g -> p g j"), after=[m2])

        kinds = lambda ap: ap.unsqueeze(1).broadcast_to([128, 2] + list(ap.shape[1:]))

        def step(i, j, s0):
            s = s0 + j
            a, b = j % 2, 1 - j % 2
            m = V.do(nc.vector.tensor_tensor, M[:, :, :, :], S[b][:, :, :, :], kinds(KN[i][:, j, :, :]), ALU.mult, after=[st["S"], st["kb"][i]])
            decay = seg(dec[:, :])[:, :, bass.ds(s, 1)].rearrange("p g o -> p (g o)").unsqueeze(1).unsqueeze(3).broadcast_to([128, 2, SEG, HD])
            d = G.do(nc.gpsimd.tensor_tensor, SD[:, :, :, :], S[b][:, :, :, 0:HD], decay, ALU.mult,
                     after=[st["S"]])
            outputs()
            m = V.do(nc.vector.tensor_reduce, pr[:, :, :], M[:, :, :, :], AX.X, ALU.add, after=[m])
            m = st["X"] = V.do(nc.vector.tensor_tensor, X[:, :, :, :], pr[:, :, :].unsqueeze(3).broadcast_to([128, 2, SEG, HD]),
                               kinds(KB[i][:, j, :, :]), ALU.mult, after=[m])
            st["S"] = V.do(nc.vector.tensor_tensor, S[a][:, :, :, 0:HD], SD[:, :, :, :], X[:, :, :, :], ALU.add, after=[m, d, st["MQ"][a]])
            held.append((i, j, s0))

        for _ in spread(0, 0):
            pass

        def groups(s0, more):
            nxt = spread(1, s0 + GRP)
            for i in range(2):
                for j in range(GRP):
                    step(i, j, s0 + GRP * i)
                    for _ in range(SPREADS):
                        next(nxt, None)
                if i == 0 and more:
                    nxt = spread(0, s0 + 2 * GRP)
            outputs()
        p.pipeline(STEPS // (2 * GRP) - 1, lambda i: groups(i * 2 * GRP, True), st)
        groups(STEPS - 2 * GRP, False)
        p.join()

        fin = S[1][:, :, :, 0:HD]
        diagonal = lambda pair, n: pair[n // 16][:, :, :, :].rearrange("p a b c -> p (a b c)")[:, (n % 16) * 128:(n % 16 + 1) * 128]
        spread_out = []
        for n in range(SEG - 1):
            two_ends = []
            for eng, f, kind, pair in ((V, nc.vector, 1, KB), (G, nc.gpsimd, 0, QB)):
                out = diagonal(pair, n).rearrange("p (h k) -> p h k", h=HEADS)
                two_ends.append((eng, f.tensor_tensor, out, fin[:, kind, n, :].unsqueeze(1).broadcast_to([128, HEADS, HD]), bd[:, :, :], ALU.mult))
            spread_out.append(two_ends)

        def build(n):
            return [eng.do(*rest) for eng, *rest in spread_out[n]] if n < SEG - 1 else None

        o_, t1, t2 = ou[:, 0, :], ou[:, 1, :], q
        scale = float(HD) ** -0.5
        mn = V.do(nc.vector.tensor_scalar, ramp[:, :], w["mnorm"], scale, None, ALU.mult)
        free = {2: None, 3: None}

        def finish(b, cm):
            m = V.do(nc.vector.tensor_tensor, o_[:, blk(b)], o_[:, blk(b)], g.ps[4 + b], ALU.add, after=[cm])
            yield
            s = A.do(nc.scalar.activation, t1[:, blk(b)], o_[:, blk(b)], ACT.Square, scale=scale, after=[m, cm])
            yield
            mm = T.do(nc.tensor.matmul, g.ps[2], bd[:, :, :].rearrange("p h d -> p (h d)"), t1[:, blk(b)], start=True, stop=True, after=[s, free[2]])
            a = free[2] = A.do(nc.scalar.activation, t2[:, blk(b)], g.ps[2], ACT.Ln, bias=g.eps_rms[:, :], scale=1.0 / HD, after=[mm])
            a = A.do(nc.scalar.activation, t2[:, blk(b)], t2[:, blk(b)], ACT.Exp, scale=-0.5, after=[a])
            yield
            m = V.do(nc.vector.scalar_tensor_tensor, o_[:, blk(b)], o_[:, blk(b)], ramp[:, :], t2[:, blk(b)], ALU.mult, ALU.mult, after=[a, m, mn])
            yield
            for c in range(4):
                t = 4 * b + c
                o = g.ps[3][:, c * 128:(c + 1) * 128]
                ts = slice(t * 128, (t + 1) * 128)
                T.do(nc.tensor.matmul, o, o_[:, ts], w["out"][:, 0, :], start=True, stop=False, after=[m, free[3]])
                T.do(nc.tensor.matmul, o, npT[:, ts], w["out"][:, 1, :], start=False, stop=False)
                mm = T.do(nc.tensor.matmul, o, g.ones_row[:, 0:128], w["out_b"], start=False, stop=True)
                if c % 2:
                    yield
            ge = gt[:, 4 * b:4 * b + 4, :]
            xx = g.x_tok[:, 4 * b:4 * b + 4, :]
            m = free[3] = V.do(nc.vector.tensor_tensor, ge, ge, g.ps[3].rearrange("p (t f) -> p t f", t=4), ALU.mult, after=[mm])
            G.do(nc.gpsimd.tensor_tensor, xx, xx, ge, ALU.add, after=[m])
            yield

        S0 = [sb(f"start_state{i}", [128, 128]) for i in range(2)]
        z = V.do(nc.vector.memset, S0[0][:, :], 0.0)
        cor, finishing = None, []
        ends = {n: build(n) for n in range(3)}
        for n in range(SEG):
            cur, nx = S0[n % 2], S0[(n + 1) % 2]
            ends[n + 3] = build(n + 3)
            if n + 1 < SEG:
                bank = g.ps[n % 2][:, 0:128]
                T.do(nc.tensor.matmul, bank, diagonal(QB, n), g.ident[:, :], start=True, stop=False, after=ends[n] + [z])
                mm = T.do(nc.tensor.matmul, bank, diagonal(KB, n), cur[:, :], start=False, stop=True, after=[z])
            ob = g.ps[4 + n // 8][:, (n % 8) * STEPS:(n % 8 + 1) * STEPS]
            cm = T.do(nc.tensor.matmul, ob, cur[:, :], ou[:, 1, n * STEPS:(n + 1) * STEPS], start=True, stop=True, after=[z])
            if n + 1 < SEG:
                z = V.do(nc.vector.tensor_copy, nx[:, :], bank, after=[mm, cor])
            cor = cm
            for block in finishing:
                next(block, None)
            if n % 8 == 7:
                finishing.append(finish(n // 8, cm))
        for block in finishing:
            for _ in block:
                pass
        p.join()


ATTN_COLS = (("wqT", 128), ("wkT", 128), ("wvT", 128), ("woT", 128), ("bq", 1), ("bk", 1))
GLA_COLS = (("Wp", 3 * KD), ("Wa", 224), ("Wb", KD), ("Wc", KD), ("Wo", KD), ("We", NEXP), ("norm", 1))
MAMBA_COLS = (("in_proj", 512), ("x_proj", 80), ("out_proj", 256), ("dt_w", 256), ("conv_w", 8), ("conv_b", 2),
              ("dt_b", 2), ("A_log", 32), ("Dp", 2))
MOE_COLS = (("w1", UNITS * 128), ("w3", UNITS * 128), ("w2", UNITS * 128), ("gate", EXPERTS), ("gate_bias", EXPERTS))
DELTA_COLS = (("ctrl", 512), ("dec_beta", 256), ("ctrl_b", 5), ("p20c", 384), ("convs", 12), ("out", 256),
              ("theta", 1), ("decay_log", 1), ("ramp_logit", 1), ("vnorm", 1), ("mnorm", 1))
BLOCKS = {"x_proj": 2, "out_proj": 2, "conv_w": 2, "A_log": 2, "w1": UNITS, "w3": UNITS, "w2": UNITS, "convs": 3, "out": 2}
ROW_PAIRS = 3


def width(cols):
    return sum(k for _, k in cols)


def views(sbuf, cols):
    out, at = {}, 0
    for name, k in cols:
        v = sbuf[:, at:at + k]
        out[name] = v.rearrange("p (i c) -> p i c", i=BLOCKS[name]) if name in BLOCKS else v
        at += k
    return out


class Context:
    pass


def build(nc):
    dram = lambda n, s: nc.dram_tensor(n, s, F32, kind="ExternalInput").ap()
    x = dram("x", (N, D))
    src = {n: dram(n, (128, width(c))) for n, c in
           (("attn_a", ATTN_COLS), ("attn_b", ATTN_COLS), ("gla", GLA_COLS), ("mamba", MAMBA_COLS), ("moe", MOE_COLS), ("delta", DELTA_COLS))}
    row_src = dram("row_biases", (ROW_PAIRS, 2 * D))
    out = nc.dram_tensor("out", (1, N, D), F32, kind="ExternalOutput").ap()

    g = Context()
    g.nc, g.p = nc, Program(nc)
    p = g.p
    g.V, g.A, g.T, g.G = p.stream(nc.vector, "vec"), p.stream(nc.scalar, "act"), p.stream(nc.tensor, "pe"), p.stream(nc.gpsimd, "pool")
    g.L, g.Lsc2 = p.stream(nc.sync, "load", 16), p.stream(nc.sync, "scratch_2", 16)
    names = []

    def uid():
        names.append(None)
        return f"_{len(names)}"

    g.uid = uid
    keep = lambda n, s, d=F32: nc.alloc_sbuf_tensor(n, s, d)
    g.x_tok, g.xnT = keep("x_tok", [128, NT, D]), keep("xnT", [128, N])
    g.ident, g.tri, g.cum = keep("ident", [128, 128]), keep("tri", [128, 128]), keep("cum", [128, 128])
    g.half_col, g.eps_ln, g.eps_rms = keep("half_col", [128, 2]), keep("eps_ln", [128, 1]), keep("eps_rms", [128, 1])
    g.ones_row, rows = keep("ones_row", [1, 128]), keep("row_biases_sb", [1, 2 * D])
    rotation, given = keep("rotation_columns", [128, 16]), keep("theta_decay", [128, 2])
    mixer_w = keep("mixer_weights", [128, max(width(c) for c in (ATTN_COLS, MAMBA_COLS, DELTA_COLS))])
    ffn_w = keep("ffn_weights", [128, max(width(GLA_COLS), width(MOE_COLS))])
    whole = nc.alloc_psum_tensor("banks", [128, 8 * 512], F32)
    g.ps = [whole[:, i * 512:(i + 1) * 512] for i in range(8)]
    g.wide = lambda i: whole[:, i * 512:(i + 2) * 512]
    g.q_scratch = nc.dram_tensor("q_scratch", (PARTS, 128, N), BF16, kind="Internal").ap()
    g.k_scratch = nc.dram_tensor("k_scratch", (PARTS, 128, N), BF16, kind="Internal").ap()

    def load(sbuf, name):
        a = src[name]
        return g.L.do(nc.sync.dma_start, sbuf[:, 0:a.shape[1]], a)

    def load_rows(k):
        return g.L.do(nc.sync.dma_start, rows[:, :], row_src[k:k + 1, :])

    for b in range(NB):
        xb = g.L.do(nc.sync.dma_start, g.x_tok[:, 4 * b:4 * b + 4, :], x[b * 512:(b + 1) * 512, :].rearrange("(t p) d -> p t d", p=128))
    at = sum(k for _, k in DELTA_COLS[:[n for n, _ in DELTA_COLS].index("theta")])
    g.L.do(nc.sync.dma_start, given[:, :], src["delta"][:, at:at + 2])
    load(mixer_w, "attn_a")
    load_rows(0)
    first = g.L.last()
    ffn_loads = p.stream(nc.sync, "load_gla", 16)
    ffn_loads.do(nc.sync.dma_start, ffn_w[:, 0:width(GLA_COLS)], src["gla"])

    G = g.G
    m = G.do(nc.gpsimd.memset, g.ident[:, :], 0.0)
    G.do(nc.gpsimd.affine_select, out=g.ident[:, :], in_=g.ident[:, :], compare_op=ALU.not_equal, fill=1.0, base=0,
         pattern=[[-1, 128]], channel_multiplier=1, after=[m])
    G.do(nc.gpsimd.memset, g.ones_row[:, :], 1.0)
    G.do(nc.gpsimd.memset, g.eps_ln[:, :], EPS_LN)
    G.do(nc.gpsimd.memset, g.eps_rms[:, :], EPS_R)
    m = G.do(nc.gpsimd.memset, g.tri[:, :], 1.0)
    m = G.do(nc.gpsimd.affine_select, out=g.tri[:, :], in_=g.tri[:, :], compare_op=ALU.is_ge, fill=0.0, base=0,
             pattern=[[1, 128]], channel_multiplier=-1, after=[m])
    m = G.do(nc.gpsimd.memset, g.half_col[:, :], 1.0)
    m = G.do(nc.gpsimd.affine_select, out=g.half_col[:, 0:1], in_=g.half_col[:, 0:1], compare_op=ALU.is_ge, fill=0.0,
             base=63, pattern=[[0, 1]], channel_multiplier=-1, after=[m])
    m = G.do(nc.gpsimd.affine_select, out=g.half_col[:, 1:2], in_=g.half_col[:, 1:2], compare_op=ALU.is_ge, fill=0.0,
             base=-64, pattern=[[0, 1]], channel_multiplier=1, after=[m])
    g.V.do(nc.vector.tensor_scalar, g.cum[:, :], g.tri[:, :], g.half_col[:, 0:1], None, ALU.subtract, after=[m])
    nc.scalar.preload_act_table_set("natural_log_exp_and_others")

    row_1, row_2 = rows[:, 0:D], rows[:, D:2 * D]
    for e in (nc.tensor, nc.vector, nc.scalar, nc.gpsimd):
        p.wait(e, [first, G.last(), g.V.last()])
    rotation_columns(g, given[:, 0:1], given[:, 1:2], rotation)
    layer_norm_T(g)
    attention(g, dict(views(mixer_w, ATTN_COLS), bv=row_1, bo=row_2), "a")
    load(mixer_w, "attn_b")
    load_rows(1)
    layer_norm_T(g)
    gla_ffn(g, views(ffn_w, GLA_COLS))
    layer_norm_T(g)
    attention(g, dict(views(mixer_w, ATTN_COLS), bv=row_1, bo=row_2), "b")
    load(mixer_w, "mamba")
    load_rows(2)
    layer_norm_T(g)
    gla_ffn(g, views(ffn_w, GLA_COLS))
    load(ffn_w, "moe")
    layer_norm_T(g)
    mamba(g, views(mixer_w, MAMBA_COLS))
    load(mixer_w, "delta")
    with ExitStack() as mem:
        tables = [mem.enter_context(nc.sbuf_tensor(f"{n}_table", [128, N], F32)) for n in ("cosine", "sine", "inverse")]
        with ExitStack() as scratch:
            beside = [scratch.enter_context(nc.sbuf_tensor(f"table_scratch{i}", [128, N], F32)) for i in range(2)]
            layer_norm_T(g)
            moe(g, views(ffn_w, MOE_COLS), lambda: rotation_tables(g, rotation, *tables, *beside))
            p.join()
        layer_norm_T(g)
        delta(g, dict(views(mixer_w, DELTA_COLS), gate_b=row_1, out_b=row_2), (*tables, rotation[:, 7:8]))
    layer_norm_T(g)
    moe(g, views(ffn_w, MOE_COLS))
    stored = g.L.do(nc.sync.dma_start, out[0].rearrange("(t p) d -> p t d", p=128), g.x_tok[:, :, :])
    p.wait(nc.sync, [stored])


def kernel(**a):
    import concourse.bacc as _bacc
    import numpy as np
    from concourse.bass_utils import run_bass_kernel_spmd as _run

    a = {k: np.asarray(v) for k, v in a.items()}
    w, b = a["L0_attn_a_qkv_w"], a["L0_attn_a_qkv_b"]
    attn_a = np.concatenate([w[0:128].T, w[128:256].T, w[256:384].T, a["L0_attn_a_out_w"].T, b[0:128, None], b[128:256, None]], 1)
    rows = [b[256:384], a["L0_attn_a_out_b"]]
    f = lambda n: a["L0_attn_b_" + n]
    kv_heads = f("wk").shape[0] // HD
    grp = HEADS // kv_heads
    again = lambda v: np.repeat(v.reshape((kv_heads, HD) + v.shape[1:]), grp, 0).reshape((HEADS * HD,) + v.shape[1:])
    attn_b = np.concatenate([f("wq").T, again(f("wk")).T, again(f("wv")).T, f("wo").T, f("bq")[:, None],
                             again(f("bk"))[:, None]], 1)
    rows += [again(f("bv")), f("bo")]
    f = lambda n: a["L0_ffn_" + n]
    blocks = lambda v: v.reshape(v.shape[0] // 128, 128, -1).transpose(1, 0, 2).reshape(128, -1)
    wc = np.zeros((128, f("Wgb").shape[1]), np.float32)
    wc[0:64], wc[64:80], wc[80], wc[96:112], wc[112] = f("Wgb"), f("Wg1b"), f("bg1"), f("Wg2b"), f("bg2")
    gla = np.concatenate([f("Wq"), f("Wk"), f("Wv"), f("Wqa"), f("Wka"), f("Wga"), f("Wg1a"), f("Wg2a"),
                          np.concatenate([f("Wqb"), f("Wkb")], 0), wc, blocks(f("Wo")), f("We"), np.tile(f("norm_w"), 2)[:, None]], 1)
    f = lambda n: a["L1_attn_a_" + n]
    dt_w = np.zeros((128, f("dt_proj_w").shape[1]), np.float32)
    dt_w[0:f("dt_proj_w").shape[0]] = f("dt_proj_w")
    mamba_w = np.concatenate([f("in_proj_w"), blocks(f("x_proj_w")), blocks(f("out_proj_w")), dt_w, blocks(f("conv_w")[:, 0, :]),
                              blocks(f("conv_b")[:, None]), blocks(f("dt_proj_b")[:, None]), blocks(f("A_log")), blocks(f("Dparam")[:, None])], 1)
    f = lambda n: a["L1_ffn_" + n]
    up = lambda r, s: np.concatenate([f(r), f(s).reshape(-1, 128, 128)], 0).transpose(2, 0, 1).reshape(128, -1)
    down = np.concatenate([f("w2").transpose(0, 2, 1), f("sw2").T.reshape(-1, 128, 128)], 0).transpose(1, 0, 2).reshape(128, -1)
    moe_w = np.concatenate([up("w1", "sw1"), up("w3", "sw3"), down, f("gate_w").T, np.tile(f("gate_bias")[None], (128, 1))], 1)
    f = lambda n: a["L1_attn_b_" + n]
    w, b = f("ctrl_W"), f("ctrl_b")
    cols = [b[0:128], b[128:256], b[256:384], np.repeat(b[384:400], HD), np.repeat(b[400:416], HD)]
    delta_w = np.concatenate([w[:, 0:384], w[:, 416:544], np.repeat(w[:, 384:416], HD, 1), np.stack(cols, 1), f("p20c_W"),
                              f("qconv_w"), f("kconv_w"), f("vconv_w"), blocks(f("out_W")), np.repeat(f("p20_theta"), 2)[:, None],
                              np.repeat(f("p20_decay_log"), 2)[:, None], f("ramp_logit")[:, None], f("vnorm_scale")[:, None],
                              np.tile(f("mnorm_scale"), HEADS)[:, None]], 1)
    rows += [b[416:544], f("out_b")]
    inputs = dict(x=a["L0_attn_a_x"][0], attn_a=attn_a, attn_b=attn_b, gla=gla, mamba=mamba_w, moe=moe_w, delta=delta_w,
                  row_biases=np.concatenate(rows).reshape(-1, 256))
    inputs = {k: np.ascontiguousarray(v) for k, v in inputs.items()}
    nc = _bacc.Bacc("TRN2", target_bir_lowering=False, num_devices=1)
    build(nc)
    nc.compile()
    return _run(nc, [inputs], core_ids=[0]).results[0]["out"]
```
